# Optimizing a Trainium2 kernel written in Bass

```python
import numpy as np
import jax
import jax.numpy as jnp

def _softmax(x, axis=-1):
    return jax.nn.softmax(x, axis=axis)

def _gelu(x):
    return jax.nn.gelu(x, approximate=True)

def _silu(x):
    return jax.nn.silu(x)

def _sigmoid(x):
    return jax.nn.sigmoid(x)

def _layernorm(x, axis=-1, eps=1e-05):
    m = jnp.mean(x, axis=axis, keepdims=True)
    v = jnp.var(x, axis=axis, keepdims=True)
    return (x - m) / jnp.sqrt(v + eps)

def _scatter_add(tgt, idx, src, axis=0):
    return tgt.at[idx].add(src)

def _segment_sum(src, seg, n):
    return jax.ops.segment_sum(src, seg, n)
kernel_name = 'mk_decoder_postln_d1_seqx_r2_952c42'

def setup_inputs(seed: int=0):
    np.random.seed(seed)
    _w = jnp.asarray

    def _rec_inputs():
        import jax
        import jax.numpy as jnp
        _rk = jax.random.key(seed)
        x = -0.000125 + 0.9999 * jax.random.normal(jax.random.fold_in(_rk, 1), (16, 512, 512), jnp.float32)
        _lenS = 512 - jax.random.randint(jax.random.fold_in(_rk, 7), (16,), 0, max(1, 512 // 4) + 1, jnp.int32)
        _lenS2 = 512 - jax.random.randint(jax.random.fold_in(_rk, 8), (16,), 0, max(1, 512 // 4) + 1, jnp.int32)
        _ctx_1024P = jax.random.normal(jax.random.fold_in(_rk, 11), (16, 16, 512), jnp.float32)
        _ctx_1024c = jax.random.dirichlet(jax.random.fold_in(_rk, 511), 0.3 * jnp.ones((16,), jnp.float32), (16, 512))
        _ctx_1024t = jnp.einsum('bsk,bkd->bsd', _ctx_1024c, _ctx_1024P)
        _ctx_1024t = _ctx_1024t * jax.lax.rsqrt(jnp.mean(jnp.square(_ctx_1024t)) + 1e-12) * 0.953939
        ctx_1024 = -1.52775e-05 + 0.999936 * (_ctx_1024t + 0.3 * jax.random.normal(jax.random.fold_in(_rk, 611), (16, 512, 512), jnp.float32))
        return (x, ctx_1024)
    x, ctx_1024 = _rec_inputs()

    def _L0_attn_setup():
        import jax, jax.numpy as jnp
        import numpy as np
        _SCAN_CHUNK = 32

        def _causal_decay_scan(x, decay, init):
            B, H, T, D = x.shape
            C = min(_SCAN_CHUNK, T)
            assert T % C == 0
            nC = T // C
            log_decay = jnp.log(jnp.clip(decay.astype(jnp.float32), 1e-08, None))
            c_idx = jnp.arange(C, dtype=jnp.float32)
            log_p = log_decay[..., None] * c_idx.reshape(1, 1, C, 1)
            p = jnp.exp(log_p)
            inv_p = jnp.exp(-log_p)
            init_p = jnp.exp(log_decay[..., None] * (c_idx + 1.0).reshape(1, 1, C, 1))
            xc = x.reshape(B, H, nC, C, D).transpose(2, 0, 1, 3, 4).astype(jnp.float32)

            def step(state, chunk):
                cs = jnp.cumsum(chunk * inv_p, axis=2)
                out = cs * p + state[:, :, None, :] * init_p
                return (out[:, :, -1, :], out)
            _, outs = jax.lax.scan(step, init.astype(jnp.float32), xc)
            return outs.transpose(1, 2, 0, 3, 4).reshape(B, H, T, D).astype(x.dtype)

        def _phi(x):
            return jax.nn.elu(x) + 1.0
        key = jax.random.key(seed)
        ks = jax.random.split(key, 5)
        B, T, hidden, H = (4, 2048, 512, 16)
        s = 1.0 / np.sqrt(hidden)
        x = jax.random.normal(ks[0], (B, T, hidden), dtype=jnp.float32)
        Wqkv = jax.random.normal(ks[1], (3 * hidden, hidden), dtype=jnp.float32) * s
        Wout = jax.random.normal(ks[2], (hidden, hidden), dtype=jnp.float32) * s
        Wgate = jax.random.normal(ks[3], (hidden, hidden), dtype=jnp.float32) * s
        bgate = jnp.zeros((hidden,), dtype=jnp.float32)
        logit = float(np.log(0.95 / 0.05))
        decay_param = jnp.full((H,), logit, dtype=jnp.float32)
        return {'x': x, 'Wqkv': Wqkv, 'Wout': Wout, 'Wgate': Wgate, 'bgate': bgate, 'decay_param': decay_param}
    _L0_attn_all = _L0_attn_setup()
    _L0_attn_in = {k: v for k, v in _L0_attn_all.items() if k in ('Wqkv', 'Wout', 'Wgate', 'bgate', 'decay_param')}
    del _L0_attn_all

    def _L0_xattn_setup():
        import jax, jax.numpy as jnp
        import numpy as np
        DECAY = 0.9
        key = jax.random.key(seed)
        k1, k2, k3 = jax.random.split(key, 3)
        B, S, D = (8, 2048, 512)
        q = jax.random.normal(k1, (B, S, D), dtype=jnp.float32)
        k = jax.random.normal(k2, (B, S, D), dtype=jnp.float32)
        v = jax.random.normal(k3, (B, S, D), dtype=jnp.float32)
        return {'q': q, 'k': k, 'v': v}
    _L0_xattn_all = _L0_xattn_setup()
    _L0_xattn_in = {k: v for k, v in _L0_xattn_all.items() if k in ()}
    del _L0_xattn_all

    def _L0_ffn_setup():
        import jax, jax.numpy as jnp
        import numpy as np
        BLOCK = 32
        W_BITS = 4
        ACT_BITS = 16

        def act_qdq(x):
            qmax = 2.0 ** (ACT_BITS - 1) - 1.0
            scale = jnp.maximum(jnp.max(jnp.abs(x)) / qmax, 1e-12)
            return jnp.clip(jnp.round(x / scale), -qmax - 1.0, qmax) * scale

        def fixed_qdq_u16(x):
            scale = 1.0 / 65536.0
            return jnp.clip(jnp.round(x / scale), 0.0, 65535.0) * scale

        def lpbq_dequant(w):
            O, I = w.shape
            qmax = 2.0 ** (W_BITS - 1) - 1.0
            wb = w.reshape(O, I // BLOCK, BLOCK)
            s = jnp.maximum(jnp.max(jnp.abs(wb), axis=-1, keepdims=True) / qmax, 1e-12)
            wq = jnp.clip(jnp.round(wb / s), -qmax - 1.0, qmax) * s
            return wq.reshape(O, I)
        key = jax.random.key(seed)
        k1, k2, k3, k4 = jax.random.split(key, 4)
        B, S, H, I = (2, 2048, 512, 1536)
        x = jax.random.normal(k1, (B, S, H), jnp.float32)
        w_gate = jax.random.normal(k2, (I, H), jnp.float32) * 0.02
        w_up = jax.random.normal(k3, (I, H), jnp.float32) * 0.02
        w_down = jax.random.normal(k4, (H, I), jnp.float32) * 0.02
        return {'x': x, 'w_gate': w_gate, 'w_up': w_up, 'w_down': w_down}
    _L0_ffn_all = _L0_ffn_setup()
    _L0_ffn_in = {k: v for k, v in _L0_ffn_all.items() if k in ('w_gate', 'w_up', 'w_down')}
    del _L0_ffn_all
    return {'x': x, 'ctx_1024': ctx_1024, 'L0_attn_Wqkv': _L0_attn_in['Wqkv'], 'L0_attn_Wout': _L0_attn_in['Wout'], 'L0_attn_Wgate': _L0_attn_in['Wgate'], 'L0_attn_bgate': _L0_attn_in['bgate'], 'L0_attn_decay_param': _L0_attn_in['decay_param'], 'L0_ffn_w_gate': _L0_ffn_in['w_gate'], 'L0_ffn_w_up': _L0_ffn_in['w_up'], 'L0_ffn_w_down': _L0_ffn_in['w_down']}

def reference(x, ctx_1024, L0_attn_Wqkv, L0_attn_Wout, L0_attn_Wgate, L0_attn_bgate, L0_attn_decay_param, L0_ffn_w_gate, L0_ffn_w_up, L0_ffn_w_down):
    import jax
    import jax.numpy as jnp

    def _L0_attn_ref(x, Wqkv, Wout, Wgate, bgate, decay_param):
        import jax, jax.numpy as jnp
        import numpy as np
        _SCAN_CHUNK = 32

        def _causal_decay_scan(x, decay, init):
            B, H, T, D = x.shape
            C = min(_SCAN_CHUNK, T)
            assert T % C == 0
            nC = T // C
            log_decay = jnp.log(jnp.clip(decay.astype(jnp.float32), 1e-08, None))
            c_idx = jnp.arange(C, dtype=jnp.float32)
            log_p = log_decay[..., None] * c_idx.reshape(1, 1, C, 1)
            p = jnp.exp(log_p)
            inv_p = jnp.exp(-log_p)
            init_p = jnp.exp(log_decay[..., None] * (c_idx + 1.0).reshape(1, 1, C, 1))
            xc = x.reshape(B, H, nC, C, D).transpose(2, 0, 1, 3, 4).astype(jnp.float32)

            def step(state, chunk):
                cs = jnp.cumsum(chunk * inv_p, axis=2)
                out = cs * p + state[:, :, None, :] * init_p
                return (out[:, :, -1, :], out)
            _, outs = jax.lax.scan(step, init.astype(jnp.float32), xc)
            return outs.transpose(1, 2, 0, 3, 4).reshape(B, H, T, D).astype(x.dtype)

        def _phi(x):
            return jax.nn.elu(x) + 1.0
        B, T, hidden = x.shape
        H = decay_param.shape[0]
        D = hidden // H
        qkv = x @ Wqkv.T
        q, k, v = jnp.split(qkv, 3, axis=-1)
        q = q.reshape(B, T, H, D).transpose(0, 2, 1, 3)
        k = k.reshape(B, T, H, D).transpose(0, 2, 1, 3)
        v = v.reshape(B, T, H, D).transpose(0, 2, 1, 3)
        q = _phi(q)
        k = _phi(k)
        decay = jax.nn.sigmoid(decay_param).reshape(1, H, 1)
        kv_init = jnp.zeros((B, H, D), dtype=x.dtype)
        ksum_init = jnp.zeros((B, H, D), dtype=x.dtype)
        running_kv = _causal_decay_scan(k * v, decay, kv_init)
        running_ksum = _causal_decay_scan(k, decay, ksum_init)
        den = jnp.clip(jnp.sum(q * running_ksum, axis=-1, keepdims=True), 1e-06, None)
        out = q * running_kv / den
        v_direct = v.transpose(0, 2, 1, 3).reshape(B, T, hidden)
        out = out.transpose(0, 2, 1, 3).reshape(B, T, hidden)
        g = jax.nn.sigmoid(out @ Wgate.T + bgate)
        out = g * out + (1.0 - g) * v_direct
        return out @ Wout.T

    def _L0_xattn_ref(q, k, v):
        import jax, jax.numpy as jnp
        import numpy as np
        DECAY = 0.9
        kv = jnp.swapaxes(k * v, 0, 1)

        def step(r, kv_t):
            r = DECAY * r + kv_t
            return (r, r)
        r0 = jnp.zeros(q.shape[:1] + q.shape[2:], dtype=q.dtype)
        _, rs = jax.lax.scan(step, r0, kv)
        return q * jnp.swapaxes(rs, 0, 1)

    def _L0_ffn_ref(x, w_gate, w_up, w_down):
        import jax, jax.numpy as jnp
        import numpy as np
        BLOCK = 32
        W_BITS = 4
        ACT_BITS = 16

        def act_qdq(x):
            qmax = 2.0 ** (ACT_BITS - 1) - 1.0
            scale = jnp.maximum(jnp.max(jnp.abs(x)) / qmax, 1e-12)
            return jnp.clip(jnp.round(x / scale), -qmax - 1.0, qmax) * scale

        def fixed_qdq_u16(x):
            scale = 1.0 / 65536.0
            return jnp.clip(jnp.round(x / scale), 0.0, 65535.0) * scale

        def lpbq_dequant(w):
            O, I = w.shape
            qmax = 2.0 ** (W_BITS - 1) - 1.0
            wb = w.reshape(O, I // BLOCK, BLOCK)
            s = jnp.maximum(jnp.max(jnp.abs(wb), axis=-1, keepdims=True) / qmax, 1e-12)
            wq = jnp.clip(jnp.round(wb / s), -qmax - 1.0, qmax) * s
            return wq.reshape(O, I)
        x = act_qdq(x)
        up = act_qdq(x @ lpbq_dequant(w_up).T)
        gate = act_qdq(x @ lpbq_dequant(w_gate).T)
        sig = fixed_qdq_u16(jax.nn.sigmoid(gate))
        gate = act_qdq(gate * sig)
        o = act_qdq(gate * up)
        return o @ lpbq_dequant(w_down).T
    x = _layernorm(x + _L0_attn_ref(x, L0_attn_Wqkv, L0_attn_Wout, L0_attn_Wgate, L0_attn_bgate, L0_attn_decay_param), axis=-1)
    x = _layernorm(x + _L0_xattn_ref(x, ctx_1024, ctx_1024), axis=-1)
    x = _layernorm(x + _L0_ffn_ref(x, L0_ffn_w_gate, L0_ffn_w_up, L0_ffn_w_down), axis=-1)
    return x

_drawn_inputs = setup_inputs


def setup_inputs(seed=0):
    import zlib

    import numpy as np

    out = dict(_drawn_inputs(seed))
    spreads = {'L0_attn_bgate': (0.0, 0.356), 'L0_attn_decay_param': (2.944438934326172, 0.6)}
    factors = {'L0_attn_Wgate': 23.084}
    for name, (base, spread) in spreads.items():
        noise = np.random.default_rng([zlib.crc32(name.encode()), seed]).standard_normal(out[name].shape)
        drawn = base * np.exp(spread * noise) if base else spread * noise
        out[name] = jnp.asarray(drawn.astype(out[name].dtype))
    for name, factor in factors.items():
        out[name] = (out[name] * factor).astype(out[name].dtype)
    return out
```

```python
import math

import numpy as np
import concourse.bass as bass
from concourse import mybir
from contextlib import ExitStack

F32 = mybir.dt.float32
F32R = mybir.dt.float32r
I16 = mybir.dt.int16
U16 = mybir.dt.uint16
ALU = mybir.AluOpType
ACT = mybir.ActivationFunctionType
AX = mybir.AxisListType

P = 128
NB, T, HID = 16, 512, 512
NH = 16
INNER = 1536
KC = HID // P
TT = T // P
MT = INNER // P
QB = 32
NQB = T // QB
XDECAY = 0.9
LN_EPS = 1e-5
QMAX16 = 32767.0
QMAX4 = 7.0
TINY = 1e-12
MAGIC = 1.5 * 2.0 ** 23
SIG_STEP = 2.0 ** -16
SIG_MAGIC = MAGIC * SIG_STEP


def low16(ap, dt):
    if len(ap.shape) == 2:
        return ap.bitcast(dt).rearrange("p (n h) -> p n h", h=2)[:, :, 0]
    return ap.bitcast(dt).rearrange("p a (n h) -> p a n h", h=2)[:, :, :, 0]


def wait(eng, sem, value):
    if isinstance(value, int) and value <= 0:
        return
    eng.wait_ge(sem, value)


def row_moments(dve, stats, msum, mdiff, m2, ve, parts_ready, square_ready, ve_ready, s):
    dve.tensor_tensor(msum, stats[:, :, 1], stats[:, :, 4], ALU.add).then_inc(parts_ready, 1)
    dve.tensor_tensor(mdiff, stats[:, :, 1], stats[:, :, 4], ALU.subtract).then_inc(parts_ready, 1)
    dve.scalar_tensor_tensor(m2, stats[:, :, 2], HID * LN_EPS, stats[:, :, 5], ALU.add, ALU.add).then_inc(parts_ready, 1)
    dve.wait_ge(parts_ready, 3 * s)
    dve.scalar_tensor_tensor(mdiff, mdiff, 0.25, mdiff, ALU.mult, ALU.mult).then_inc(square_ready, 1)
    dve.wait_ge(square_ready, s)
    dve.scalar_tensor_tensor(ve, m2, 1.0 / HID, mdiff, ALU.mult, ALU.add).then_inc(ve_ready, 1)


def prepare_weights(nc, w_attn, w_ffn, w_ffn_hl, wah, wal):
    NT = 3 * MT
    NA = 5
    with ExitStack() as ctx:
        def sb(name, shape, dt=F32):
            return ctx.enter_context(nc.sbuf_tensor(name, shape, dt))

        def sem(name):
            return ctx.enter_context(nc.semaphore(name))

        stage = sb("wa_stage", [P, 2, KC, T])
        w_raw = sb("w_raw", [P, 2, T])
        w_int = sb("w_int", [P, 2, T])
        w_deq = sb("w_deq", [P, 2, T])
        w_hi = sb("w_hi", [P, 2, T], F32R)
        w_lo = sb("w_lo", [P, 2, T], F32R)
        blk_max = sb("blk_max", [P, 2, NQB])
        blk_scale = sb("blk_scale", [P, 2, NQB])
        blk_inv = sb("blk_inv", [P, 2, NQB])
        ident = sb("w_ident", [P, P])
        turned = [ctx.enter_context(nc.psum_tensor(f"w_turned{i}", [P, T], F32)) for i in range(2)]
        wa_in = [sem(f"wa_in{i}") for i in range(2)]
        raw_in = [sem(f"w_raw_in{i}") for i in range(2)]
        stored = [sem(f"w_stored{i}") for i in range(2)]
        ident_ready = sem("w_ident_ready")
        wah_ready, wal_ready = sem("wah_ready"), sem("wal_ready")
        max_ready, scale_ready, inv_ready = sem("max_ready"), sem("scale_ready"), sem("inv_ready")
        ratio_ready, int_ready, deq_ready = sem("ratio_ready"), sem("int_ready"), sem("deq_ready")
        turned_ready, hi_ready, lo_ready = sem("turned_ready"), sem("hi_ready"), sem("lo_ready")

        with nc.Block() as block:
            @block.sync
            def _(sp):
                for g in range(NA):
                    if g >= 2:
                        sp.wait_ge(wal_ready, g - 1)
                    sp.dma_start(stage[:, g % 2], w_attn[:, :, g]).then_inc(wa_in[g % 2], 16)
                for u in range(2):
                    sp.dma_start(w_raw[:, u], w_ffn[u]).then_inc(raw_in[u], 16)
                with sp.Fori(0, NT // 2 - 1) as i:
                    for u in range(2):
                        t = 2 * i + u
                        sp.wait_ge(ratio_ready, t + 1)
                        sp.dma_start(w_raw[:, u], w_ffn[t + 2]).then_inc(raw_in[u], 16)
                        sp.wait_ge(lo_ready, t + 1)
                        sp.dma_start(w_ffn_hl[0, t], w_hi[:, u].bitcast(F32)).then_inc(stored[u], 16)
                        sp.dma_start(w_ffn_hl[1, t], w_lo[:, u].bitcast(F32)).then_inc(stored[u], 16)
                for u in range(2):
                    t = NT - 2 + u
                    sp.wait_ge(lo_ready, t + 1)
                    sp.dma_start(w_ffn_hl[0, t], w_hi[:, u].bitcast(F32)).then_inc(stored[u], 16)
                    sp.dma_start(w_ffn_hl[1, t], w_lo[:, u].bitcast(F32)).then_inc(stored[u], 16)
                for u in range(2):
                    sp.wait_ge(stored[u], 32 * (NT // 2))

            @block.gpsimd
            def _(pool):
                pool.memset(ident[:], 0.0).then_inc(ident_ready, 1)
                pool.wait_ge(ident_ready, 1)
                pool.affine_select(out=ident[:], in_=ident[:], compare_op=ALU.not_equal, fill=1.0,
                                   base=0, pattern=[[-1, P]], channel_multiplier=1).then_inc(ident_ready, 1)

                def ratio(t, u):
                    pool.wait_ge(inv_ready, t + 1)
                    wait(pool, int_ready, t - 1)
                    wait(pool, deq_ready, t - 1)
                    pool.tensor_tensor(
                        w_int[:, u].rearrange("p (b q) -> p b q", q=QB),
                        w_raw[:, u].rearrange("p (b q) -> p b q", q=QB),
                        blk_inv[:, u].unsqueeze(2).to_broadcast([P, NQB, QB]), ALU.mult).then_inc(ratio_ready, 1)
                for t in range(2):
                    ratio(t, t)
                with pool.Fori(1, NT // 2) as i:
                    for u in range(2):
                        ratio(2 * i + u, u)

            @block.vector
            def _(dve):
                for g in range(NA):
                    dve.wait_ge(wah_ready, g + 1)
                    dve.tensor_tensor(wal[:, :, g], stage[:, g % 2], wah[:, :, g].bitcast(F32),
                                      ALU.subtract).then_inc(wal_ready, 1)

                def scales(t, u, k):
                    dve.wait_ge(raw_in[u], 16 * (k + 1))
                    wait(dve, ratio_ready, t - 1)
                    dve.tensor_reduce(blk_max[:, u], w_raw[:, u].rearrange("p (b q) -> p b q", q=QB), AX.X,
                                      ALU.max, apply_absolute_value=True).then_inc(max_ready, 1)
                    dve.wait_ge(max_ready, t + 1)
                    dve.tensor_scalar(blk_scale[:, u], blk_max[:, u], 1.0 / QMAX4, TINY,
                                      ALU.mult, ALU.max).then_inc(scale_ready, 1)
                    dve.wait_ge(scale_ready, t + 1)
                    dve.reciprocal(blk_inv[:, u], blk_scale[:, u]).then_inc(inv_ready, 1)

                def quantize(t, u):
                    dve.wait_ge(ratio_ready, t + 1)
                    dve.tensor_scalar(w_int[:, u], w_int[:, u], MAGIC, -MAGIC, ALU.add, ALU.add).then_inc(int_ready, 1)
                    dve.wait_ge(int_ready, t + 1)
                    wait(dve, turned_ready, t - 1)
                    dve.tensor_tensor(
                        w_deq[:, u].rearrange("p (b q) -> p b q", q=QB),
                        w_int[:, u].rearrange("p (b q) -> p b q", q=QB),
                        blk_scale[:, u].unsqueeze(2).to_broadcast([P, NQB, QB]), ALU.mult).then_inc(deq_ready, 1)

                def low_half(t, u):
                    dve.wait_ge(hi_ready, t + 1)
                    dve.tensor_tensor(w_lo[:, u], turned[u][:], w_hi[:, u].bitcast(F32), ALU.subtract).then_inc(lo_ready, 1)

                scales(0, 0, 0)
                scales(1, 1, 0)
                quantize(0, 0)
                quantize(1, 1)
                with dve.Fori(1, NT // 2) as i:
                    for u in range(2):
                        scales(2 * i + u, u, i)
                        low_half(2 * i + u - 2, u)
                    for u in range(2):
                        quantize(2 * i + u, u)
                low_half(NT - 2, 0)
                low_half(NT - 1, 1)

            @block.tensor
            def _(pe):
                pe.wait_ge(ident_ready, 2)

                def turn(t, u):
                    pe.wait_ge(deq_ready, t + 1)
                    wait(pe, lo_ready, t - 1)
                    for k in range(KC):
                        mm = pe.transpose(turned[u][:, k * P:(k + 1) * P], w_deq[:, u, k * P:(k + 1) * P], ident[:])
                    mm.then_inc(turned_ready, 1)
                for t in range(2):
                    turn(t, t)
                with pe.Fori(1, NT // 2) as i:
                    for u in range(2):
                        turn(2 * i + u, u)

            @block.scalar
            def _(act):
                for g in range(NA):
                    act.wait_ge(wa_in[g % 2], 16 * (g // 2 + 1))
                    act.activation(wah[:, :, g], stage[:, g % 2], ACT.Copy).then_inc(wah_ready, 1)

                def high_half(t, u, k):
                    act.wait_ge(turned_ready, t + 1)
                    wait(act, stored[u], 32 * k)
                    act.activation(w_hi[:, u], turned[u][:], ACT.Copy).then_inc(hi_ready, 1)
                for t in range(2):
                    high_half(t, t, 0)
                with act.Fori(1, NT // 2) as i:
                    for u in range(2):
                        high_half(2 * i + u, u, i)


def attention_phase(nc, xT, x, ctx_in, b_gate, decay_in, wah, wal, x2_dram, amax_x2):
    with ExitStack() as ctx:
        def sb(name, shape, dt=F32):
            return ctx.enter_context(nc.sbuf_tensor(name, shape, dt))

        def sem(name):
            return ctx.enter_context(nc.semaphore(name))

        xt_raw = sb("xt_raw", [P, 2, T])
        xh = sb("xh", [P, KC, T], F32R)
        xl = sb("xl", [P, KC, T], F32R)
        xrow = sb("xrow", [P, TT, HID])
        csq = sb("csq", [P, TT, HID])
        csq_h = sb("csq_h", [P, TT, HID], F32R)
        csq_l = sb("csq_l", [P, TT, HID], F32R)
        phi = sb("phi", [P, 2, 2, T])
        v_sb = sb("v_sb", [P, 2, KC, T])
        att = sb("att", [P, KC, T])
        ah = sb("ah", [P, KC, T], F32R)
        al = sb("al", [P, KC, T], F32R)
        kv = sb("kv", [P, 2, T])
        qks = sb("qks", [P, KC, T])
        den_rec = sb("den_rec", [NH, T])
        stripf = sb("stripf", [P, T])
        strip_h = sb("strip_h", [P, T], F32R)
        strip_l = sb("strip_l", [P, T], F32R)
        head_sum = sb("head_sum", [P, KC, NH])
        head_bc = sb("head_bc", [NH, KC, P])
        c09 = sb("c09", [P, 1])
        decay = sb("decay", [P, KC])
        half_bg = sb("half_bg", [P, KC])
        dtmp = sb("dtmp", [P, KC])
        dtmp2 = sb("dtmp2", [P, KC])
        mhalf = sb("mhalf", [P, TT])
        stats = [sb(f"stats{n}", [P, TT, 6]) for n in range(2)]
        msum = [sb(f"msum{n}", [P, TT]) for n in range(2)]
        mdiff = [sb(f"mdiff{n}", [P, TT]) for n in range(2)]
        msq = [sb(f"msq{n}", [P, TT]) for n in range(2)]
        var_eps = [sb(f"var_eps{n}", [P, TT]) for n in range(2)]
        rstd = [sb(f"rstd{n}", [P, TT]) for n in range(2)]
        nmr = [sb(f"nmr{n}", [P, TT]) for n in range(2)]
        amax_step = sb("amax_step", [P, 1])

        qk_ps = [ctx.enter_context(nc.psum_tensor(f"qk_ps{i}", [P, 2, T], F32)) for i in range(2)]
        v_ps = [ctx.enter_context(nc.psum_tensor(f"v_ps{i}", [P, T], F32)) for i in range(2)]
        mix_ps = [ctx.enter_context(nc.psum_tensor(f"mix_ps{i}", [P, T], F32)) for i in range(2)]

        xt_in = [sem(f"xt_in{i}") for i in range(2)]
        xrow_in, ctx_landed, x2_stored, small_in = sem("xrow_in"), sem("ctx_landed"), sem("x2_stored"), sem("small_in")
        xh_ready, xl_ready = sem("xh_ready"), sem("xl_ready")
        qk_ready, v_ready = sem("qk_ready"), sem("v_ready")
        neg_ready, e_ready, v_copied = sem("neg_ready"), sem("e_ready"), sem("v_copied")
        phi_ready, kv_ready, ks_scanned, kv_scanned = sem("phi_ready"), sem("kv_ready"), sem("ks_scanned"), sem("kv_scanned")
        qks_ready, qkv_ready = sem("qks_ready"), sem("qkv_ready")
        den_ready, den_clipped, rec_ready, bc_ready, o_ready = (
            sem("den_ready"), sem("den_clipped"), sem("rec_ready"), sem("bc_ready"), sem("o_ready"))
        oh_ready, ol_ready, diff_ready = sem("oh_ready"), sem("ol_ready"), sem("diff_ready")
        gate_ready, tanh_ready, gated, mixed = sem("gate_ready"), sem("tanh_ready"), sem("gated"), sem("mixed")
        mh_ready, ml_ready, proj_ready = sem("mh_ready"), sem("ml_ready"), sem("proj_ready")
        y_ready = [sem("y1_ready"), sem("y2_ready")]
        stats_ready = [sem("stats1_ready"), sem("stats2_ready")]
        moments_ready = [sem("moments1_ready"), sem("moments2_ready")]
        square_ready = [sem("square1_ready"), sem("square2_ready")]
        ve_ready = [sem("ve1_ready"), sem("ve2_ready")]
        rstd_ready = [sem("rstd1_ready"), sem("rstd2_ready")]
        nmr_ready = [sem("nmr1_ready"), sem("nmr2_ready")]
        norm_ready = [sem("norm1_ready"), sem("norm2_ready")]
        sq_ready, sqh_ready, sql_ready, scan_ready = sem("sq_ready"), sem("sqh_ready"), sem("sql_ready"), sem("scan_ready")
        amax_step_ready, amax_taken = sem("amax_step_ready"), sem("amax_taken")
        const_pool, const_dve, const_act = sem("const_pool"), sem("const_dve"), sem("const_act")
        NPOOL = 11

        with nc.Block() as block:
            @block.sync
            def _(sp):
                def load_xt(b, k):
                    wait(sp, xl_ready, 4 * b + k - 1)
                    sp.dma_start(xt_raw[:, k % 2], xT[b, k]).then_inc(xt_in[k % 2], 16)

                def step(s, front, back, nxt):
                    if nxt:
                        for k in range(KC):
                            load_xt(s + 1, k)
                    if back:
                        sp.wait_ge(norm_ready[1], TT * s)
                        sp.dma_start(x2_dram[s - 1], xrow[:]).then_inc(x2_stored, 16)
                    if front:
                        wait(sp, sql_ready, s)
                        sp.dma_start(csq[:], ctx_in[s]).then_inc(ctx_landed, 16)
                        if back:
                            sp.wait_ge(x2_stored, 16 * s)
                            sp.wait_ge(amax_step_ready, s)
                        sp.dma_start(xrow[:], x[s]).then_inc(xrow_in, 16)

                for k in range(KC):
                    load_xt(0, k)
                    if k == 0:
                        for c in range(KC):
                            sp.dma_start(half_bg[:, c:c + 1], b_gate[c]).then_inc(small_in, 16)
                            sp.dma_start(dtmp[:, c:c + 1], decay_in[c]).then_inc(small_in, 16)
                step(0, True, False, True)
                with sp.Fori(0, (NB - 2) // 2) as i:
                    for u in range(2):
                        step(2 * i + 1 + u, True, True, True)
                step(NB - 1, True, True, False)
                step(NB, False, True, False)
                sp.wait_ge(x2_stored, 16 * NB)

            @block.gpsimd
            def _(pool):
                pool.memset(head_sum[:], 1.0).then_inc(const_pool, 1)
                pool.memset(head_bc[:], 1.0).then_inc(const_pool, 1)
                pool.memset(stripf[:], 0.0).then_inc(const_pool, 1)
                pool.memset(mhalf[:], -0.5).then_inc(const_pool, 1)
                pool.memset(c09[:], XDECAY).then_inc(const_pool, 1)
                pool.memset(amax_x2[:], 0.0).then_inc(const_pool, 1)
                D = HID // NH
                pool.wait_ge(const_pool, 6)
                pool.affine_select(out=head_sum[:], in_=head_sum[:], compare_op=ALU.is_ge, fill=0.0,
                                   base=0, pattern=[[P, KC], [-D, NH]], channel_multiplier=1).then_inc(const_pool, 1)
                pool.affine_select(out=head_bc[:], in_=head_bc[:], compare_op=ALU.is_ge, fill=0.0,
                                   base=0, pattern=[[P, KC], [1, P]], channel_multiplier=-D).then_inc(const_pool, 1)
                pool.affine_select(out=stripf[:], in_=stripf[:], compare_op=ALU.not_equal, fill=1.0,
                                   base=0, pattern=[[-1, T]], channel_multiplier=1).then_inc(const_pool, 1)
                pool.wait_ge(const_pool, 9)
                pool.affine_select(out=head_sum[:], in_=head_sum[:], compare_op=ALU.is_ge, fill=0.0,
                                   base=D - 1, pattern=[[-P, KC], [D, NH]], channel_multiplier=-1).then_inc(const_pool, 1)
                pool.affine_select(out=head_bc[:], in_=head_bc[:], compare_op=ALU.is_ge, fill=0.0,
                                   base=D - 1, pattern=[[-P, KC], [-1, P]], channel_multiplier=D).then_inc(const_pool, 1)

                def root(n, s):
                    pool.wait_ge(ve_ready[n], s)
                    pool.tensor_tensor(rstd[n][:], var_eps[n][:], mhalf[:], ALU.pow).then_inc(rstd_ready[n], 1)

                def step(s, front, back):
                    if back:
                        pool.wait_ge(ctx_landed, 16 * s)
                        pool.tensor_tensor(csq[:], csq[:], csq[:], ALU.mult).then_inc(sq_ready, 1)
                        pool.wait_ge(sqh_ready, s)
                        pool.tensor_tensor(csq_l[:], csq[:], csq_h[:].bitcast(F32), ALU.subtract).then_inc(sql_ready, 1)
                        root(0, s)
                        root(1, s)

                with pool.Fori(0, (NB - 2) // 2) as i:
                    for u in range(2):
                        step(2 * i + 1 + u, True, True)
                step(NB - 1, True, True)
                step(NB, False, True)

            @block.scalar
            def _(act):
                act.wait_ge(small_in, 16 * 2 * KC)
                act.activation(dtmp2[:], dtmp[:], ACT.Tanh, scale=0.5).then_inc(const_act, 1)
                act.wait_ge(const_dve, 1)

                def split_x(b):
                    wait(act, v_ready, KC * b)
                    for k in range(KC):
                        act.wait_ge(xt_in[k % 2], 16 * (2 * b + k // 2 + 1))
                        act.activation(xh[:, k], xt_raw[:, k % 2], ACT.Copy).then_inc(xh_ready, 1)

                def front_tile(b, c, par):
                    n = KC * b + c
                    act.wait_ge(qk_ready, n + 1)
                    wait(act, qkv_ready, n - 1)
                    act.activation(phi[:, c % 2], qk_ps[c % 2][:], ACT.Relu, scale=-1.0).then_inc(neg_ready, 1)
                    act.wait_ge(neg_ready, n + 1)
                    act.activation(phi[:, c % 2], phi[:, c % 2], ACT.Exp, scale=-1.0).then_inc(e_ready, 1)
                    act.wait_ge(v_ready, n + 1)
                    act.activation(v_sb[:, par, c], v_ps[c % 2][:], ACT.Copy).then_inc(v_copied, 1)

                def normalise(n, s):
                    act.wait_ge(nmr_ready[n], s)
                    for j in range(TT):
                        act.activation(xrow[:, j], xrow[:, j], ACT.Identity, scale=rstd[n][:, j:j + 1],
                                       bias=nmr[n][:, j:j + 1]).then_inc(norm_ready[n], 1)

                def step(s, par, front, back, nxt):
                    if front:
                        front_tile(s, 0, par)
                    if back:
                        for m in range(KC):
                            act.wait_ge(gate_ready, KC * (s - 1) + m + 1)
                            bank = mix_ps[(m + 1) % 2]
                            act.activation(bank[:], bank[:], ACT.Tanh, scale=0.5,
                                           bias=half_bg[:, m:m + 1]).then_inc(tanh_ready, 1)
                        for m in range(KC):
                            act.wait_ge(mixed, KC * (s - 1) + m + 1)
                            act.activation(ah[:, m], att[:, m], ACT.Copy).then_inc(mh_ready, 1)
                    if front:
                        front_tile(s, 1, par)
                    if back:
                        act.wait_ge(sq_ready, s)
                        wait(act, scan_ready, TT * (s - 1) if not isinstance(s, int) or s > 1 else 0)
                        act.activation(csq_h[:], csq[:], ACT.Copy).then_inc(sqh_ready, 1)
                    if front:
                        front_tile(s, 2, par)
                        front_tile(s, 3, par)
                    if nxt:
                        split_x(s + 1)
                    if back:
                        normalise(0, s)
                        normalise(1, s)
                    if front:
                        for c in range(KC):
                            act.wait_ge(o_ready, KC * s + c + 1)
                            act.activation(ah[:, c], att[:, c], ACT.Copy).then_inc(oh_ready, 1)

                split_x(0)
                step(0, 0, True, False, True)
                step(1, 1, True, True, True)
                step(2, 0, True, True, True)
                with act.Fori(1, (NB - 2) // 2) as i:
                    for u in range(2):
                        step(2 * i + 1 + u, (1 + u) % 2, True, True, True)
                step(NB - 1, 1, True, True, False)
                step(NB, 0, False, True, False)

            @block.vector
            def _(dve):
                dve.wait_ge(small_in, 16 * 2 * KC)
                dve.tensor_scalar(half_bg[:], half_bg[:], 0.5, None, ALU.mult).then_inc(const_dve, 1)
                dve.wait_ge(const_act, 1)
                dve.tensor_scalar(decay[:], dtmp2[:], 0.5, 0.5, ALU.mult, ALU.add).then_inc(const_dve, 1)
                dve.wait_ge(const_dve, 2)
                dve.tensor_scalar(decay[:], decay[:], 1e-8, None, ALU.max).then_inc(const_dve, 1)
                dve.wait_ge(const_pool, NPOOL)
                dve.tensor_tensor_scan(stripf[:], c09[:, 0:1].to_broadcast([P, T]), stripf[:], 0.0,
                                       ALU.mult, ALU.add).then_inc(const_dve, 1)
                dve.wait_ge(const_dve, 4)
                dve.tensor_copy(strip_h[:], stripf[:]).then_inc(const_dve, 1)
                dve.wait_ge(const_dve, 5)
                dve.tensor_tensor(strip_l[:], stripf[:], strip_h[:].bitcast(F32), ALU.subtract).then_inc(const_dve, 1)

                def split_x(b):
                    for k in range(KC):
                        dve.wait_ge(xh_ready, KC * b + k + 1)
                        dve.tensor_tensor(xl[:, k], xt_raw[:, k % 2], xh[:, k].bitcast(F32),
                                          ALU.subtract).then_inc(xl_ready, 1)

                def front_scans(b, c, par):
                    n = KC * b + c
                    sl = c % 2
                    dve.wait_ge(e_ready, n + 1)
                    dve.scalar_tensor_tensor(phi[:, sl], qk_ps[sl][:], 0.0, phi[:, sl], ALU.max, ALU.add).then_inc(phi_ready, 1)
                    dve.wait_ge(phi_ready, n + 1)
                    wait(dve, den_ready, b)
                    dve.tensor_tensor_scan(qks[:, c], decay[:, c:c + 1].to_broadcast([P, T]), phi[:, sl, 1], 0.0,
                                           ALU.mult, ALU.add).then_inc(ks_scanned, 1)
                    dve.wait_ge(v_copied, n + 1)
                    dve.tensor_tensor(kv[:, sl], phi[:, sl, 1], v_sb[:, par, c], ALU.mult).then_inc(kv_ready, 1)
                    dve.wait_ge(ks_scanned, n + 1)
                    dve.tensor_tensor(qks[:, c], phi[:, sl, 0], qks[:, c], ALU.mult).then_inc(qks_ready, 1)
                    dve.wait_ge(kv_ready, n + 1)
                    dve.tensor_tensor_scan(kv[:, sl], decay[:, c:c + 1].to_broadcast([P, T]), kv[:, sl], 0.0,
                                           ALU.mult, ALU.add).then_inc(kv_scanned, 1)

                def front_product(b, c):
                    dve.wait_ge(kv_scanned, KC * b + c + 1)
                    dve.tensor_tensor(att[:, c], phi[:, c % 2, 0], kv[:, c % 2], ALU.mult).then_inc(qkv_ready, 1)

                def norm_scalars(n, s):
                    dve.wait_ge(stats_ready[n], TT * s)
                    row_moments(dve, stats[n], msum[n][:], mdiff[n][:], msq[n][:], var_eps[n][:],
                                moments_ready[n], square_ready[n], ve_ready[n], s)

                def norm_bias(n, s):
                    dve.wait_ge(rstd_ready[n], s)
                    dve.scalar_tensor_tensor(nmr[n][:], msum[n][:], -0.5, rstd[n][:],
                                             ALU.mult, ALU.mult).then_inc(nmr_ready[n], 1)

                def step(s, par, front, back, nxt):
                    if front:
                        front_scans(s, 0, par)
                    if back:
                        for m in range(KC):
                            n = KC * (s - 1) + m + 1
                            dve.wait_ge(tanh_ready, n)
                            dve.wait_ge(diff_ready, n)
                            dve.scalar_tensor_tensor(att[:, m], mix_ps[(m + 1) % 2][:], 1.0, att[:, m],
                                                     ALU.add, ALU.mult).then_inc(gated, 1)
                            dve.wait_ge(gated, n)
                            dve.scalar_tensor_tensor(att[:, m], att[:, m], 0.5, v_sb[:, 1 - par, m],
                                                     ALU.mult, ALU.add).then_inc(mixed, 1)
                        for m in range(KC):
                            dve.wait_ge(mh_ready, KC * (s - 1) + m + 1)
                            dve.tensor_tensor(al[:, m], att[:, m], ah[:, m].bitcast(F32), ALU.subtract).then_inc(ml_ready, 1)
                        dve.wait_ge(ml_ready, KC * s)
                    if front:
                        front_product(s, 0)
                        for c in range(1, KC):
                            front_scans(s, c, par)
                            front_product(s, c)
                    if nxt:
                        split_x(s + 1)
                    if back:
                        dve.wait_ge(xrow_in, 16 * s)
                        for j in range(TT):
                            n = TT * (s - 1) + j + 1
                            dve.wait_ge(proj_ready, n)
                            dve.tensor_tensor(xrow[:, j], mix_ps[(j + 1) % 2][:], xrow[:, j], ALU.add).then_inc(y_ready[0], 1)
                            dve.wait_ge(y_ready[0], n)
                            dve.bn_stats(stats[0][:, j], xrow[:, j]).then_inc(stats_ready[0], 1)
                        norm_scalars(0, s)
                    if front:
                        dve.wait_ge(den_ready, s + 1)
                        dve.tensor_scalar(den_rec[:], mix_ps[1][0:NH, :], 1e-6, None, ALU.max).then_inc(den_clipped, 1)
                        dve.wait_ge(den_clipped, s + 1)
                        dve.reciprocal(den_rec[:], den_rec[:]).then_inc(rec_ready, 1)
                    if back:
                        norm_bias(0, s)
                        for j in range(TT):
                            n = TT * (s - 1) + j + 1
                            dve.wait_ge(norm_ready[0], n)
                            dve.wait_ge(scan_ready, n)
                            dve.scalar_tensor_tensor(xrow[:, j], mix_ps[j % 2][:], 1.0, xrow[:, j],
                                                     ALU.add, ALU.mult).then_inc(y_ready[1], 1)
                            dve.wait_ge(y_ready[1], n)
                            dve.bn_stats(stats[1][:, j], xrow[:, j]).then_inc(stats_ready[1], 1)
                        norm_scalars(1, s)
                        norm_bias(1, s)
                    if front:
                        for c in range(KC):
                            n = KC * s + c + 1
                            dve.wait_ge(bc_ready, n)
                            dve.wait_ge(qkv_ready, n)
                            dve.tensor_tensor(att[:, c], att[:, c], mix_ps[c % 2][:], ALU.mult).then_inc(o_ready, 1)
                        for c in range(KC):
                            n = KC * s + c + 1
                            dve.wait_ge(oh_ready, n)
                            dve.tensor_tensor(al[:, c], att[:, c], ah[:, c].bitcast(F32), ALU.subtract).then_inc(ol_ready, 1)
                            dve.wait_ge(ol_ready, n)
                            dve.tensor_tensor(att[:, c], att[:, c], v_sb[:, par, c], ALU.subtract).then_inc(diff_ready, 1)
                    if back:
                        dve.wait_ge(norm_ready[1], TT * s)
                        dve.tensor_reduce(amax_step[:], xrow[:].rearrange("p j c -> p (j c)"), AX.X, ALU.max,
                                          apply_absolute_value=True).then_inc(amax_step_ready, 1)
                        dve.wait_ge(amax_step_ready, s)
                        dve.tensor_tensor(amax_x2[:], amax_x2[:], amax_step[:], ALU.max).then_inc(amax_taken, 1)
                        dve.wait_ge(amax_taken, s)

                split_x(0)
                step(0, 0, True, False, True)
                with dve.Fori(0, (NB - 2) // 2) as i:
                    for u in range(2):
                        step(2 * i + 1 + u, (1 + u) % 2, True, True, True)
                step(NB - 1, 1, True, True, False)
                step(NB, 0, False, True, False)

            @block.tensor
            def _(pe):
                pe.wait_ge(const_pool, NPOOL)
                pe.wait_ge(const_dve, 6)

                def product(out, stat, mov):
                    n = len(stat)
                    for k in range(n):
                        (sh, sl_), (mh, ml) = stat[k], mov[k]
                        pe.matmul(out, sh, mh, start=(k == 0), stop=False)
                        pe.matmul(out, sh, ml, start=False, stop=False)
                        mm = pe.matmul(out, sl_, mh, start=False, stop=(k == n - 1))
                    return mm

                def w_tile(g, m):
                    cols = slice(m * P, (m + 1) * P)
                    return [(wah[:, k, g, cols], wal[:, k, g, cols]) for k in range(KC)]

                x_halves = [(xh[:, k], xl[:, k]) for k in range(KC)]
                a_halves = [(ah[:, k], al[:, k]) for k in range(KC)]

                def qkv(b, c):
                    n = KC * b + c
                    if c == 0:
                        pe.wait_ge(xl_ready, KC * (b + 1))
                    wait(pe, phi_ready, n - 1)
                    product(qk_ps[c % 2][:, 0], w_tile(0, c), x_halves)
                    product(qk_ps[c % 2][:, 1], w_tile(1, c), x_halves).then_inc(qk_ready, 1)
                    wait(pe, v_copied, n - 1)
                    product(v_ps[c % 2][:], w_tile(2, c), x_halves).then_inc(v_ready, 1)

                def gate(s):
                    pe.wait_ge(ol_ready, KC * s)
                    for m in range(KC):
                        if m < 2:
                            pe.wait_ge(o_ready, KC * s - m)
                        else:
                            pe.wait_ge(gated, KC * (s - 1) + m - 1)
                        product(mix_ps[(m + 1) % 2][:], w_tile(3, m), a_halves).then_inc(gate_ready, 1)

                def project(s):
                    pe.wait_ge(ml_ready, KC * s)
                    for j in range(TT):
                        if j < 2:
                            pe.wait_ge(gated, KC * (s - 1) + j + 3)
                        else:
                            pe.wait_ge(y_ready[0], TT * (s - 1) + j - 1)
                        stat = [(ah[:, k, j * P:(j + 1) * P], al[:, k, j * P:(j + 1) * P]) for k in range(KC)]
                        mov = [(wah[:, k, 4], wal[:, k, 4]) for k in range(KC)]
                        product(mix_ps[(j + 1) % 2][:], stat, mov).then_inc(proj_ready, 1)

                def denominators(s, back):
                    pe.wait_ge(qks_ready, KC * (s + 1))
                    if back:
                        pe.wait_ge(y_ready[0], TT * (s - 1) + 3)
                    for c in range(KC):
                        mm = pe.matmul(mix_ps[1][0:NH, :], head_sum[:, c], qks[:, c], start=(c == 0), stop=(c == KC - 1))
                    mm.then_inc(den_ready, 1)

                def context_scan(s, front):
                    pe.wait_ge(sql_ready, s)
                    for j in range(TT):
                        if j == 0:
                            pe.wait_ge(y_ready[0], TT * s)
                        elif j == 1 and front:
                            pe.wait_ge(den_clipped, s + 1)
                        elif j >= 2:
                            pe.wait_ge(y_ready[1], TT * (s - 1) + j - 1)
                        stat = [(strip_h[:, (j - i) * P:(j - i + 1) * P], strip_l[:, (j - i) * P:(j - i + 1) * P])
                                for i in range(j + 1)]
                        mov = [(csq_h[:, i], csq_l[:, i]) for i in range(j + 1)]
                        product(mix_ps[j % 2][:], stat, mov).then_inc(scan_ready, 1)

                def broadcast(s, back):
                    pe.wait_ge(rec_ready, s + 1)
                    for c in range(KC):
                        if c < 2 and back:
                            pe.wait_ge(y_ready[1], TT * (s - 1) + c + 3)
                        elif c >= 2:
                            pe.wait_ge(o_ready, KC * s + c - 1)
                        pe.matmul(mix_ps[c % 2][:], head_bc[:, c], den_rec[:], start=True, stop=True).then_inc(bc_ready, 1)

                def step(s, front, back):
                    if front:
                        qkv(s, 0)
                    if back:
                        gate(s)
                    if front:
                        for c in range(1, KC):
                            qkv(s, c)
                    if back:
                        project(s)
                    if front:
                        denominators(s, back)
                    if back:
                        context_scan(s, front)
                    if front:
                        broadcast(s, back)

                step(0, True, False)
                with pe.Fori(0, (NB - 2) // 2) as i:
                    for u in range(2):
                        step(2 * i + 1 + u, True, True)
                step(NB - 1, True, True)
                step(NB, False, True)


def up_gate_phase(nc, x2_dram, w_ffn_hl, up_dram, gate_dram, amax_x2, amax_gu, scales):
    NM = 2 * MT
    GM = 4
    NG = NM // GM
    with ExitStack() as ctx:
        def sb(name, shape, dt=F32):
            return ctx.enter_context(nc.sbuf_tensor(name, shape, dt))

        def sem(name):
            return ctx.enter_context(nc.semaphore(name))

        wh = sb("ug_wh", [P, NM, KC, P], F32R)
        wl = sb("ug_wl", [P, NM, KC, P], F32R)
        x2 = sb("ug_x2", [P, TT, HID])
        qh = sb("ug_qh", [P, 2, KC, T], F32R)
        ql = sb("ug_ql", [P, 2, KC, T], F32R)
        group = sb("ug_group", [P, 4, GM, T])
        ident = sb("ug_ident", [P, P])
        gmax = sb("ug_gmax", [P, NG])
        turn_ps = [ctx.enter_context(nc.psum_tensor(f"ug_turn{i}", [P, T], F32)) for i in range(2)]
        out_ps = [ctx.enter_context(nc.psum_tensor(f"ug_out{i}", [P, T], F32)) for i in range(6)]

        w_in, x2_in = sem("ug_w_in"), sem("ug_x2_in")
        stored = [sem(f"ug_stored{i}") for i in range(4)]
        consts, amax_all, scale_ready, inv_ready = sem("ug_consts"), sem("ug_amax_all"), sem("ug_scale_ready"), sem("ug_inv_ready")
        tq_ready, turned, qh_ready, ql_ready = sem("ug_tq_ready"), sem("ug_turned"), sem("ug_qh_ready"), sem("ug_ql_ready")
        out_ready, out_act, out_dve, gmax_ready, gmax_taken = (
            sem("ug_out_ready"), sem("ug_out_act"), sem("ug_out_dve"), sem("ug_gmax_ready"), sem("ug_gmax_taken"))
        s_x, inv_x = scales[:, 0:1], scales[:, 1:2]

        with nc.Block() as block:
            @block.sync
            def _(sp):
                sp.dma_start(x2[:], x2_dram[0]).then_inc(x2_in, 16)
                for half, w in ((0, wh), (1, wl)):
                    for g in range(NG):
                        sp.dma_start(w[:, g * GM:(g + 1) * GM].bitcast(F32),
                                     w_ffn_hl[half, g * GM:(g + 1) * GM].rearrange("m p n -> p m n")).then_inc(w_in, 16)

                def step(b, k, par, nxt):
                    if nxt:
                        sp.wait_ge(turned, KC * (b + 1))
                        sp.dma_start(x2[:], x2_dram[b + 1]).then_inc(x2_in, 16)
                    for g in range(NG):
                        sp.wait_ge(out_act, (GM // 2) * (NG * b + g + 1))
                        sp.wait_ge(out_dve, (GM // 2) * (NG * b + g + 1))
                        dst = (up_dram if g < NG // 2 else gate_dram)[(NG // 2) * b + g % (NG // 2)]
                        sp.dma_start(dst, group[:, (NG * par + g) % 4].rearrange("p m t -> p (m t)")).then_inc(
                            stored[(NG * par + g) % 4], 16)
                with sp.Fori(0, NB // 2 - 1) as i:
                    for u in range(2):
                        step(2 * i + u, i, u, True)
                step(NB - 2, NB // 2 - 1, 0, True)
                step(NB - 1, NB // 2 - 1, 1, False)
                for sl in range(4):
                    sp.wait_ge(stored[sl], 16 * NB * NG // 4)

            @block.gpsimd
            def _(pool):
                pool.memset(ident[:], 0.0).then_inc(consts, 1)
                pool.memset(amax_gu[:], 0.0).then_inc(consts, 1)
                pool.partition_all_reduce(amax_x2[:], amax_x2[:], P, bass.bass_isa.ReduceOp.max).then_inc(amax_all, 1)
                pool.wait_ge(consts, 2)
                pool.affine_select(out=ident[:], in_=ident[:], compare_op=ALU.not_equal, fill=1.0,
                                   base=0, pattern=[[-1, P]], channel_multiplier=1).then_inc(consts, 1)

            def slot(par, g):
                return (NG * par + g) % 4

            @block.scalar
            def _(act):
                act.wait_ge(inv_ready, 1)

                def high(b, par):
                    for c in range(KC):
                        act.wait_ge(turned, KC * b + c + 1)
                        act.activation(qh[:, par, c], low16(turn_ps[c % 2][:], I16), ACT.Copy).then_inc(qh_ready, 1)

                def outputs(b, par, k, g):
                    n = NG * par + g
                    wait(act, stored[n % 4], 16 * (3 * k + n // 4))
                    wait(act, gmax_ready, NG * b + g - 3 if not isinstance(b, int) or NG * b + g >= 4 else 0)
                    for m in range(g * GM, (g + 1) * GM, 2):
                        act.wait_ge(out_ready, NM * b + m + 1)
                        act.activation(group[:, n % 4, m % GM], out_ps[m % 6][:], ACT.Copy, scale=s_x).then_inc(out_act, 1)

                def step(b, par, k, nxt):
                    for g in range(NG):
                        outputs(b, par, k, g)
                        if g == 3 and nxt:
                            high(b + 1, 1 - par)
                high(0, 0)
                step(0, 0, 0, True)
                step(1, 1, 0, True)
                with act.Fori(1, NB // 2 - 1) as i:
                    for u in range(2):
                        step(2 * i + u, u, i, True)
                step(NB - 2, 0, NB // 2 - 1, True)
                step(NB - 1, 1, NB // 2 - 1, False)

            @block.vector
            def _(dve):
                dve.wait_ge(amax_all, 1)
                dve.tensor_scalar(s_x, amax_x2[:], 1.0 / QMAX16, TINY, ALU.mult, ALU.max).then_inc(scale_ready, 1)
                dve.wait_ge(scale_ready, 1)
                dve.reciprocal(inv_x, s_x).then_inc(inv_ready, 1)
                dve.wait_ge(inv_ready, 1)

                def quantize(b):
                    dve.wait_ge(x2_in, 16 * (b + 1))
                    dve.tensor_scalar(x2[:], x2[:], inv_x, MAGIC, ALU.mult, ALU.add).then_inc(tq_ready, 1)

                def low(b, par):
                    for c in range(KC):
                        dve.wait_ge(qh_ready, KC * b + c + 1)
                        dve.tensor_tensor(ql[:, par, c], low16(turn_ps[c % 2][:], I16), qh[:, par, c].bitcast(F32),
                                          ALU.subtract).then_inc(ql_ready, 1)

                def outputs(b, par, k, g):
                    n = NG * par + g
                    wait(dve, stored[n % 4], 16 * (3 * k + n // 4))
                    for m in range(g * GM + 1, (g + 1) * GM, 2):
                        dve.wait_ge(out_ready, NM * b + m + 1)
                        dve.tensor_scalar(group[:, n % 4, m % GM], out_ps[m % 6][:], s_x, None, ALU.mult).then_inc(out_dve, 1)
                    dve.wait_ge(out_act, (GM // 2) * (NG * b + g + 1))
                    dve.wait_ge(out_dve, (GM // 2) * (NG * b + g + 1))
                    dve.tensor_reduce(gmax[:, g:g + 1], group[:, n % 4].rearrange("p m t -> p (m t)"), AX.X, ALU.max,
                                      apply_absolute_value=True).then_inc(gmax_ready, 1)

                def step(b, par, k, nxt):
                    for g in range(NG):
                        if g == 1 and nxt:
                            quantize(b + 1)
                        outputs(b, par, k, g)
                        if g == 3 and nxt:
                            low(b + 1, 1 - par)
                    dve.wait_ge(gmax_ready, NG * (b + 1))
                    dve.tensor_tensor(amax_gu[:], amax_gu[:], gmax[:], ALU.max).then_inc(gmax_taken, 1)
                    dve.wait_ge(gmax_taken, b + 1)

                dve.wait_ge(consts, 3)
                quantize(0)
                low(0, 0)
                step(0, 0, 0, True)
                step(1, 1, 0, True)
                with dve.Fori(1, NB // 2 - 1) as i:
                    for u in range(2):
                        step(2 * i + u, u, i, True)
                step(NB - 2, 0, NB // 2 - 1, True)
                step(NB - 1, 1, NB // 2 - 1, False)

            @block.tensor
            def _(pe):
                pe.wait_ge(consts, 3)

                def turn(b, tiles):
                    pe.wait_ge(tq_ready, b + 1)
                    for c in tiles:
                        wait(pe, ql_ready, KC * b + c - 1)
                        for j in range(TT):
                            mm = pe.transpose(turn_ps[c % 2][:, j * P:(j + 1) * P], x2[:, j, c * P:(c + 1) * P], ident[:])
                        mm.then_inc(turned, 1)

                def tile(b, par, m):
                    wait(pe, out_act if m % 2 == 0 else out_dve,
                         MT * b + m // 2 - 2 if not isinstance(b, int) or MT * b + m // 2 > 2 else 0)
                    for k in range(KC):
                        o = out_ps[m % 6][:]
                        pe.matmul(o, wh[:, m, k], qh[:, par, k], start=(k == 0), stop=False)
                        pe.matmul(o, wh[:, m, k], ql[:, par, k], start=False, stop=False)
                        mm = pe.matmul(o, wl[:, m, k], qh[:, par, k], start=False, stop=(k == KC - 1))
                    mm.then_inc(out_ready, 1)

                def step(b, par, nxt):
                    pe.wait_ge(ql_ready, KC * (b + 1))
                    for m in range(NM):
                        tile(b, par, m)
                        if m == 15 and nxt:
                            turn(b + 1, (0, 1))
                        if m == 17 and nxt:
                            turn(b + 1, (2, 3))
                turn(0, range(KC))
                pe.wait_ge(w_in, 16 * 2 * NG)
                step(0, 0, True)
                step(1, 1, True)
                with pe.Fori(1, NB // 2 - 1) as i:
                    for u in range(2):
                        step(2 * i + u, u, True)
                step(NB - 2, 0, True)
                step(NB - 1, 1, False)


def quantizer(dve, scale, inv, amax, sem, count):
    dve.tensor_scalar(scale, amax, 1.0 / QMAX16, TINY, ALU.mult, ALU.max).then_inc(sem, 1)
    dve.wait_ge(sem, count + 1)
    dve.reciprocal(inv, scale).then_inc(sem, 1)
    dve.wait_ge(sem, count + 2)
    return count + 2


NCH = NB * 3
CH = 4 * T


def silu_max_phase(nc, gate_dram, amax_gu, amax_gs, scales):
    with ExitStack() as ctx:
        def sb(name, shape, dt=F32):
            return ctx.enter_context(nc.sbuf_tensor(name, shape, dt))

        def sem(name):
            return ctx.enter_context(nc.semaphore(name))

        R = 3
        g = sb("sm_g", [P, R, CH])
        sg = sb("sm_sg", [P, R, CH])
        step_max = sb("sm_step_max", [P, 1])
        magic = sb("sm_magic", [P, 1])
        g_in = [sem(f"sm_g_in{i}") for i in range(R)]
        consts, amax_all, sc = sem("sm_consts"), sem("sm_amax_all"), sem("sm_scales")
        tg_ready, sig_ready, ts_ready, gs_ready, max_ready, taken = (
            sem("sm_tg_ready"), sem("sm_sig_ready"), sem("sm_ts_ready"), sem("sm_gs_ready"), sem("sm_max_ready"), sem("sm_taken"))
        s_u, inv_u, s_g, inv_g = (scales[:, i:i + 1] for i in range(2, 6))

        with nc.Block() as block:
            @block.sync
            def _(sp):
                for t in range(R):
                    sp.dma_start(g[:, t], gate_dram[t]).then_inc(g_in[t], 16)
                with sp.Fori(1, NCH // R) as i:
                    for u in range(R):
                        sp.wait_ge(gs_ready, R * i + u - R + 1)
                        sp.dma_start(g[:, u], gate_dram[R * i + u]).then_inc(g_in[u], 16)

            @block.gpsimd
            def _(pool):
                pool.memset(amax_gs[:], 0.0).then_inc(consts, 1)
                pool.memset(magic[:], MAGIC).then_inc(consts, 1)
                pool.partition_all_reduce(amax_gu[:], amax_gu[:], P, bass.bass_isa.ReduceOp.max).then_inc(amax_all, 1)

            @block.scalar
            def _(act):
                act.wait_ge(sc, 6)
                act.wait_ge(consts, 2)
                with act.Fori(0, NCH // R) as i:
                    for u in range(R):
                        t = R * i + u
                        act.wait_ge(g_in[u], 16 * i + 16)
                        act.activation(g[:, u], g[:, u], ACT.Identity, scale=inv_g, bias=magic[:]).then_inc(tg_ready, 1)
                        act.wait_ge(tg_ready, t + 1)
                        act.wait_ge(max_ready, t + 1)
                        act.activation(sg[:, u], low16(g[:, u], I16), ACT.Sigmoid, scale=s_g).then_inc(sig_ready, 1)

            @block.vector
            def _(dve):
                dve.wait_ge(amax_all, 1)
                dve.tensor_reduce(step_max[:], amax_gu[:, 0:3], AX.X, ALU.max).then_inc(sc, 1)
                dve.wait_ge(sc, 1)
                n = quantizer(dve, s_u, inv_u, step_max[:], sc, 1)
                dve.tensor_reduce(step_max[:], amax_gu[:, 3:6], AX.X, ALU.max).then_inc(sc, 1)
                dve.wait_ge(sc, n + 1)
                quantizer(dve, s_g, inv_g, step_max[:], sc, n + 1)
                dve.wait_ge(consts, 2)
                dve.sem_inc(max_ready, R)
                with dve.Fori(0, NCH // R) as i:
                    for u in range(R):
                        t = R * i + u
                        dve.wait_ge(sig_ready, t + 1)
                        dve.tensor_scalar(sg[:, u], sg[:, u], 65535.0 * SIG_STEP, SIG_MAGIC, ALU.min, ALU.add).then_inc(ts_ready, 1)
                        dve.wait_ge(ts_ready, t + 1)
                        dve.tensor_tensor(sg[:, u], low16(g[:, u], I16), low16(sg[:, u], U16), ALU.mult).then_inc(gs_ready, 1)
                        dve.wait_ge(gs_ready, t + 1)
                        dve.tensor_reduce(step_max[:], sg[:, u], AX.X, ALU.max, apply_absolute_value=True).then_inc(max_ready, 1)
                        dve.wait_ge(max_ready, R + t + 1)
                        dve.tensor_tensor(amax_gs[:], amax_gs[:], step_max[:], ALU.max).then_inc(taken, 1)
                        dve.wait_ge(taken, t + 1)


def product_phase(nc, up_dram, gate_dram, o_dram, amax_gs, amax_o, scales):
    with ExitStack() as ctx:
        def sb(name, shape, dt=F32):
            return ctx.enter_context(nc.sbuf_tensor(name, shape, dt))

        def sem(name):
            return ctx.enter_context(nc.semaphore(name))

        R = 3
        g = sb("pr_g", [P, R, CH])
        up = sb("pr_up", [P, R, CH])
        sg = sb("pr_sg", [P, R, CH])
        o = sb("pr_o", [P, R, CH])
        step_max = sb("pr_step_max", [P, 1])
        tmp = sb("pr_tmp", [P, 4])
        magic = sb("pr_magic", [P, 1])
        g_in = [sem(f"pr_g_in{i}") for i in range(R)]
        up_in = [sem(f"pr_up_in{i}") for i in range(R)]
        o_out = [sem(f"pr_o_out{i}") for i in range(R)]
        consts, amax_all, sc = sem("pr_consts"), sem("pr_amax_all"), sem("pr_scales")
        tg_ready, sig_ready, ts_ready, gs_ready, tgs_ready, tu_ready, o_ready, max_ready, taken = (
            sem("pr_tg_ready"), sem("pr_sig_ready"), sem("pr_ts_ready"), sem("pr_gs_ready"), sem("pr_tgs_ready"),
            sem("pr_tu_ready"), sem("pr_o_ready"), sem("pr_max_ready"), sem("pr_taken"))
        s_u, inv_u, s_g, inv_g, s_gs, inv_gs, gs_factor = (scales[:, i:i + 1] for i in range(2, 9))

        with nc.Block() as block:
            @block.sync
            def _(sp):
                def load(t, u):
                    sp.dma_start(g[:, u], gate_dram[t]).then_inc(g_in[u], 16)
                    sp.dma_start(up[:, u], up_dram[t]).then_inc(up_in[u], 16)
                for t in range(R):
                    load(t, t)
                with sp.Fori(0, NCH // R - 1) as i:
                    for u in range(R):
                        sp.wait_ge(o_ready, R * i + u + 1)
                        sp.dma_start(o_dram[R * i + u], o[:, u]).then_inc(o_out[u], 16)
                        load(R * i + u + R, u)
                for u in range(R):
                    sp.wait_ge(o_ready, NCH - R + u + 1)
                    sp.dma_start(o_dram[NCH - R + u], o[:, u]).then_inc(o_out[u], 16)
                for u in range(R):
                    sp.wait_ge(o_out[u], 16 * (NCH // R))

            @block.gpsimd
            def _(pool):
                pool.memset(amax_o[:], 0.0).then_inc(consts, 1)
                pool.memset(magic[:], MAGIC).then_inc(consts, 1)
                pool.partition_all_reduce(amax_gs[:], amax_gs[:], P, bass.bass_isa.ReduceOp.max).then_inc(amax_all, 1)

            @block.scalar
            def _(act):
                act.wait_ge(sc, 5)
                act.wait_ge(consts, 2)

                def tail(t, u):
                    act.wait_ge(gs_ready, t + 1)
                    act.activation(sg[:, u], sg[:, u], ACT.Identity, scale=gs_factor, bias=magic[:]).then_inc(tgs_ready, 1)

                def head(t, u, k):
                    act.wait_ge(g_in[u], 16 * k + 16)
                    act.activation(g[:, u], g[:, u], ACT.Identity, scale=inv_g, bias=magic[:]).then_inc(tg_ready, 1)
                    act.wait_ge(tg_ready, t + 1)
                    wait(act, o_ready, t + 1 - R)
                    act.activation(sg[:, u], low16(g[:, u], I16), ACT.Sigmoid, scale=s_g).then_inc(sig_ready, 1)
                    act.wait_ge(up_in[u], 16 * k + 16)
                    act.activation(up[:, u], up[:, u], ACT.Identity, scale=inv_u, bias=magic[:]).then_inc(tu_ready, 1)
                head(0, 0, 0)
                for t in range(1, R):
                    head(t, t, 0)
                    tail(t - 1, t - 1)
                with act.Fori(1, NCH // R) as i:
                    for u in range(R):
                        head(R * i + u, u, i)
                        tail(R * i + u - 1, (u - 1) % R)
                tail(NCH - 1, R - 1)

            @block.vector
            def _(dve):
                dve.wait_ge(amax_all, 1)
                dve.tensor_scalar(tmp[:, 0:1], s_g, SIG_STEP, None, ALU.mult).then_inc(sc, 1)
                dve.wait_ge(sc, 1)
                dve.tensor_tensor(tmp[:, 1:2], tmp[:, 0:1], amax_gs[:], ALU.mult).then_inc(sc, 1)
                dve.wait_ge(sc, 2)
                quantizer(dve, s_gs, inv_gs, tmp[:, 1:2], sc, 2)
                dve.tensor_tensor(gs_factor, tmp[:, 0:1], inv_gs, ALU.mult).then_inc(sc, 1)
                dve.wait_ge(consts, 2)

                def head(t, u):
                    dve.wait_ge(sig_ready, t + 1)
                    dve.tensor_scalar(sg[:, u], sg[:, u], 65535.0 * SIG_STEP, SIG_MAGIC, ALU.min, ALU.add).then_inc(ts_ready, 1)
                    dve.wait_ge(ts_ready, t + 1)
                    dve.tensor_tensor(sg[:, u], low16(g[:, u], I16), low16(sg[:, u], U16), ALU.mult).then_inc(gs_ready, 1)

                def tail(t, u, k):
                    dve.wait_ge(tgs_ready, t + 1)
                    dve.wait_ge(tu_ready, t + 1)
                    wait(dve, o_out[u], 16 * k)
                    dve.tensor_tensor(o[:, u], low16(sg[:, u], I16), low16(up[:, u], I16), ALU.mult).then_inc(o_ready, 1)
                    dve.wait_ge(o_ready, t + 1)
                    dve.tensor_reduce(step_max[:], o[:, u], AX.X, ALU.max, apply_absolute_value=True).then_inc(max_ready, 1)
                    dve.wait_ge(max_ready, t + 1)
                    dve.tensor_tensor(amax_o[:], amax_o[:], step_max[:], ALU.max).then_inc(taken, 1)
                    dve.wait_ge(taken, t + 1)
                head(0, 0)
                for t in range(1, R):
                    head(t, t)
                    tail(t - 1, t - 1, 0)
                head(R, 0)
                tail(R - 1, R - 1, 0)
                for t in range(R + 1, 2 * R):
                    head(t, t % R)
                    tail(t - 1, (t - 1) % R, 1)
                with dve.Fori(2, NCH // R) as i:
                    head(R * i, 0)
                    tail(R * i - 1, R - 1, i - 1)
                    for u in range(1, R):
                        head(R * i + u, u)
                        tail(R * i + u - 1, u - 1, i)
                tail(NCH - 1, R - 1, NCH // R - 1)


def down_phase(nc, o_dram, x2_dram, w_ffn_hl, out, amax_o, scales):
    with ExitStack() as ctx:
        def sb(name, shape, dt=F32):
            return ctx.enter_context(nc.sbuf_tensor(name, shape, dt))

        def sem(name):
            return ctx.enter_context(nc.semaphore(name))

        NC3 = 3
        wh = sb("dn_wh", [P, MT, KC, P], F32R)
        wl = sb("dn_wl", [P, MT, KC, P], F32R)
        oi = sb("dn_o", [P, NC3, CH])
        oh = sb("dn_oh", [P, 2, MT, T], F32R)
        ol = sb("dn_ol", [P, 2, MT, T], F32R)
        x2 = sb("dn_x2", [P, 2, TT, HID])
        magic = sb("dn_magic", [P, 1])
        mhalf = sb("dn_mhalf", [P, TT])
        tmp = sb("dn_tmp", [P, 4])
        stats = sb("dn_stats", [P, TT, 6])
        msum, mdiff, msq = (sb(f"dn_{n}", [P, TT]) for n in ("msum", "mdiff", "msq"))
        var_eps = sb("dn_var_eps", [P, TT])
        rstd = sb("dn_rstd", [P, TT])
        nmr = sb("dn_nmr", [P, TT])
        out_ps = [ctx.enter_context(nc.psum_tensor(f"dn_ps{i}", [P, HID], F32)) for i in range(8)]
        w_in = sem("dn_w_in")
        o_in = [sem(f"dn_o_in{i}") for i in range(NC3)]
        x2_in = [sem(f"dn_x2_in{i}") for i in range(2)]
        stored = [sem(f"dn_stored{i}") for i in range(2)]
        consts, amax_all, sc = sem("dn_consts"), sem("dn_amax_all"), sem("dn_scales")
        square_ready = sem("dn_square_ready")
        t_ready, oh_ready, ol_ready, y_ready, sum_ready, stats_ready, moments_ready, ve_ready, rstd_ready, nmr_ready, norm_ready = (
            sem("dn_t_ready"), sem("dn_oh_ready"), sem("dn_ol_ready"), sem("dn_y_ready"), sem("dn_sum_ready"),
            sem("dn_stats_ready"), sem("dn_moments_ready"), sem("dn_ve_ready"), sem("dn_rstd_ready"), sem("dn_nmr_ready"),
            sem("dn_norm_ready"))
        s_u, s_gs, s_o, inv_o, o_factor = (scales[:, i:i + 1] for i in (2, 6, 9, 10, 11))

        with nc.Block() as block:
            @block.sync
            def _(sp):
                def load_o(b, n):
                    sp.dma_start(oi[:, n], o_dram[NC3 * b + n]).then_inc(o_in[n], 16)
                for n in range(NC3):
                    load_o(0, n)
                for u in range(2):
                    sp.dma_start(x2[:, u], x2_dram[u]).then_inc(x2_in[u], 16)
                for half, w in ((0, wh), (1, wl)):
                    for n in range(NC3):
                        t0 = 2 * MT + n * KC
                        sp.dma_start(w[:, n * KC:(n + 1) * KC].bitcast(F32),
                                     w_ffn_hl[half, t0:t0 + KC].rearrange("m p n -> p m n")).then_inc(w_in, 16)

                def step(b, u, k, load_x2, nxt):
                    if nxt:
                        for n in range(NC3):
                            sp.wait_ge(ol_ready, NC3 * b + n + 1)
                            load_o(b + 1, n)
                    sp.wait_ge(norm_ready, TT * (b + 1))
                    sp.dma_start(out[b], x2[:, u]).then_inc(stored[u], 16)
                    if load_x2:
                        sp.wait_ge(stored[u], 16 * (k + 1))
                        sp.dma_start(x2[:, u], x2_dram[b + 2]).then_inc(x2_in[u], 16)
                with sp.Fori(0, NB // 2 - 1) as i:
                    for u in range(2):
                        step(2 * i + u, u, i, True, True)
                step(NB - 2, 0, 0, False, True)
                step(NB - 1, 1, 0, False, False)
                for u in range(2):
                    sp.wait_ge(stored[u], 16 * (NB // 2))

            @block.gpsimd
            def _(pool):
                pool.memset(magic[:], MAGIC).then_inc(consts, 1)
                pool.memset(mhalf[:], -0.5).then_inc(consts, 1)
                pool.partition_all_reduce(amax_o[:], amax_o[:], P, bass.bass_isa.ReduceOp.max).then_inc(amax_all, 1)
                pool.wait_ge(consts, 2)
                with pool.Fori(0, NB) as b:
                    pool.wait_ge(ve_ready, b + 1)
                    pool.tensor_tensor(rstd[:], var_eps[:], mhalf[:], ALU.pow).then_inc(rstd_ready, 1)

            @block.scalar
            def _(act):
                def split(b, u):
                    wait(act, y_ready, TT * (b - 1) if not isinstance(b, int) or b > 1 else 0)
                    for n in range(NC3):
                        act.wait_ge(t_ready, NC3 * b + n + 1)
                        act.activation(oh[:, u, n * KC:(n + 1) * KC].rearrange("p m t -> p (m t)"),
                                       low16(oi[:, n], I16), ACT.Copy).then_inc(oh_ready, 1)

                def normalise(b, u):
                    act.wait_ge(nmr_ready, b + 1)
                    for j in range(TT):
                        act.activation(x2[:, u, j], x2[:, u, j], ACT.Identity, scale=rstd[:, j:j + 1],
                                       bias=nmr[:, j:j + 1]).then_inc(norm_ready, 1)
                split(0, 0)
                split(1, 1)
                normalise(0, 0)
                with act.Fori(0, NB // 2 - 1) as i:
                    for u in range(2):
                        split(2 * i + 2 + u, u)
                        normalise(2 * i + 1 + u, 1 - u)
                normalise(NB - 1, 1)

            @block.vector
            def _(dve):
                dve.wait_ge(amax_all, 1)
                dve.tensor_tensor(tmp[:, 0:1], s_gs, s_u, ALU.mult).then_inc(sc, 1)
                dve.wait_ge(sc, 1)
                dve.tensor_tensor(tmp[:, 1:2], tmp[:, 0:1], amax_o[:], ALU.mult).then_inc(sc, 1)
                dve.wait_ge(sc, 2)
                quantizer(dve, s_o, inv_o, tmp[:, 1:2], sc, 2)
                dve.tensor_tensor(o_factor, tmp[:, 0:1], inv_o, ALU.mult).then_inc(sc, 1)
                dve.wait_ge(sc, 5)
                dve.wait_ge(consts, 2)

                def split(b, u, k):
                    for n in range(NC3):
                        dve.wait_ge(o_in[n], 16 * (b + 1))
                        dve.tensor_scalar(oi[:, n], oi[:, n], o_factor, MAGIC, ALU.mult, ALU.add).then_inc(t_ready, 1)
                    for n in range(NC3):
                        dve.wait_ge(oh_ready, NC3 * b + n + 1)
                        dve.tensor_tensor(ol[:, u, n * KC:(n + 1) * KC].rearrange("p m t -> p (m t)"), low16(oi[:, n], I16),
                                          oh[:, u, n * KC:(n + 1) * KC].rearrange("p m t -> p (m t)").bitcast(F32),
                                          ALU.subtract).then_inc(ol_ready, 1)

                def finish(b, u, k):
                    dve.wait_ge(x2_in[u], 16 * (k + 1))
                    for j in range(TT):
                        n = TT * b + j + 1
                        dve.wait_ge(y_ready, n)
                        dve.scalar_tensor_tensor(x2[:, u, j], out_ps[TT * u + j][:], s_o, x2[:, u, j],
                                                 ALU.mult, ALU.add).then_inc(sum_ready, 1)
                        dve.wait_ge(sum_ready, n)
                        dve.bn_stats(stats[:, j], x2[:, u, j]).then_inc(stats_ready, 1)
                    wait(dve, norm_ready, TT * b)
                    dve.wait_ge(stats_ready, TT * (b + 1))
                    row_moments(dve, stats, msum[:], mdiff[:], msq[:], var_eps[:], moments_ready, square_ready, ve_ready, b + 1)
                    dve.wait_ge(rstd_ready, b + 1)
                    dve.scalar_tensor_tensor(nmr[:], msum[:], -0.5, rstd[:], ALU.mult, ALU.mult).then_inc(nmr_ready, 1)
                split(0, 0, 0)
                split(1, 1, 0)
                finish(0, 0, 0)
                split(2, 0, 1)
                finish(1, 1, 0)
                split(3, 1, 1)
                with dve.Fori(1, NB // 2 - 1) as i:
                    finish(2 * i, 0, i)
                    split(2 * i + 2, 0, i + 1)
                    finish(2 * i + 1, 1, i)
                    split(2 * i + 3, 1, i + 1)
                finish(NB - 2, 0, NB // 2 - 1)
                finish(NB - 1, 1, NB // 2 - 1)

            @block.tensor
            def _(pe):
                def step(b, u):
                    pe.wait_ge(ol_ready, NC3 * (b + 1))
                    wait(pe, sum_ready, TT * (b - 1) if not isinstance(b, int) or b > 1 else 0)
                    for j in range(TT):
                        rows = slice(j * P, (j + 1) * P)
                        o = out_ps[TT * u + j][:].rearrange("p (m n) -> p m n", n=P)
                        for k in range(MT):
                            n, kb = k // KC, k % KC
                            mh, ml = (w[:, n * KC:(n + 1) * KC, kb] for w in (wh, wl))
                            pe.matmul(o, oh[:, u, k, rows], mh, start=(k == 0), stop=False)
                            pe.matmul(o, oh[:, u, k, rows], ml, start=False, stop=False)
                            mm = pe.matmul(o, ol[:, u, k, rows], mh, start=False, stop=(k == MT - 1))
                        mm.then_inc(y_ready, 1)
                pe.wait_ge(w_in, 16 * 2 * NC3)
                step(0, 0)
                step(1, 1)
                with pe.Fori(1, NB // 2) as i:
                    for u in range(2):
                        step(2 * i + u, u)


def decoder(nc, xT, x, ctx_in, w_attn, w_ffn, b_gate, decay, out):
    def scratch(name, shape):
        return nc.dram_tensor(name, shape, F32, kind="Internal").ap()

    w_ffn_hl = scratch("w_ffn_hl", (2, 3 * MT, P, T))
    x2_dram = scratch("x2_rows", (NB, P, TT, HID))
    up_dram = scratch("up_products", (NCH, P, CH))
    gate_dram = scratch("gate_products", (NCH, P, CH))
    o_dram = scratch("product", (NCH, P, CH))
    with ExitStack() as ctx:
        def sb(name, shape, dt=F32):
            return ctx.enter_context(nc.sbuf_tensor(name, shape, dt))
        amax_x2 = sb("amax_x2", [P, 1])
        amax_gu = sb("amax_gu", [P, 6])
        amax_gs = sb("amax_gs", [P, 1])
        amax_o = sb("amax_o", [P, 1])
        scales = sb("scales", [P, 16])
        with ExitStack() as attn:
            wah = attn.enter_context(nc.sbuf_tensor("wah", [P, KC, 5, T], F32R))
            wal = attn.enter_context(nc.sbuf_tensor("wal", [P, KC, 5, T], F32R))
            prepare_weights(nc, w_attn, w_ffn, w_ffn_hl, wah, wal)
            attention_phase(nc, xT, x, ctx_in, b_gate, decay, wah, wal, x2_dram, amax_x2)
        up_gate_phase(nc, x2_dram, w_ffn_hl, up_dram, gate_dram, amax_x2, amax_gu, scales)
        silu_max_phase(nc, gate_dram, amax_gu, amax_gs, scales)
        product_phase(nc, up_dram, gate_dram, o_dram, amax_gs, amax_o, scales)
        down_phase(nc, o_dram, x2_dram, w_ffn_hl, out, amax_o, scales)


def kernel(**inputs):
    import concourse.bacc as bacc
    from concourse.bass_utils import run_bass_kernel_spmd

    a = {k: np.asarray(v) for k, v in inputs.items()}
    arrays = {
        "xT": np.ascontiguousarray(a["x"].transpose(0, 2, 1)).reshape(NB, KC, P, T),
        "x_rows": np.ascontiguousarray(a["x"].reshape(NB, TT, P, HID).transpose(0, 2, 1, 3)),
        "ctx_rows": np.ascontiguousarray(a["ctx_1024"].reshape(NB, TT, P, HID).transpose(0, 2, 1, 3)),
        "w_attn": np.ascontiguousarray(np.concatenate(
            [a["L0_attn_Wqkv"], a["L0_attn_Wgate"], a["L0_attn_Wout"]]).reshape(5, HID, KC, P).transpose(3, 2, 0, 1)),
        "w_ffn": np.ascontiguousarray(np.concatenate(
            [a["L0_ffn_w_up"].reshape(MT, P, HID), a["L0_ffn_w_gate"].reshape(MT, P, HID),
             a["L0_ffn_w_down"].reshape(KC, P, 3, HID).transpose(2, 0, 1, 3).reshape(MT, P, HID)])),
        "b_gate": np.ascontiguousarray(a["L0_attn_bgate"].reshape(KC, P, 1)),
        "decay": np.ascontiguousarray(np.repeat(a["L0_attn_decay_param"], HID // NH).reshape(KC, P, 1)),
    }
    nc = bacc.Bacc("TRN2", target_bir_lowering=False, num_devices=1)
    args = [nc.dram_tensor(f"in_{k}", v.shape, mybir.dt.from_np(v.dtype), kind="ExternalInput").ap()
            for k, v in arrays.items()]
    out = nc.dram_tensor("out_rows", (NB, P, TT, HID), F32, kind="ExternalOutput").ap()
    decoder(nc, *args, out)
    r = run_bass_kernel_spmd(nc, [{f"in_{k}": v for k, v in arrays.items()}], core_ids=[0])
    rows = r.results[0]["out_rows"]
    return np.ascontiguousarray(rows.transpose(0, 2, 1, 3)).reshape(NB, T, HID)
```

```python
import math

import numpy as np
import concourse.bass as bass
from concourse import mybir
from contextlib import ExitStack

F32 = mybir.dt.float32
F32R = mybir.dt.float32r
I16 = mybir.dt.int16
U16 = mybir.dt.uint16
ALU = mybir.AluOpType
ACT = mybir.ActivationFunctionType
AX = mybir.AxisListType

P = 128
NB, T, HID = 16, 512, 512
NH = 16
INNER = 1536
KC = HID // P
TT = T // P
MT = INNER // P
QB = 32
NQB = T // QB
WG = 4
NWG = 3 * MT // WG
XDECAY = 0.9
LN_EPS = 1e-5
QMAX16 = 32767.0
QMAX4 = 7.0
TINY = 1e-12
MAGIC = 1.5 * 2.0 ** 23
SIG_STEP = 2.0 ** -16
SIG_MAGIC = MAGIC * SIG_STEP


def low16(ap, dt):
    if len(ap.shape) == 2:
        return ap.bitcast(dt).rearrange("p (n h) -> p n h", h=2)[:, :, 0]
    return ap.bitcast(dt).rearrange("p a (n h) -> p a n h", h=2)[:, :, :, 0]


def wait(eng, sem, value):
    if isinstance(value, int) and value <= 0:
        return
    eng.wait_ge(sem, value)


def row_moments(dve, stats, msum, mdiff, m2, ve, parts_ready, square_ready, ve_ready, s):
    dve.tensor_tensor(msum, stats[:, :, 1], stats[:, :, 4], ALU.add).then_inc(parts_ready, 1)
    dve.tensor_tensor(mdiff, stats[:, :, 1], stats[:, :, 4], ALU.subtract).then_inc(parts_ready, 1)
    dve.scalar_tensor_tensor(m2, stats[:, :, 2], HID * LN_EPS, stats[:, :, 5], ALU.add, ALU.add).then_inc(parts_ready, 1)
    dve.wait_ge(parts_ready, 3 * s)
    dve.scalar_tensor_tensor(mdiff, mdiff, 0.25, mdiff, ALU.mult, ALU.mult).then_inc(square_ready, 1)
    dve.wait_ge(square_ready, s)
    dve.scalar_tensor_tensor(ve, m2, 1.0 / HID, mdiff, ALU.mult, ALU.add).then_inc(ve_ready, 1)


def phase_semaphore(nc, used, name):
    handle = nc.alloc_semaphore(name)
    used.append(handle)
    return handle


def prepare_weights(nc, w_attn, w_ffn, w_ffn_hl, wah, wal):
    NA = 5
    AR = 3
    DVE_TILES = WG // 2
    with ExitStack() as ctx:
        used = []
        ctx.callback(lambda: (nc.clear_and_free_semaphores(used), nc.all_engine_barrier()))

        def sb(name, shape, dt=F32):
            return ctx.enter_context(nc.sbuf_tensor(name, shape, dt))

        def sem(name):
            return phase_semaphore(nc, used, name)

        stage = sb("wa_stage", [P, AR, KC, T])
        w_raw = sb("w_raw", [P, 2, WG, T])
        w_int = sb("w_int", [P, 2, WG, T])
        w_deq = sb("w_deq", [P, 2, WG, T])
        w_hi = sb("w_hi", [P, 2, WG, T], F32R)
        w_lo = sb("w_lo", [P, 2, WG, T], F32R)
        blk_max = sb("blk_max", [P, 2, WG * NQB])
        blk_scale = sb("blk_scale", [P, 2, WG * NQB])
        blk_inv = sb("blk_inv", [P, 2, WG * NQB])
        ident = sb("w_ident", [P, P])
        turned = [ctx.enter_context(nc.psum_tensor(f"w_turned{i}", [P, WG, T], F32)) for i in range(2)]
        wa_in = [sem(f"wa_in{i}") for i in range(AR)]
        raw_in = [sem(f"w_raw_in{i}") for i in range(2)]
        stored = [sem(f"w_stored{i}") for i in range(2)]
        ident_ready = sem("w_ident_ready")
        wah_ready, wal_ready = sem("wah_ready"), sem("wal_ready")
        max_ready, scale_ready, inv_ready = sem("max_ready"), sem("scale_ready"), sem("inv_ready")
        ratio_ready, int_ready = sem("ratio_ready"), sem("int_ready")
        deq_dve_ready, deq_pool_ready = sem("deq_dve_ready"), sem("deq_pool_ready")
        turned_ready, hi_ready, lo_ready = sem("turned_ready"), sem("hi_ready"), sem("lo_ready")

        def blocks(ap):
            return ap.rearrange("p m (b q) -> p (m b) q", q=QB)

        def per_block(ap, tiles):
            n = len(tiles)
            return ap[:, tiles[0] * NQB:(tiles[-1] + 1) * NQB].unsqueeze(2).to_broadcast([P, n * NQB, QB])

        def multiply_scales(eng, g, u, tiles):
            part = slice(tiles[0], tiles[-1] + 1)
            return eng.tensor_tensor(blocks(w_deq[:, u, part]), blocks(w_int[:, u, part]),
                                     per_block(blk_scale[:, u], tiles), ALU.mult)

        with nc.Block() as block:
            @block.sync
            def _(sp):
                def load_ffn(g, u):
                    sp.dma_start(w_raw[:, u], w_ffn[g]).then_inc(raw_in[u], 16)

                def load_attn(a):
                    if a >= AR:
                        sp.wait_ge(wal_ready, a - AR + 1)
                    sp.dma_start(stage[:, a % AR], w_attn[:, :, a]).then_inc(wa_in[a % AR], 16)

                def step(g, u):
                    sp.wait_ge(ratio_ready, g + 1)
                    load_ffn(g + 2, u)
                load_ffn(0, 0)
                load_attn(0)
                load_ffn(1, 1)
                for a in range(1, NA):
                    load_attn(a)
                step(0, 0)
                with sp.Fori(0, NWG // 2 - 1) as i:
                    step(2 * i + 1, 1)
                    step(2 * i + 2, 0)
                sp.wait_ge(stored[0], 32 * ((NWG + 1) // 2))
                sp.wait_ge(stored[1], 32 * (NWG // 2))

            @block.gpsimd
            def _(pool):
                pool.memset(ident[:], 0.0).then_inc(ident_ready, 1)
                pool.wait_ge(ident_ready, 1)
                pool.affine_select(out=ident[:], in_=ident[:], compare_op=ALU.not_equal, fill=1.0,
                                   base=0, pattern=[[-1, P]], channel_multiplier=1).then_inc(ident_ready, 1)

                def ratio(g, u):
                    pool.wait_ge(inv_ready, g + 1)
                    wait(pool, deq_dve_ready, g - 1)
                    wait(pool, deq_pool_ready, g - 1)
                    pool.tensor_tensor(blocks(w_int[:, u]), blocks(w_raw[:, u]), per_block(blk_inv[:, u], range(WG)),
                                       ALU.mult).then_inc(ratio_ready, 1)

                def scaled(g, u):
                    pool.wait_ge(int_ready, g + 1)
                    wait(pool, turned_ready, g - 1)
                    multiply_scales(pool, g, u, range(DVE_TILES, WG)).then_inc(deq_pool_ready, 1)
                ratio(0, 0)
                ratio(1, 1)
                scaled(0, 0)
                ratio(2, 0)
                scaled(1, 1)
                with pool.Fori(1, NWG // 2) as i:
                    ratio(2 * i + 1, 1)
                    scaled(2 * i, 0)
                    ratio(2 * i + 2, 0)
                    scaled(2 * i + 1, 1)
                scaled(NWG - 1, 0)

            @block.vector
            def _(dve):
                def attn_low(a):
                    dve.wait_ge(wah_ready, a + 1)
                    dve.tensor_tensor(wal[:, :, a], stage[:, a % AR], wah[:, :, a].bitcast(F32),
                                      ALU.subtract).then_inc(wal_ready, 1)

                def scales(g, u, k):
                    dve.wait_ge(raw_in[u], 16 * (k + 1))
                    wait(dve, deq_pool_ready, g - 1)
                    dve.tensor_reduce(blk_max[:, u], blocks(w_raw[:, u]), AX.X,
                                      ALU.max, apply_absolute_value=True).then_inc(max_ready, 1)
                    dve.wait_ge(max_ready, g + 1)
                    dve.tensor_scalar(blk_scale[:, u], blk_max[:, u], 1.0 / QMAX4, TINY,
                                      ALU.mult, ALU.max).then_inc(scale_ready, 1)
                    dve.wait_ge(scale_ready, g + 1)
                    dve.reciprocal(blk_inv[:, u], blk_scale[:, u]).then_inc(inv_ready, 1)

                def quantize(g, u):
                    dve.wait_ge(ratio_ready, g + 1)
                    dve.tensor_scalar(w_int[:, u], w_int[:, u], MAGIC, -MAGIC, ALU.add, ALU.add).then_inc(int_ready, 1)
                    dve.wait_ge(int_ready, g + 1)
                    wait(dve, turned_ready, g - 1)
                    multiply_scales(dve, g, u, range(DVE_TILES)).then_inc(deq_dve_ready, 1)

                def low_half(g, u):
                    dve.wait_ge(hi_ready, g + 1)
                    dve.tensor_tensor(w_lo[:, u], turned[u][:], w_hi[:, u].bitcast(F32), ALU.subtract).then_inc(lo_ready, 1)

                scales(0, 0, 0)
                attn_low(0)
                scales(1, 1, 0)
                quantize(0, 0)
                attn_low(1)
                scales(2, 0, 1)
                quantize(1, 1)
                low_half(0, 0)
                with dve.Fori(1, NWG // 2) as i:
                    scales(2 * i + 1, 1, i)
                    quantize(2 * i, 0)
                    low_half(2 * i - 1, 1)
                    scales(2 * i + 2, 0, i + 1)
                    quantize(2 * i + 1, 1)
                    low_half(2 * i, 0)
                quantize(NWG - 1, 0)
                low_half(NWG - 2, 1)
                attn_low(2)
                low_half(NWG - 1, 0)
                for a in range(AR, NA):
                    attn_low(a)

            @block.tensor
            def _(pe):
                pe.wait_ge(ident_ready, 2)

                def turn(g, u):
                    pe.wait_ge(deq_dve_ready, g + 1)
                    pe.wait_ge(deq_pool_ready, g + 1)
                    wait(pe, lo_ready, g - 1)
                    for m in range(WG):
                        for k in range(KC):
                            mm = pe.transpose(turned[u][:, m, k * P:(k + 1) * P], w_deq[:, u, m, k * P:(k + 1) * P], ident[:])
                    mm.then_inc(turned_ready, 1)
                turn(0, 0)
                turn(1, 1)
                turn(2, 0)
                with pe.Fori(1, NWG // 2) as i:
                    turn(2 * i + 1, 1)
                    turn(2 * i + 2, 0)

            @block.scalar
            def _(act):
                def attn_high(a):
                    act.wait_ge(wa_in[a % AR], 16 * (a // AR + 1))
                    act.activation(wah[:, :, a], stage[:, a % AR], ACT.Copy).then_inc(wah_ready, 1)

                def high_half(g, u, k):
                    act.wait_ge(turned_ready, g + 1)
                    wait(act, stored[u], 32 * k)
                    act.activation(w_hi[:, u], turned[u][:], ACT.Copy).then_inc(hi_ready, 1)

                def store(g, u):
                    act.wait_ge(lo_ready, g + 1)
                    act.dma_start(w_ffn_hl[0, g], w_hi[:, u].bitcast(F32)).then_inc(stored[u], 16)
                    act.dma_start(w_ffn_hl[1, g], w_lo[:, u].bitcast(F32)).then_inc(stored[u], 16)
                for a in range(AR):
                    attn_high(a)
                high_half(0, 0, 0)
                high_half(1, 1, 0)
                store(0, 0)
                high_half(2, 0, 1)
                store(1, 1)
                for a in range(AR, NA):
                    attn_high(a)
                with act.Fori(1, NWG // 2) as i:
                    high_half(2 * i + 1, 1, i)
                    store(2 * i, 0)
                    high_half(2 * i + 2, 0, i + 1)
                    store(2 * i + 1, 1)
                store(NWG - 1, 0)


def attention_phase(nc, xT, x, ctx_in, b_gate, decay_in, wah, wal, x2_dram, amax_x2):
    with ExitStack() as ctx:
        used = []
        ctx.callback(lambda: (nc.clear_and_free_semaphores(used), nc.all_engine_barrier()))

        def sb(name, shape, dt=F32):
            return ctx.enter_context(nc.sbuf_tensor(name, shape, dt))

        def sem(name):
            return phase_semaphore(nc, used, name)

        xt_raw = sb("xt_raw", [P, 2, T])
        xh = sb("xh", [P, KC, T], F32R)
        xl = sb("xl", [P, KC, T], F32R)
        xrow = sb("xrow", [P, TT, HID])
        csq = sb("csq", [P, TT, HID])
        csq_h = sb("csq_h", [P, TT, HID], F32R)
        csq_l = sb("csq_l", [P, TT, HID], F32R)
        phi = sb("phi", [P, 2, 2, T])
        v_sb = sb("v_sb", [P, 2, KC, T])
        att = sb("att", [P, KC, T])
        ah = sb("ah", [P, KC, T], F32R)
        al = sb("al", [P, KC, T], F32R)
        kv = sb("kv", [P, 2, T])
        qks = sb("qks", [P, KC, T])
        den_rec = sb("den_rec", [NH, T])
        stripf = sb("stripf", [P, T])
        strip_h = sb("strip_h", [P, T], F32R)
        strip_l = sb("strip_l", [P, T], F32R)
        head_sum = sb("head_sum", [P, KC, NH])
        head_bc = sb("head_bc", [NH, KC, P])
        c09 = sb("c09", [P, 1])
        decay = sb("decay", [P, KC])
        half_bg = sb("half_bg", [P, KC])
        dtmp = sb("dtmp", [P, KC])
        dtmp2 = sb("dtmp2", [P, KC])
        mhalf = sb("mhalf", [P, TT])
        stats = [sb(f"stats{n}", [P, TT, 6]) for n in range(2)]
        msum = [sb(f"msum{n}", [P, TT]) for n in range(2)]
        mdiff = [sb(f"mdiff{n}", [P, TT]) for n in range(2)]
        msq = [sb(f"msq{n}", [P, TT]) for n in range(2)]
        var_eps = [sb(f"var_eps{n}", [P, TT]) for n in range(2)]
        rstd = [sb(f"rstd{n}", [P, TT]) for n in range(2)]
        nmr = [sb(f"nmr{n}", [P, TT]) for n in range(2)]
        amax_step = sb("amax_step", [P, 1])

        qk_ps = [ctx.enter_context(nc.psum_tensor(f"qk_ps{i}", [P, 2, T], F32)) for i in range(2)]
        v_ps = [ctx.enter_context(nc.psum_tensor(f"v_ps{i}", [P, T], F32)) for i in range(2)]
        mix_ps = [ctx.enter_context(nc.psum_tensor(f"mix_ps{i}", [P, T], F32)) for i in range(2)]
        den_bank = qk_ps[0][0:NH, 0]
        bc_banks = [qk_ps[1][:, 0], qk_ps[1][:, 1], v_ps[1][:], v_ps[0][:]]

        xt_in = [sem(f"xt_in{i}") for i in range(2)]
        xrow_in, ctx_landed, x2_stored, small_in = sem("xrow_in"), sem("ctx_landed"), sem("x2_stored"), sem("small_in")
        xh_ready, xl_ready = sem("xh_ready"), sem("xl_ready")
        qk_ready, v_ready = sem("qk_ready"), sem("v_ready")
        neg_ready, e_ready, v_copied = sem("neg_ready"), sem("e_ready"), sem("v_copied")
        phi_ready, kv_ready, ks_scanned, kv_scanned = sem("phi_ready"), sem("kv_ready"), sem("ks_scanned"), sem("kv_scanned")
        qks_ready, qkv_ready = sem("qks_ready"), sem("qkv_ready")
        den_ready, den_clipped, rec_ready, bc_ready, o_ready = (
            sem("den_ready"), sem("den_clipped"), sem("rec_ready"), sem("bc_ready"), sem("o_ready"))
        oh_ready, ol_ready, diff_ready = sem("oh_ready"), sem("ol_ready"), sem("diff_ready")
        gate_ready, tanh_ready, gated, mixed = sem("gate_ready"), sem("tanh_ready"), sem("gated"), sem("mixed")
        mh_ready, ml_ready, proj_ready = sem("mh_ready"), sem("ml_ready"), sem("proj_ready")
        y_ready = [sem("y1_ready"), sem("y2_ready")]
        stats_ready = [sem("stats1_ready"), sem("stats2_ready")]
        moments_ready = [sem("moments1_ready"), sem("moments2_ready")]
        square_ready = [sem("square1_ready"), sem("square2_ready")]
        ve_ready = [sem("ve1_ready"), sem("ve2_ready")]
        rstd_ready = [sem("rstd1_ready"), sem("rstd2_ready")]
        nmr_ready = [sem("nmr1_ready"), sem("nmr2_ready")]
        norm_ready = [sem("norm1_ready"), sem("norm2_ready")]
        sq_ready, sqh_ready, sql_ready, scan_ready = sem("sq_ready"), sem("sqh_ready"), sem("sql_ready"), sem("scan_ready")
        amax_step_ready, amax_taken = sem("amax_step_ready"), sem("amax_taken")
        const_pool, const_dve, const_act = sem("const_pool"), sem("const_dve"), sem("const_act")
        NPOOL = 11

        with nc.Block() as block:
            @block.sync
            def _(sp):
                def load_xt(b, k):
                    wait(sp, xl_ready, 4 * b + k - 1)
                    sp.dma_start(xt_raw[:, k % 2], xT[b, k]).then_inc(xt_in[k % 2], 16)

                def step(s, front, back, nxt):
                    if nxt:
                        for k in range(KC):
                            load_xt(s + 1, k)
                    if back:
                        sp.wait_ge(norm_ready[1], TT * s)
                        sp.dma_start(x2_dram[s - 1], xrow[:]).then_inc(x2_stored, 16)
                    if front:
                        wait(sp, sql_ready, s)
                        sp.dma_start(csq[:], ctx_in[s]).then_inc(ctx_landed, 16)
                        if back:
                            sp.wait_ge(x2_stored, 16 * s)
                            sp.wait_ge(amax_step_ready, s)
                        sp.dma_start(xrow[:], x[s]).then_inc(xrow_in, 16)

                for k in range(KC):
                    load_xt(0, k)
                    if k == 0:
                        for c in range(KC):
                            sp.dma_start(half_bg[:, c:c + 1], b_gate[c]).then_inc(small_in, 16)
                            sp.dma_start(dtmp[:, c:c + 1], decay_in[c]).then_inc(small_in, 16)
                step(0, True, False, True)
                with sp.Fori(0, (NB - 2) // 2) as i:
                    for u in range(2):
                        step(2 * i + 1 + u, True, True, True)
                step(NB - 1, True, True, False)
                step(NB, False, True, False)
                sp.wait_ge(x2_stored, 16 * NB)

            @block.gpsimd
            def _(pool):
                pool.memset(head_sum[:], 1.0).then_inc(const_pool, 1)
                pool.memset(head_bc[:], 1.0).then_inc(const_pool, 1)
                pool.memset(stripf[:], 0.0).then_inc(const_pool, 1)
                pool.memset(mhalf[:], -0.5).then_inc(const_pool, 1)
                pool.memset(c09[:], XDECAY).then_inc(const_pool, 1)
                pool.memset(amax_x2[:], 0.0).then_inc(const_pool, 1)
                D = HID // NH
                pool.wait_ge(const_pool, 6)
                pool.affine_select(out=head_sum[:], in_=head_sum[:], compare_op=ALU.is_ge, fill=0.0,
                                   base=0, pattern=[[P, KC], [-D, NH]], channel_multiplier=1).then_inc(const_pool, 1)
                pool.affine_select(out=head_bc[:], in_=head_bc[:], compare_op=ALU.is_ge, fill=0.0,
                                   base=0, pattern=[[P, KC], [1, P]], channel_multiplier=-D).then_inc(const_pool, 1)
                pool.affine_select(out=stripf[:], in_=stripf[:], compare_op=ALU.not_equal, fill=1.0,
                                   base=0, pattern=[[-1, T]], channel_multiplier=1).then_inc(const_pool, 1)
                pool.wait_ge(const_pool, 9)
                pool.affine_select(out=head_sum[:], in_=head_sum[:], compare_op=ALU.is_ge, fill=0.0,
                                   base=D - 1, pattern=[[-P, KC], [D, NH]], channel_multiplier=-1).then_inc(const_pool, 1)
                pool.affine_select(out=head_bc[:], in_=head_bc[:], compare_op=ALU.is_ge, fill=0.0,
                                   base=D - 1, pattern=[[-P, KC], [-1, P]], channel_multiplier=D).then_inc(const_pool, 1)

                def root(n, s):
                    pool.wait_ge(ve_ready[n], s)
                    pool.tensor_tensor(rstd[n][:], var_eps[n][:], mhalf[:], ALU.pow).then_inc(rstd_ready[n], 1)

                def step(s, front, back):
                    if back:
                        pool.wait_ge(ctx_landed, 16 * s)
                        pool.tensor_tensor(csq[:], csq[:], csq[:], ALU.mult).then_inc(sq_ready, 1)
                        pool.wait_ge(sqh_ready, s)
                        pool.tensor_tensor(csq_l[:], csq[:], csq_h[:].bitcast(F32), ALU.subtract).then_inc(sql_ready, 1)
                        root(0, s)
                        root(1, s)

                with pool.Fori(0, (NB - 2) // 2) as i:
                    for u in range(2):
                        step(2 * i + 1 + u, True, True)
                step(NB - 1, True, True)
                step(NB, False, True)

            @block.scalar
            def _(act):
                act.wait_ge(small_in, 16 * 2 * KC)
                act.activation(dtmp2[:], dtmp[:], ACT.Tanh, scale=0.5).then_inc(const_act, 1)
                act.wait_ge(const_dve, 1)

                def split_x(b):
                    wait(act, v_ready, KC * b)
                    for k in range(KC):
                        act.wait_ge(xt_in[k % 2], 16 * (2 * b + k // 2 + 1))
                        act.activation(xh[:, k], xt_raw[:, k % 2], ACT.Copy).then_inc(xh_ready, 1)

                def front_tile(b, c, par):
                    n = KC * b + c
                    act.wait_ge(qk_ready, n + 1)
                    wait(act, qkv_ready, n - 1)
                    act.activation(phi[:, c % 2], qk_ps[c % 2][:], ACT.Relu, scale=-1.0).then_inc(neg_ready, 1)
                    act.wait_ge(neg_ready, n + 1)
                    act.activation(phi[:, c % 2], phi[:, c % 2], ACT.Exp, scale=-1.0).then_inc(e_ready, 1)
                    act.wait_ge(v_ready, n + 1)
                    act.activation(v_sb[:, par, c], v_ps[c % 2][:], ACT.Copy).then_inc(v_copied, 1)

                def normalise(n, s):
                    act.wait_ge(nmr_ready[n], s)
                    for j in range(TT):
                        act.activation(xrow[:, j], xrow[:, j], ACT.Identity, scale=rstd[n][:, j:j + 1],
                                       bias=nmr[n][:, j:j + 1]).then_inc(norm_ready[n], 1)

                def step(s, par, front, back, nxt):
                    if front:
                        front_tile(s, 0, par)
                    if back:
                        for m in range(KC):
                            act.wait_ge(gate_ready, KC * (s - 1) + m + 1)
                            bank = mix_ps[(m + 1) % 2]
                            act.activation(bank[:], bank[:], ACT.Tanh, scale=0.5,
                                           bias=half_bg[:, m:m + 1]).then_inc(tanh_ready, 1)
                        for m in range(KC):
                            act.wait_ge(mixed, KC * (s - 1) + m + 1)
                            act.activation(ah[:, m], att[:, m], ACT.Copy).then_inc(mh_ready, 1)
                    if front:
                        front_tile(s, 1, par)
                    if back:
                        act.wait_ge(sq_ready, s)
                        wait(act, scan_ready, TT * (s - 1) if not isinstance(s, int) or s > 1 else 0)
                        act.activation(csq_h[:], csq[:], ACT.Copy).then_inc(sqh_ready, 1)
                    if front:
                        front_tile(s, 2, par)
                        front_tile(s, 3, par)
                    if nxt:
                        split_x(s + 1)
                    if back:
                        normalise(0, s)
                    if front:
                        for c in range(KC):
                            act.wait_ge(o_ready, KC * s + c + 1)
                            act.activation(ah[:, c], att[:, c], ACT.Copy).then_inc(oh_ready, 1)
                    if back:
                        normalise(1, s)

                split_x(0)
                step(0, 0, True, False, True)
                step(1, 1, True, True, True)
                step(2, 0, True, True, True)
                with act.Fori(1, (NB - 2) // 2) as i:
                    for u in range(2):
                        step(2 * i + 1 + u, (1 + u) % 2, True, True, True)
                step(NB - 1, 1, True, True, False)
                step(NB, 0, False, True, False)

            @block.vector
            def _(dve):
                dve.wait_ge(small_in, 16 * 2 * KC)
                dve.tensor_scalar(half_bg[:], half_bg[:], 0.5, None, ALU.mult).then_inc(const_dve, 1)
                dve.wait_ge(const_act, 1)
                dve.tensor_scalar(decay[:], dtmp2[:], 0.5, 0.5, ALU.mult, ALU.add).then_inc(const_dve, 1)
                dve.wait_ge(const_dve, 2)
                dve.tensor_scalar(decay[:], decay[:], 1e-8, None, ALU.max).then_inc(const_dve, 1)
                dve.wait_ge(const_pool, NPOOL)
                dve.tensor_tensor_scan(stripf[:], c09[:, 0:1].to_broadcast([P, T]), stripf[:], 0.0,
                                       ALU.mult, ALU.add).then_inc(const_dve, 1)
                dve.wait_ge(const_dve, 4)
                dve.tensor_copy(strip_h[:], stripf[:]).then_inc(const_dve, 1)
                dve.wait_ge(const_dve, 5)
                dve.tensor_tensor(strip_l[:], stripf[:], strip_h[:].bitcast(F32), ALU.subtract).then_inc(const_dve, 1)

                def split_x(b, tiles=range(KC)):
                    for k in tiles:
                        dve.wait_ge(xh_ready, KC * b + k + 1)
                        dve.tensor_tensor(xl[:, k], xt_raw[:, k % 2], xh[:, k].bitcast(F32),
                                          ALU.subtract).then_inc(xl_ready, 1)

                def front_scans(b, c, par, between=None):
                    n = KC * b + c
                    sl = c % 2
                    dve.wait_ge(e_ready, n + 1)
                    dve.scalar_tensor_tensor(phi[:, sl], qk_ps[sl][:], 0.0, phi[:, sl], ALU.max, ALU.add).then_inc(phi_ready, 1)
                    dve.wait_ge(phi_ready, n + 1)
                    wait(dve, den_ready, b)
                    dve.tensor_tensor_scan(qks[:, c], decay[:, c:c + 1].to_broadcast([P, T]), phi[:, sl, 1], 0.0,
                                           ALU.mult, ALU.add).then_inc(ks_scanned, 1)
                    dve.wait_ge(v_copied, n + 1)
                    dve.tensor_tensor(kv[:, sl], phi[:, sl, 1], v_sb[:, par, c], ALU.mult).then_inc(kv_ready, 1)
                    if between:
                        between()
                    dve.wait_ge(ks_scanned, n + 1)
                    dve.tensor_tensor(qks[:, c], phi[:, sl, 0], qks[:, c], ALU.mult).then_inc(qks_ready, 1)
                    dve.wait_ge(kv_ready, n + 1)
                    dve.tensor_tensor_scan(kv[:, sl], decay[:, c:c + 1].to_broadcast([P, T]), kv[:, sl], 0.0,
                                           ALU.mult, ALU.add).then_inc(kv_scanned, 1)

                def front_product(b, c):
                    dve.wait_ge(kv_scanned, KC * b + c + 1)
                    dve.tensor_tensor(att[:, c], phi[:, c % 2, 0], kv[:, c % 2], ALU.mult).then_inc(qkv_ready, 1)

                def norm_scalars(n, s):
                    dve.wait_ge(stats_ready[n], TT * s)
                    row_moments(dve, stats[n], msum[n][:], mdiff[n][:], msq[n][:], var_eps[n][:],
                                moments_ready[n], square_ready[n], ve_ready[n], s)

                def norm_bias(n, s):
                    dve.wait_ge(rstd_ready[n], s)
                    dve.scalar_tensor_tensor(nmr[n][:], msum[n][:], -0.5, rstd[n][:],
                                             ALU.mult, ALU.mult).then_inc(nmr_ready[n], 1)

                def second_residual(s, tiles):
                    for j in tiles:
                        n = TT * (s - 1) + j + 1
                        dve.wait_ge(norm_ready[0], n)
                        dve.wait_ge(scan_ready, n)
                        dve.scalar_tensor_tensor(xrow[:, j], mix_ps[j % 2][:], 1.0, xrow[:, j],
                                                 ALU.add, ALU.mult).then_inc(y_ready[1], 1)
                        dve.wait_ge(y_ready[1], n)
                        dve.bn_stats(stats[1][:, j], xrow[:, j]).then_inc(stats_ready[1], 1)

                def quotient(b, tiles):
                    for c in tiles:
                        n = KC * b + c + 1
                        dve.wait_ge(bc_ready, n)
                        dve.wait_ge(qkv_ready, n)
                        dve.tensor_tensor(att[:, c], att[:, c], bc_banks[c], ALU.mult).then_inc(o_ready, 1)

                def reciprocals(b):
                    dve.wait_ge(den_ready, b + 1)
                    dve.tensor_scalar(den_rec[:], den_bank, 1e-6, None, ALU.max).then_inc(den_clipped, 1)
                    dve.wait_ge(den_clipped, b + 1)
                    dve.reciprocal(den_rec[:], den_rec[:]).then_inc(rec_ready, 1)

                def split_quotient(b, par, tiles):
                    for c in tiles:
                        n = KC * b + c + 1
                        dve.wait_ge(oh_ready, n)
                        dve.tensor_tensor(al[:, c], att[:, c], ah[:, c].bitcast(F32), ALU.subtract).then_inc(ol_ready, 1)
                        dve.wait_ge(ol_ready, n)
                        dve.tensor_tensor(att[:, c], att[:, c], v_sb[:, par, c], ALU.subtract).then_inc(diff_ready, 1)

                def scale_difference(s, m):
                    n = KC * (s - 1) + m + 1
                    dve.wait_ge(tanh_ready, n)
                    dve.wait_ge(diff_ready, n)
                    dve.scalar_tensor_tensor(att[:, m], mix_ps[(m + 1) % 2][:], 1.0, att[:, m],
                                             ALU.add, ALU.mult).then_inc(gated, 1)

                def add_v(s, m, par):
                    dve.wait_ge(gated, KC * (s - 1) + m + 1)
                    dve.scalar_tensor_tensor(att[:, m], att[:, m], 0.5, v_sb[:, 1 - par, m],
                                             ALU.mult, ALU.add).then_inc(mixed, 1)

                def largest(s):
                    dve.wait_ge(norm_ready[1], TT * s)
                    dve.tensor_reduce(amax_step[:], xrow[:].rearrange("p j c -> p (j c)"), AX.X, ALU.max,
                                      apply_absolute_value=True).then_inc(amax_step_ready, 1)
                    dve.wait_ge(amax_step_ready, s)
                    dve.tensor_tensor(amax_x2[:], amax_x2[:], amax_step[:], ALU.max).then_inc(amax_taken, 1)
                    dve.wait_ge(amax_taken, s)

                def step(s, par, front, back, nxt, due=True):
                    if front and back:
                        front_scans(s, 0, par, lambda: scale_difference(s, 0))
                    elif front:
                        front_scans(s, 0, par)
                    else:
                        scale_difference(s, 0)
                    if back:
                        add_v(s, 0, par)
                        for m in range(1, KC):
                            scale_difference(s, m)
                            add_v(s, m, par)
                        for m in range(KC):
                            dve.wait_ge(mh_ready, KC * (s - 1) + m + 1)
                            dve.tensor_tensor(al[:, m], att[:, m], ah[:, m].bitcast(F32), ALU.subtract).then_inc(ml_ready, 1)
                        dve.wait_ge(ml_ready, KC * s)
                        if due:
                            largest(s - 1)
                    if front:
                        front_product(s, 0)
                        for c in range(1, KC):
                            front_scans(s, c, par)
                            front_product(s, c)
                    if back:
                        dve.wait_ge(xrow_in, 16 * s)
                        for j in range(TT):
                            n = TT * (s - 1) + j + 1
                            dve.wait_ge(proj_ready, n)
                            dve.tensor_tensor(xrow[:, j], mix_ps[(j + 1) % 2][:], xrow[:, j], ALU.add).then_inc(y_ready[0], 1)
                            dve.wait_ge(y_ready[0], n)
                            dve.bn_stats(stats[0][:, j], xrow[:, j]).then_inc(stats_ready[0], 1)
                            if j == 1 and nxt:
                                split_x(s + 1, (0, 1))
                            if j == 1 and front:
                                reciprocals(s)
                        norm_scalars(0, s)
                    else:
                        split_x(s + 1, (0, 1))
                        reciprocals(s)
                    if front:
                        quotient(s, (0, 1))
                    if back:
                        norm_bias(0, s)
                    if front:
                        quotient(s, (2, 3))
                    if back:
                        second_residual(s, (0,))
                    if nxt:
                        split_x(s + 1, (2, 3))
                    if back:
                        second_residual(s, (1,))
                    if front:
                        split_quotient(s, par, (0, 1))
                    if back:
                        second_residual(s, (2,))
                    if front:
                        split_quotient(s, par, (2,))
                    if back:
                        second_residual(s, (3,))
                        norm_scalars(1, s)
                    if front:
                        split_quotient(s, par, (3,))
                    if back:
                        norm_bias(1, s)
                split_x(0)
                step(0, 0, True, False, True)
                step(1, 1, True, True, True, due=False)
                with dve.Fori(1, (NB - 2) // 2) as i:
                    for u in range(2):
                        step(2 * i + u, u, True, True, True)
                step(NB - 2, 0, True, True, True)
                step(NB - 1, 1, True, True, False)
                step(NB, 0, False, True, False)
                largest(NB)

            @block.tensor
            def _(pe):
                pe.wait_ge(const_pool, NPOOL)
                pe.wait_ge(const_dve, 6)

                def product(out, stat, mov):
                    n = len(stat)
                    for k in range(n):
                        (sh, sl_), (mh, ml) = stat[k], mov[k]
                        pe.matmul(out, sh, mh, start=(k == 0), stop=False)
                        pe.matmul(out, sh, ml, start=False, stop=False)
                        mm = pe.matmul(out, sl_, mh, start=False, stop=(k == n - 1))
                    return mm

                def w_tile(g, m):
                    cols = slice(m * P, (m + 1) * P)
                    return [(wah[:, k, g, cols], wal[:, k, g, cols]) for k in range(KC)]

                x_halves = [(xh[:, k], xl[:, k]) for k in range(KC)]
                a_halves = [(ah[:, k], al[:, k]) for k in range(KC)]

                def qkv(b, c):
                    n = KC * b + c
                    if c == 0:
                        pe.wait_ge(xl_ready, KC * (b + 1))
                    wait(pe, phi_ready, n - 1)
                    product(qk_ps[c % 2][:, 0], w_tile(0, c), x_halves)
                    product(qk_ps[c % 2][:, 1], w_tile(1, c), x_halves).then_inc(qk_ready, 1)
                    wait(pe, v_copied, n - 1)
                    if c == 0:
                        wait(pe, o_ready, KC * b)
                    product(v_ps[c % 2][:], w_tile(2, c), x_halves).then_inc(v_ready, 1)

                def gate(s):
                    pe.wait_ge(ol_ready, KC * s)
                    for m in range(KC):
                        if m >= 2:
                            pe.wait_ge(gated, KC * (s - 1) + m - 1)
                        product(mix_ps[(m + 1) % 2][:], w_tile(3, m), a_halves).then_inc(gate_ready, 1)

                def project(s, tiles):
                    if 0 in tiles:
                        pe.wait_ge(ml_ready, KC * s)
                    for j in tiles:
                        if j < 2:
                            pe.wait_ge(gated, KC * (s - 1) + j + 3)
                        else:
                            pe.wait_ge(y_ready[0], TT * (s - 1) + j - 1)
                        stat = [(ah[:, k, j * P:(j + 1) * P], al[:, k, j * P:(j + 1) * P]) for k in range(KC)]
                        mov = [(wah[:, k, 4], wal[:, k, 4]) for k in range(KC)]
                        product(mix_ps[(j + 1) % 2][:], stat, mov).then_inc(proj_ready, 1)

                def denominators(s):
                    pe.wait_ge(qks_ready, KC * (s + 1))
                    for c in range(KC):
                        mm = pe.matmul(den_bank, head_sum[:, c], qks[:, c], start=(c == 0), stop=(c == KC - 1))
                    mm.then_inc(den_ready, 1)

                def broadcast(s):
                    pe.wait_ge(rec_ready, s + 1)
                    pe.wait_ge(v_copied, KC * (s + 1))
                    for c in range(KC):
                        pe.matmul(bc_banks[c], head_bc[:, c], den_rec[:], start=True, stop=True).then_inc(bc_ready, 1)

                def context_scan(s):
                    pe.wait_ge(sql_ready, s)
                    for j in range(TT):
                        if j < 2:
                            pe.wait_ge(y_ready[0], TT * s - j)
                        else:
                            pe.wait_ge(y_ready[1], TT * (s - 1) + j - 1)
                        stat = [(strip_h[:, (j - i) * P:(j - i + 1) * P], strip_l[:, (j - i) * P:(j - i + 1) * P])
                                for i in range(j + 1)]
                        mov = [(csq_h[:, i], csq_l[:, i]) for i in range(j + 1)]
                        product(mix_ps[j % 2][:], stat, mov).then_inc(scan_ready, 1)

                def step(s, front, back):
                    if front:
                        qkv(s, 0)
                    if back:
                        gate(s)
                    if front:
                        for c in range(1, KC):
                            qkv(s, c)
                    if back:
                        project(s, (0, 1))
                    if front:
                        denominators(s)
                    if back:
                        project(s, (2, 3))
                    if front:
                        broadcast(s)
                    if back:
                        context_scan(s)

                step(0, True, False)
                with pe.Fori(0, (NB - 2) // 2) as i:
                    for u in range(2):
                        step(2 * i + 1 + u, True, True)
                step(NB - 1, True, True)
                step(NB, False, True)


NCH = NB * 3
CH = 4 * T
QUICK = 2


def up_gate_phase(nc, x2_dram, w_ffn_hl, up_dram, gate_dram, amax_x2, acc, rmax, scales):
    NM = 2 * MT
    GM = 4
    NG = NM // GM
    with ExitStack() as ctx:
        used = []
        ctx.callback(lambda: (nc.clear_and_free_semaphores(used), nc.all_engine_barrier()))

        def sb(name, shape, dt=F32):
            return ctx.enter_context(nc.sbuf_tensor(name, shape, dt))

        def sem(name):
            return phase_semaphore(nc, used, name)

        wh = sb("ug_wh", [P, NM, KC, P], F32R)
        wl = sb("ug_wl", [P, NM, KC, P], F32R)
        x2 = sb("ug_x2", [P, TT, HID])
        qh = sb("ug_qh", [P, 2, KC, T], F32R)
        ql = sb("ug_ql", [P, 2, KC, T], F32R)
        group = sb("ug_group", [P, 4, CH])
        silu = sb("ug_silu", [P, 2, CH])
        ident = sb("ug_ident", [P, P])
        step_max = sb("ug_step_max", [P, 3, 3])
        turn_ps = [ctx.enter_context(nc.psum_tensor(f"ug_turn{i}", [P, T], F32)) for i in range(2)]
        out_ps = [ctx.enter_context(nc.psum_tensor(f"ug_out{i}", [P, T], F32)) for i in range(6)]

        w_in = [sem(f"ug_w_in{i}") for i in range(NG)]
        x2_in = sem("ug_x2_in")
        stored = [sem(f"ug_stored{i}") for i in range(4)]
        consts, amax_all, scale_ready, inv_ready = sem("ug_consts"), sem("ug_amax_all"), sem("ug_scale_ready"), sem("ug_inv_ready")
        tq_ready, turned, qh_ready, ql_ready = sem("ug_tq_ready"), sem("ug_turned"), sem("ug_qh_ready"), sem("ug_ql_ready")
        out_ready, evacuated, silu_ready, prod_ready, rmax_ready = (
            sem("ug_out_ready"), sem("ug_evacuated"), sem("ug_silu_ready"), sem("ug_prod_ready"), sem("ug_rmax_ready"))
        step_max_ready, acc_ready = sem("ug_step_max_ready"), sem("ug_acc_ready")
        s_x, inv_x = scales[:, 0:1], scales[:, 1:2]

        def slot(par, g):
            return (NG * par + g) % 4

        with nc.Block() as block:
            @block.sync
            def _(sp):
                sp.dma_start(x2[:], x2_dram[0]).then_inc(x2_in, 16)
                for g in range(NG):
                    group_at = NWG // 3 * (g % 2) + g // 2
                    for half, w in ((0, wh), (1, wl)):
                        sp.dma_start(w[:, g * GM:(g + 1) * GM].rearrange("p m k n -> p m (k n)").bitcast(F32),
                                     w_ffn_hl[half, group_at]).then_inc(w_in[g], 16)

                def step(b, par, nxt):
                    if nxt:
                        sp.wait_ge(turned, KC * (b + 1))
                        sp.dma_start(x2[:], x2_dram[b + 1]).then_inc(x2_in, 16)
                    for g in range(NG):
                        sp.wait_ge(evacuated, GM * (NG * b + g + 1))
                        dst = (gate_dram if g % 2 else up_dram)[3 * b + g // 2]
                        sp.dma_start(dst, group[:, slot(par, g)]).then_inc(stored[slot(par, g)], 16)
                with sp.Fori(0, NB // 2 - 1) as i:
                    for u in range(2):
                        step(2 * i + u, u, True)
                step(NB - 2, 0, True)
                step(NB - 1, 1, False)
                for sl in range(4):
                    sp.wait_ge(stored[sl], 16 * NB * NG // 4)

            @block.gpsimd
            def _(pool):
                pool.memset(ident[:], 0.0).then_inc(consts, 1)
                pool.memset(acc[:], -3e38).then_inc(consts, 1)
                pool.partition_all_reduce(amax_x2[:], amax_x2[:], P, bass.bass_isa.ReduceOp.max).then_inc(amax_all, 1)
                pool.wait_ge(consts, 2)
                pool.affine_select(out=ident[:], in_=ident[:], compare_op=ALU.not_equal, fill=1.0,
                                   base=0, pattern=[[-1, P]], channel_multiplier=1).then_inc(consts, 1)

            @block.scalar
            def _(act):
                act.wait_ge(inv_ready, 1)

                def high(b, par):
                    for c in range(KC):
                        act.wait_ge(turned, KC * b + c + 1)
                        act.activation(qh[:, par, c], low16(turn_ps[c % 2][:], I16), ACT.Copy).then_inc(qh_ready, 1)

                def outputs(b, par, k, g, first):
                    n = NG * par + g
                    wait(act, stored[n % 4], 16 * (3 * k + n // 4))
                    if not (first and n < 4):
                        act.wait_ge(prod_ready, 3 * b + g // 2 - 1)
                    for m in range(GM):
                        act.wait_ge(out_ready, NM * b + g * GM + m + 1)
                        act.activation(group[:, n % 4, m * T:(m + 1) * T], out_ps[(g * GM + m) % 6][:], ACT.Copy,
                                       scale=s_x).then_inc(evacuated, 1)
                    if g % 2:
                        p = 3 * par + g // 2
                        act.wait_ge(evacuated, GM * (NG * b + g + 1))
                        if not (first and p < 2):
                            act.wait_ge(rmax_ready, 3 * b + g // 2 - 1)
                        act.activation(silu[:, p % 2], group[:, n % 4], ACT.Silu).then_inc(silu_ready, 1)

                def step(b, par, k, nxt, first=False):
                    for g in range(NG):
                        outputs(b, par, k, g, first)
                        if g == 2 and nxt:
                            high(b + 1, 1 - par)
                high(0, 0)
                step(0, 0, 0, True, True)
                step(1, 1, 0, True)
                with act.Fori(1, NB // 2 - 1) as i:
                    for u in range(2):
                        step(2 * i + u, u, i, True)
                step(NB - 2, 0, NB // 2 - 1, True)
                step(NB - 1, 1, NB // 2 - 1, False)

            @block.vector
            def _(dve):
                dve.wait_ge(amax_all, 1)
                dve.tensor_scalar(s_x, amax_x2[:], 1.0 / QMAX16, TINY, ALU.mult, ALU.max).then_inc(scale_ready, 1)
                dve.wait_ge(scale_ready, 1)
                dve.reciprocal(inv_x, s_x).then_inc(inv_ready, 1)
                dve.wait_ge(inv_ready, 1)

                def quantize(b):
                    dve.wait_ge(x2_in, 16 * (b + 1))
                    dve.tensor_scalar(x2[:], x2[:], inv_x, MAGIC, ALU.mult, ALU.add).then_inc(tq_ready, 1)

                def low(b, par):
                    for c in range(KC):
                        dve.wait_ge(qh_ready, KC * b + c + 1)
                        dve.tensor_tensor(ql[:, par, c], low16(turn_ps[c % 2][:], I16), qh[:, par, c].bitcast(F32),
                                          ALU.subtract).then_inc(ql_ready, 1)

                def largest(b, par, g):
                    q = g // 2
                    part = group[:, slot(par, g)]
                    dve.wait_ge(evacuated, GM * (NG * b + g + 1))
                    if g % 2 == 0:
                        dve.tensor_reduce(step_max[:, 0, q:q + 1], part, AX.X, ALU.max,
                                          apply_absolute_value=True).then_inc(step_max_ready, 1)
                        return
                    dve.tensor_reduce(step_max[:, 1, q:q + 1], part, AX.X, ALU.max).then_inc(step_max_ready, 1)
                    dve.tensor_reduce(step_max[:, 2, q:q + 1], part, AX.X, ALU.min, negate=True).then_inc(step_max_ready, 1)
                    sil = silu[:, (3 * par + q) % 2]
                    dve.wait_ge(silu_ready, 3 * b + q + 1)
                    dve.tensor_tensor(sil, sil, group[:, slot(par, g - 1)], ALU.mult).then_inc(prod_ready, 1)
                    dve.wait_ge(prod_ready, 3 * b + q + 1)
                    t = 3 * b + q
                    dve.tensor_reduce(rmax[:, bass.ds(t, 1)], sil, AX.X, ALU.max, apply_absolute_value=True).then_inc(rmax_ready, 1)

                def step(b, par, nxt):
                    for g in range(NG):
                        if g == 1 and nxt:
                            quantize(b + 1)
                        if g == 3 and nxt:
                            low(b + 1, 1 - par)
                        largest(b, par, g)
                    dve.wait_ge(step_max_ready, 9 * (b + 1))
                    dve.tensor_tensor(acc[:], acc[:], step_max[:], ALU.max).then_inc(acc_ready, 1)
                    dve.wait_ge(acc_ready, b + 1)

                dve.wait_ge(consts, 3)
                quantize(0)
                low(0, 0)
                with dve.Fori(0, NB // 2 - 1) as i:
                    for u in range(2):
                        step(2 * i + u, u, True)
                step(NB - 2, 0, True)
                step(NB - 1, 1, False)

            @block.tensor
            def _(pe):
                pe.wait_ge(consts, 3)

                def turn(b, tiles):
                    pe.wait_ge(tq_ready, b + 1)
                    for c in tiles:
                        wait(pe, ql_ready, KC * b + c - 1)
                        for j in range(TT):
                            mm = pe.transpose(turn_ps[c % 2][:, j * P:(j + 1) * P], x2[:, j, c * P:(c + 1) * P], ident[:])
                        mm.then_inc(turned, 1)

                def tile(b, par, m, first):
                    if not (first and m < 6):
                        pe.wait_ge(evacuated, NM * b + m - 5)
                    for k in range(KC):
                        o = out_ps[m % 6][:]
                        pe.matmul(o, wh[:, m, k], qh[:, par, k], start=(k == 0), stop=False)
                        pe.matmul(o, wh[:, m, k], ql[:, par, k], start=False, stop=False)
                        mm = pe.matmul(o, wl[:, m, k], qh[:, par, k], start=False, stop=(k == KC - 1))
                    mm.then_inc(out_ready, 1)

                def step(b, par, nxt, first=False):
                    pe.wait_ge(ql_ready, KC * (b + 1))
                    for m in range(NM):
                        if first and m % GM == 0:
                            pe.wait_ge(w_in[m // GM], 32)
                        tile(b, par, m, first)
                        if m == 11 and nxt:
                            turn(b + 1, (0, 1))
                        if m == 13 and nxt:
                            turn(b + 1, (2, 3))
                turn(0, range(KC))
                step(0, 0, True, True)
                step(1, 1, True)
                with pe.Fori(1, NB // 2 - 1) as i:
                    for u in range(2):
                        step(2 * i + u, u, True)
                step(NB - 2, 0, True)
                step(NB - 1, 1, False)


def quantizer(dve, scale, inv, amax, sem, count):
    dve.tensor_scalar(scale, amax, 1.0 / QMAX16, TINY, ALU.mult, ALU.max).then_inc(sem, 1)
    dve.wait_ge(sem, count + 1)
    dve.reciprocal(inv, scale).then_inc(sem, 1)
    dve.wait_ge(sem, count + 2)
    return count + 2


def scales_phase(nc, up_dram, gate_dram, acc, rmax, scales):
    MARGIN = 2e-4 * QMAX16 * QMAX16
    SILU_SURE = 0.28
    with ExitStack() as ctx:
        used = []
        ctx.callback(lambda: (nc.clear_and_free_semaphores(used), nc.all_engine_barrier()))

        def sb(name, shape, dt=F32):
            return ctx.enter_context(nc.sbuf_tensor(name, shape, dt))

        def sem(name):
            return phase_semaphore(nc, used, name)

        R = 3
        gate = sb("sc_gate", [P, R, CH])
        up = sb("sc_up", [P, R, CH])
        gs = sb("sc_gs", [P, R, CH])
        packed = sb("sc_packed", [P, 3 + NCH])
        packed_all = sb("sc_packed_all", [P, 3 + NCH])
        gmag = sb("sc_gmag", [P, 1])
        top = sb("sc_top", [P, 4])
        amax_gs = sb("sc_amax_gs", [P, 1])
        amax_o = sb("sc_amax_o", [P, 1])
        part_max = sb("sc_part_max", [P, 1])
        tmp = sb("sc_tmp", [P, 8])
        magic = sb("sc_magic", [P, 1])
        best = sb("sc_best", [P, 8])
        best_at = sb("sc_best_at", [P, 8], mybir.dt.uint32)
        go_through = sb("sc_go_through", [P, 1], mybir.dt.int32)
        s_u, inv_u, s_g, inv_g, s_gs, inv_gs, gs_factor, s_o, inv_o, o_factor = (scales[:, i:i + 1] for i in range(2, 12))

        consts, packed_ready, all_ready, sc, top_ready, top_sig = (
            sem("sc_consts"), sem("sc_packed_ready"), sem("sc_all_ready"), sem("sc_scalars"), sem("sc_top_ready"), sem("sc_top_sig"))
        decided, gs_known, gs_reduced, gs_max_part, o_max_part, o_reduced = (
            sem("sc_decided"), sem("sc_gs_known"), sem("sc_gs_reduced"), sem("sc_gs_max_part"), sem("sc_o_max_part"), sem("sc_o_reduced"))
        a_in = [sem(f"sc_a_in{i}") for i in range(R)]
        a_round, a_sig, a_sig_round, a_gs, a_max, a_taken = (
            sem("sc_a_round"), sem("sc_a_sig"), sem("sc_a_sig_round"), sem("sc_a_gs"), sem("sc_a_max"), sem("sc_a_taken"))
        g_in = [sem(f"sc_g_in{i}") for i in range(R)]
        up_in = [sem(f"sc_up_in{i}") for i in range(R)]
        p_round, p_sig, p_up, p_sig_round, p_gs, p_gs_round, p_prod, p_max, p_taken = (
            sem("sc_p_round"), sem("sc_p_sig"), sem("sc_p_up"), sem("sc_p_sig_round"), sem("sc_p_gs"), sem("sc_p_gs_round"),
            sem("sc_p_prod"), sem("sc_p_max"), sem("sc_p_taken"))

        def all_needed(eng):
            eng.wait_ge(decided, 1)
            return eng.value_load(go_through[0:1, 0:1], min_val=0, max_val=1)

        with nc.Block() as block:
            @block.sync
            def _(sp):
                every = all_needed(sp)

                def load_pair(slot, t):
                    sp.dma_start(gate[:, slot], gate_dram[t]).then_inc(g_in[slot], 16)
                    sp.dma_start(up[:, slot], up_dram[t]).then_inc(up_in[slot], 16)
                with sp.If(every > 0):
                    for u in range(R):
                        sp.dma_start(gate[:, u], gate_dram[u]).then_inc(a_in[u], 16)
                    with sp.Fori(0, NCH // R - 1) as i:
                        for u in range(R):
                            sp.wait_ge(a_gs, R * i + u + 1)
                            sp.dma_start(gate[:, u], gate_dram[R * i + u + R]).then_inc(a_in[u], 16)
                    sp.wait_ge(a_gs, NCH)
                    for u in range(R):
                        load_pair(u, u)
                    with sp.Fori(0, NCH // R - 1) as i:
                        for u in range(R):
                            sp.wait_ge(p_prod, R * i + u + 1)
                            load_pair(u, R * i + u + R)
                with sp.Else():
                    at = [sp.value_load(best_at[0:1, n:n + 1], min_val=0, max_val=NCH - 1) for n in range(QUICK)]
                    for n in range(QUICK):
                        load_pair(n, at[n])

            @block.gpsimd
            def _(pool):
                pool.memset(magic[:], MAGIC).then_inc(consts, 1)
                pool.memset(amax_o[:], 0.0).then_inc(consts, 1)
                pool.wait_ge(packed_ready, 2)
                pool.partition_all_reduce(packed_all[:], packed[:], P, bass.bass_isa.ReduceOp.max).then_inc(all_ready, 1)
                every = all_needed(pool)
                with pool.If(every > 0):
                    pool.wait_ge(gs_max_part, 1)
                    pool.partition_all_reduce(amax_gs[:], amax_gs[:], P, bass.bass_isa.ReduceOp.max).then_inc(gs_reduced, 1)
                with pool.Else():
                    pool.memset(part_max[:], 0.0).then_inc(gs_reduced, 1)
                pool.wait_ge(o_max_part, 1)
                pool.partition_all_reduce(amax_o[:], amax_o[:], P, bass.bass_isa.ReduceOp.max).then_inc(o_reduced, 1)

            @block.scalar
            def _(act):
                act.wait_ge(top_ready, 1)
                act.activation(top[:, 1:2], low16(top[:, 0:1], I16), ACT.Sigmoid, scale=s_g).then_inc(top_sig, 1)
                act.wait_ge(consts, 2)
                every = all_needed(act)

                def head(t, u, k):
                    act.wait_ge(g_in[u], 16 * k + 16)
                    act.activation(gate[:, u], gate[:, u], ACT.Identity, scale=inv_g, bias=magic[:]).then_inc(p_round, 1)
                    act.wait_ge(p_round, t + 1)
                    wait(act, p_max, t + 1 - R)
                    act.activation(gs[:, u], low16(gate[:, u], I16), ACT.Sigmoid, scale=s_g).then_inc(p_sig, 1)
                    act.wait_ge(up_in[u], 16 * k + 16)
                    act.activation(up[:, u], up[:, u], ACT.Identity, scale=inv_u, bias=magic[:]).then_inc(p_up, 1)

                def tail(t, u):
                    act.wait_ge(p_gs, t + 1)
                    act.activation(gs[:, u], gs[:, u], ACT.Identity, scale=gs_factor, bias=magic[:]).then_inc(p_gs_round, 1)
                with act.If(every > 0):
                    for u in range(R):
                        act.wait_ge(a_in[u], 16)
                        act.activation(gate[:, u], gate[:, u], ACT.Identity, scale=inv_g, bias=magic[:]).then_inc(a_round, 1)
                        act.wait_ge(a_round, u + 1)
                        act.activation(gs[:, u], low16(gate[:, u], I16), ACT.Sigmoid, scale=s_g).then_inc(a_sig, 1)
                    with act.Fori(1, NCH // R) as i:
                        for u in range(R):
                            t = R * i + u
                            act.wait_ge(a_in[u], 16 * i + 16)
                            act.activation(gate[:, u], gate[:, u], ACT.Identity, scale=inv_g, bias=magic[:]).then_inc(a_round, 1)
                            act.wait_ge(a_round, t + 1)
                            act.wait_ge(a_max, t + 1 - R)
                            act.activation(gs[:, u], low16(gate[:, u], I16), ACT.Sigmoid, scale=s_g).then_inc(a_sig, 1)
                    act.wait_ge(gs_known, 1)
                    head(0, 0, 0)
                    for t in range(1, R):
                        head(t, t, 0)
                        tail(t - 1, t - 1)
                    with act.Fori(1, NCH // R) as i:
                        for u in range(R):
                            head(R * i + u, u, i)
                            tail(R * i + u - 1, (u - 1) % R)
                    tail(NCH - 1, R - 1)
                with act.Else():
                    for n in range(QUICK):
                        head(n, n, 0)
                    act.wait_ge(gs_known, 1)
                    for n in range(QUICK):
                        tail(n, n)

            @block.vector
            def _(dve):
                for n in range(3):
                    dve.tensor_reduce(packed[:, n:n + 1], acc[:, n], AX.X, ALU.max).then_inc(sc, 1)
                dve.tensor_copy(packed[:, 3:], rmax[:]).then_inc(packed_ready, 1)
                dve.wait_ge(sc, 3)
                dve.memset(part_max[:], 0.0).then_inc(packed_ready, 1)
                dve.wait_ge(all_ready, 1)
                dve.tensor_tensor(gmag[:], packed_all[:, 1:2], packed_all[:, 2:3], ALU.max).then_inc(sc, 1)
                dve.wait_ge(sc, 4)
                n = quantizer(dve, s_u, inv_u, packed_all[:, 0:1], sc, 4)
                n = quantizer(dve, s_g, inv_g, gmag[:], sc, n)
                dve.tensor_scalar(top[:, 0:1], packed_all[:, 1:2], inv_g, MAGIC, ALU.mult, ALU.add).then_inc(top_ready, 1)
                dve.max(best[:], packed_all[:, 3:]).then_inc(sc, 1)
                dve.tensor_tensor(tmp[:, 0:1], s_u, s_g, ALU.mult).then_inc(sc, 1)
                dve.wait_ge(sc, 10)
                dve.max_index(best_at[:], best[:], packed_all[:, 3:]).then_inc(sc, 1)
                dve.scalar_tensor_tensor(tmp[:, 1:2], tmp[:, 0:1], MARGIN, best[:, QUICK:QUICK + 1],
                                         ALU.mult, ALU.add).then_inc(sc, 1)
                dve.wait_ge(sc, 12)
                dve.tensor_tensor(tmp[:, 2:3], tmp[:, 1:2], best[:, 0:1], ALU.is_ge).then_inc(sc, 1)
                dve.wait_ge(top_sig, 1)
                dve.tensor_scalar(top[:, 2:3], top[:, 1:2], 65535.0 * SIG_STEP, SIG_MAGIC, ALU.min, ALU.add).then_inc(top_ready, 1)
                dve.wait_ge(top_ready, 2)
                dve.tensor_tensor(top[:, 3:4], low16(top[:, 0:1], I16), low16(top[:, 2:3], U16), ALU.mult).then_inc(top_ready, 1)
                dve.tensor_scalar(tmp[:, 3:4], s_g, SIG_STEP, None, ALU.mult).then_inc(sc, 1)
                dve.wait_ge(top_ready, 3)
                dve.wait_ge(sc, 14)
                dve.tensor_tensor(tmp[:, 4:5], top[:, 3:4], tmp[:, 3:4], ALU.mult).then_inc(sc, 1)
                dve.tensor_copy(amax_gs[:], top[:, 3:4]).then_inc(sc, 1)
                dve.wait_ge(sc, 16)
                dve.scalar_tensor_tensor(tmp[:, 5:6], tmp[:, 4:5], SILU_SURE, tmp[:, 2:3], ALU.is_lt, ALU.max).then_inc(sc, 1)
                dve.wait_ge(sc, 17)
                dve.tensor_copy(go_through[:], tmp[:, 5:6]).then_inc(decided, 1)
                dve.wait_ge(consts, 2)
                every = all_needed(dve)

                def round_sigmoid(buf, done):
                    dve.tensor_scalar(buf, buf, 65535.0 * SIG_STEP, SIG_MAGIC, ALU.min, ALU.add).then_inc(done, 1)

                with dve.If(every > 0):
                    dve.memset(amax_gs[:], 0.0).then_inc(a_taken, 1)
                    with dve.Fori(0, NCH // R) as i:
                        for u in range(R):
                            t = R * i + u
                            dve.wait_ge(a_sig, t + 1)
                            round_sigmoid(gs[:, u], a_sig_round)
                            dve.wait_ge(a_sig_round, t + 1)
                            dve.tensor_tensor(gs[:, u], low16(gate[:, u], I16), low16(gs[:, u], U16), ALU.mult).then_inc(a_gs, 1)
                            dve.wait_ge(a_gs, t + 1)
                            dve.wait_ge(a_taken, t + 1)
                            dve.tensor_reduce(part_max[:], gs[:, u], AX.X, ALU.max, apply_absolute_value=True).then_inc(a_max, 1)
                            dve.wait_ge(a_max, t + 1)
                            dve.tensor_tensor(amax_gs[:], amax_gs[:], part_max[:], ALU.max).then_inc(a_taken, 1)
                    dve.wait_ge(a_taken, NCH + 1)
                    dve.tensor_copy(tmp[:, 6:7], amax_gs[:]).then_inc(gs_max_part, 1)
                with dve.Else():
                    dve.tensor_copy(tmp[:, 6:7], amax_gs[:]).then_inc(gs_max_part, 1)
                dve.wait_ge(gs_reduced, 1)
                dve.tensor_tensor(tmp[:, 4:5], tmp[:, 3:4], amax_gs[:], ALU.mult).then_inc(sc, 1)
                dve.wait_ge(sc, 18)
                n = quantizer(dve, s_gs, inv_gs, tmp[:, 4:5], sc, 18)
                dve.tensor_tensor(gs_factor, tmp[:, 3:4], inv_gs, ALU.mult).then_inc(gs_known, 1)

                def head(t, u):
                    dve.wait_ge(p_sig, t + 1)
                    round_sigmoid(gs[:, u], p_sig_round)
                    dve.wait_ge(p_sig_round, t + 1)
                    dve.tensor_tensor(gs[:, u], low16(gate[:, u], I16), low16(gs[:, u], U16), ALU.mult).then_inc(p_gs, 1)

                def tail(t, u):
                    dve.wait_ge(p_gs_round, t + 1)
                    dve.wait_ge(p_up, t + 1)
                    dve.tensor_tensor(gs[:, u], low16(gs[:, u], I16), low16(up[:, u], I16), ALU.mult).then_inc(p_prod, 1)
                    dve.wait_ge(p_prod, t + 1)
                    wait(dve, p_taken, t)
                    dve.tensor_reduce(part_max[:], gs[:, u], AX.X, ALU.max, apply_absolute_value=True).then_inc(p_max, 1)
                    dve.wait_ge(p_max, t + 1)
                    dve.tensor_tensor(amax_o[:], amax_o[:], part_max[:], ALU.max).then_inc(p_taken, 1)
                with dve.If(every > 0):
                    for t in range(R):
                        head(t, t)
                        tail(t, t)
                    with dve.Fori(1, NCH // R) as i:
                        for u in range(R):
                            head(R * i + u, u)
                            tail(R * i + u, u)
                    dve.wait_ge(p_taken, NCH)
                    dve.memset(part_max[:], 0.0).then_inc(o_max_part, 1)
                with dve.Else():
                    for n in range(QUICK):
                        head(n, n)
                    for n in range(QUICK):
                        tail(n, n)
                    dve.wait_ge(p_taken, QUICK)
                    dve.memset(part_max[:], 0.0).then_inc(o_max_part, 1)
                dve.wait_ge(o_reduced, 1)
                dve.tensor_tensor(tmp[:, 0:1], s_gs, s_u, ALU.mult).then_inc(sc, 1)
                dve.wait_ge(sc, 21)
                dve.tensor_tensor(tmp[:, 1:2], tmp[:, 0:1], amax_o[:], ALU.mult).then_inc(sc, 1)
                dve.wait_ge(sc, 22)
                quantizer(dve, s_o, inv_o, tmp[:, 1:2], sc, 22)
                dve.tensor_tensor(o_factor, tmp[:, 0:1], inv_o, ALU.mult).then_inc(sc, 1)
                dve.wait_ge(sc, 25)


def down_phase(nc, up_dram, gate_dram, x2_dram, w_ffn_hl, out, scales):
    with ExitStack() as ctx:
        used = []
        ctx.callback(lambda: (nc.clear_and_free_semaphores(used), nc.all_engine_barrier()))

        def sb(name, shape, dt=F32):
            return ctx.enter_context(nc.sbuf_tensor(name, shape, dt))

        def sem(name):
            return phase_semaphore(nc, used, name)

        NC3 = 3
        wh = sb("dn_wh", [P, MT, KC, P], F32R)
        wl = sb("dn_wl", [P, MT, KC, P], F32R)
        gate = sb("dn_gate", [P, NC3, CH])
        up = sb("dn_up", [P, NC3, CH])
        gs = sb("dn_gs", [P, NC3, CH])
        oh = sb("dn_oh", [P, NC3, KC, T], F32R)
        ol = sb("dn_ol", [P, NC3, KC, T], F32R)
        x2 = sb("dn_x2", [P, 2, TT, HID])
        magic = sb("dn_magic", [P, 1])
        mhalf = sb("dn_mhalf", [P, TT])
        tick = sb("dn_tick", [P, 1])
        stats = sb("dn_stats", [P, TT, 6])
        msum, mdiff, msq = (sb(f"dn_{n}", [P, TT]) for n in ("msum", "mdiff", "msq"))
        var_eps = sb("dn_var_eps", [P, TT])
        rstd = sb("dn_rstd", [P, TT])
        nmr = sb("dn_nmr", [P, TT])
        out_ps = [ctx.enter_context(nc.psum_tensor(f"dn_ps{i}", [P, HID], F32)) for i in range(8)]
        w_in = [sem(f"dn_w_in{i}") for i in range(NC3)]
        g_in = [sem(f"dn_g_in{i}") for i in range(NC3)]
        up_in = [sem(f"dn_up_in{i}") for i in range(NC3)]
        x2_in = [sem(f"dn_x2_in{i}") for i in range(2)]
        stored = [sem(f"dn_stored{i}") for i in range(2)]
        consts, tick_done = sem("dn_consts"), sem("dn_tick_done")
        g_round, sig_ready, sig_round, gs_ready, gs_round, up_round, prod_ready, prod_round, oh_ready, ol_ready = (
            sem("dn_g_round"), sem("dn_sig_ready"), sem("dn_sig_round"), sem("dn_gs_ready"), sem("dn_gs_round"),
            sem("dn_up_round"), sem("dn_prod_ready"), sem("dn_prod_round"), sem("dn_oh_ready"), sem("dn_ol_ready"))
        part_used, y_ready, sum_ready, stats_ready, moments_ready, square_ready, ve_ready, rstd_ready, nmr_ready, norm_ready = (
            sem("dn_part_used"), sem("dn_y_ready"), sem("dn_sum_ready"), sem("dn_stats_ready"), sem("dn_moments_ready"),
            sem("dn_square_ready"), sem("dn_ve_ready"), sem("dn_rstd_ready"), sem("dn_nmr_ready"), sem("dn_norm_ready"))
        s_u, inv_u, s_g, inv_g, s_gs, inv_gs, gs_factor, s_o, inv_o, o_factor = (scales[:, i:i + 1] for i in range(2, 12))

        def earlier(b, n, back):
            return (b, n - back) if n >= back else (b - 1, n - back + NC3)

        def chunk_steps(b, n, begin, carry_on, finish, last):
            if b < NB if isinstance(b, int) else True:
                begin(b, n)
            for back, f in ((1, carry_on), (2, finish)):
                bb, nn = earlier(b, n, back)
                if not isinstance(bb, int) or 0 <= bb < NB:
                    f(bb, nn)
            if n in last and (not isinstance(b, int) or b >= 2):
                last[n](b - 2)

        with nc.Block() as block:
            @block.sync
            def _(sp):
                def load_gate(b, n):
                    sp.dma_start(gate[:, n], gate_dram[NC3 * b + n]).then_inc(g_in[n], 16)

                def load_up(b, n):
                    sp.dma_start(up[:, n], up_dram[NC3 * b + n]).then_inc(up_in[n], 16)
                for n in range(NC3):
                    load_gate(0, n)
                    load_up(0, n)
                    for half, w in ((0, wh), (1, wl)):
                        sp.dma_start(w[:, n * KC:(n + 1) * KC].rearrange("p m k n -> p m (k n)").bitcast(F32),
                                     w_ffn_hl[half, NWG // 3 * 2 + n]).then_inc(w_in[n], 16)
                for u in range(2):
                    sp.dma_start(x2[:, u], x2_dram[u]).then_inc(x2_in[u], 16)

                def step(b, u, k, nxt):
                    for n in range(NC3):
                        if nxt:
                            sp.wait_ge(gs_ready, NC3 * b + n + 1)
                            load_gate(b + 1, n)
                        bb, nn = earlier(b, n, 2)
                        if not isinstance(bb, int) or 0 <= bb < NB - 1:
                            sp.wait_ge(ol_ready, NC3 * bb + nn + 1)
                            load_up(bb + 1, nn)
                    if k is not None:
                        sp.wait_ge(stored[u], 16 * k)
                        sp.dma_start(x2[:, u], x2_dram[b]).then_inc(x2_in[u], 16)
                step(0, 0, None, True)
                step(1, 1, None, True)
                with sp.Fori(1, NB // 2 - 1) as i:
                    for u in range(2):
                        step(2 * i + u, u, i, True)
                step(NB - 2, 0, NB // 2 - 1, True)
                step(NB - 1, 1, NB // 2 - 1, False)
                for u in range(2):
                    sp.wait_ge(stored[u], 16 * (NB // 2))

            @block.gpsimd
            def _(pool):
                pool.memset(magic[:], MAGIC).then_inc(consts, 1)
                pool.memset(mhalf[:], -0.5).then_inc(consts, 1)
                pool.wait_ge(consts, 2)

                def round_gate(b, n, with_up):
                    wait(pool, tick_done, NC3 * b + n)
                    pool.wait_ge(g_in[n], 16 * (b + 1))
                    if with_up:
                        bb, nn = earlier(b, n, 1)
                        pool.wait_ge(up_in[nn], 16 * (bb + 1))
                    pool.tensor_tensor(tick[:], mhalf[:, 0:1], mhalf[:, 0:1], ALU.mult).then_inc(tick_done, 1)
                    pool.tensor_scalar(gate[:, n], gate[:, n], inv_g, MAGIC, ALU.mult, ALU.add).then_inc(g_round, 1)
                    if with_up:
                        round_up(nn)

                def round_up(n):
                    pool.tensor_scalar(up[:, n], up[:, n], inv_u, MAGIC, ALU.mult, ALU.add).then_inc(up_round, 1)

                def root(b):
                    pool.wait_ge(ve_ready, b + 1)
                    pool.tensor_tensor(rstd[:], var_eps[:], mhalf[:], ALU.pow).then_inc(rstd_ready, 1)
                for b in range(2):
                    for n in range(NC3):
                        round_gate(b, n, b + n > 0)
                with pool.Fori(2, NB) as b:
                    for n in range(NC3):
                        round_gate(b, n, True)
                    root(b - 2)
                pool.wait_ge(up_in[NC3 - 1], 16 * NB)
                round_up(NC3 - 1)
                root(NB - 2)
                root(NB - 1)

            @block.scalar
            def _(act):
                act.wait_ge(consts, 2)

                def begin(b, n):
                    t = NC3 * b + n
                    act.wait_ge(g_round, t + 1)
                    wait(act, prod_ready, t - NC3 + 1)
                    act.activation(gs[:, n], low16(gate[:, n], I16), ACT.Sigmoid, scale=s_g).then_inc(sig_ready, 1)

                def carry_on(b, n):
                    act.wait_ge(gs_ready, NC3 * b + n + 1)
                    act.activation(gs[:, n], gs[:, n], ACT.Identity, scale=gs_factor, bias=magic[:]).then_inc(gs_round, 1)

                def finish(b, n):
                    t = NC3 * b + n
                    act.wait_ge(prod_ready, t + 1)
                    act.activation(up[:, n], up[:, n], ACT.Identity, scale=o_factor, bias=magic[:]).then_inc(prod_round, 1)
                    act.wait_ge(prod_round, t + 1)
                    if not isinstance(b, int) or b > 0:
                        if n < 2:
                            act.wait_ge(part_used, 2 * (b - 1) + n + 1)
                        else:
                            act.wait_ge(y_ready, TT * b)
                    act.activation(oh[:, n].rearrange("p m t -> p (m t)"), low16(up[:, n], I16), ACT.Copy).then_inc(oh_ready, 1)

                def normalise(b, par):
                    act.wait_ge(nmr_ready, b + 1)
                    for j in range(TT):
                        act.activation(x2[:, par, j], x2[:, par, j], ACT.Identity, scale=rstd[:, j:j + 1],
                                       bias=nmr[:, j:j + 1]).then_inc(norm_ready, 1)
                    act.wait_ge(norm_ready, TT * (b + 1))
                    act.dma_start(out[b], x2[:, par]).then_inc(stored[par], 16)

                def step(b, par):
                    for n in range(NC3):
                        chunk_steps(b, n, begin, carry_on, finish, {2: lambda bb: normalise(bb, par)})
                step(0, 0)
                step(1, 1)
                with act.Fori(1, NB // 2) as i:
                    for u in range(2):
                        step(2 * i + u, u)
                step(NB, 0)
                normalise(NB - 1, 1)

            @block.vector
            def _(dve):
                def begin(b, n):
                    t = NC3 * b + n
                    dve.wait_ge(sig_ready, t + 1)
                    dve.tensor_scalar(gs[:, n], gs[:, n], 65535.0 * SIG_STEP, SIG_MAGIC, ALU.min, ALU.add).then_inc(sig_round, 1)
                    dve.wait_ge(sig_round, t + 1)
                    dve.tensor_tensor(gs[:, n], low16(gate[:, n], I16), low16(gs[:, n], U16), ALU.mult).then_inc(gs_ready, 1)

                def carry_on(b, n):
                    t = NC3 * b + n
                    dve.wait_ge(gs_round, t + 1)
                    dve.wait_ge(up_round, t + 1)
                    dve.tensor_tensor(up[:, n], low16(gs[:, n], I16), low16(up[:, n], I16), ALU.mult).then_inc(prod_ready, 1)

                def finish(b, n):
                    dve.wait_ge(oh_ready, NC3 * b + n + 1)
                    dve.tensor_tensor(ol[:, n].rearrange("p m t -> p (m t)"), low16(up[:, n], I16),
                                      oh[:, n].rearrange("p m t -> p (m t)").bitcast(F32), ALU.subtract).then_inc(ol_ready, 1)

                def sums(b, par, k):
                    dve.wait_ge(x2_in[par], 16 * (k + 1))
                    for j in range(TT):
                        n = TT * b + j + 1
                        dve.wait_ge(y_ready, n)
                        dve.scalar_tensor_tensor(x2[:, par, j], out_ps[TT * par + j][:], s_o, x2[:, par, j],
                                                 ALU.mult, ALU.add).then_inc(sum_ready, 1)
                        dve.wait_ge(sum_ready, n)
                        dve.bn_stats(stats[:, j], x2[:, par, j]).then_inc(stats_ready, 1)
                    wait(dve, norm_ready, TT * b)
                    dve.wait_ge(stats_ready, TT * (b + 1))
                    row_moments(dve, stats, msum[:], mdiff[:], msq[:], var_eps[:], moments_ready, square_ready, ve_ready, b + 1)

                def norm_bias(b):
                    dve.wait_ge(rstd_ready, b + 1)
                    dve.scalar_tensor_tensor(nmr[:], msum[:], -0.5, rstd[:], ALU.mult, ALU.mult).then_inc(nmr_ready, 1)

                def step(b, par, k):
                    for n in range(NC3):
                        chunk_steps(b, n, begin, carry_on, finish, {0: lambda bb: sums(bb, par, k), 1: norm_bias})
                step(0, 0, 0)
                step(1, 1, 0)
                step(2, 0, 0)
                step(3, 1, 0)
                with dve.Fori(2, NB // 2) as i:
                    for u in range(2):
                        step(2 * i + u, u, i - 1)
                step(NB, 0, NB // 2 - 1)
                sums(NB - 1, 1, NB // 2 - 1)
                norm_bias(NB - 1)

            @block.tensor
            def _(pe):
                def step(b, u, first=False):
                    for n in range(NC3):
                        if first:
                            pe.wait_ge(w_in[n], 32)
                        pe.wait_ge(ol_ready, NC3 * b + n + 1)
                        if n == 0 and (not isinstance(b, int) or b > 1):
                            pe.wait_ge(sum_ready, TT * (b - 1))
                        for j in range(TT):
                            rows = slice(j * P, (j + 1) * P)
                            o = out_ps[TT * u + j][:].rearrange("p (m n) -> p m n", n=P)
                            for k in range(KC):
                                mh, ml = (w[:, n * KC:(n + 1) * KC, k] for w in (wh, wl))
                                pe.matmul(o, oh[:, n, k, rows], mh, start=(n == 0 and k == 0), stop=False)
                                pe.matmul(o, oh[:, n, k, rows], ml, start=False, stop=False)
                                mm = pe.matmul(o, ol[:, n, k, rows], mh, start=False, stop=(n == NC3 - 1 and k == KC - 1))
                            if n == NC3 - 1:
                                mm.then_inc(y_ready, 1)
                        if n < NC3 - 1:
                            mm.then_inc(part_used, 1)
                step(0, 0, True)
                step(1, 1)
                with pe.Fori(1, NB // 2) as i:
                    for u in range(2):
                        step(2 * i + u, u)


def decoder(nc, xT, x, ctx_in, w_attn, w_ffn, b_gate, decay, out):
    def scratch(name, shape):
        return nc.dram_tensor(name, shape, F32, kind="Internal").ap()

    w_ffn_hl = scratch("w_ffn_hl", (2, NWG, P, WG, T))
    x2_dram = scratch("x2_rows", (NB, P, TT, HID))
    up_dram = scratch("up_products", (NCH, P, CH))
    gate_dram = scratch("gate_products", (NCH, P, CH))
    with ExitStack() as ctx:
        def sb(name, shape, dt=F32):
            return ctx.enter_context(nc.sbuf_tensor(name, shape, dt))
        amax_x2 = sb("amax_x2", [P, 1])
        acc = sb("acc", [P, 3, 3])
        rmax = sb("rmax", [P, NCH])
        scales = sb("scales", [P, 12])
        with ExitStack() as attn:
            wah = attn.enter_context(nc.sbuf_tensor("wah", [P, KC, 5, T], F32R))
            wal = attn.enter_context(nc.sbuf_tensor("wal", [P, KC, 5, T], F32R))
            prepare_weights(nc, w_attn, w_ffn, w_ffn_hl, wah, wal)
            attention_phase(nc, xT, x, ctx_in, b_gate, decay, wah, wal, x2_dram, amax_x2)
        up_gate_phase(nc, x2_dram, w_ffn_hl, up_dram, gate_dram, amax_x2, acc, rmax, scales)
        scales_phase(nc, up_dram, gate_dram, acc, rmax, scales)
        down_phase(nc, up_dram, gate_dram, x2_dram, w_ffn_hl, out, scales)


def kernel(**inputs):
    import concourse.bacc as bacc
    from concourse.bass_utils import run_bass_kernel_spmd

    a = {k: np.asarray(v) for k, v in inputs.items()}
    arrays = {
        "xT": np.ascontiguousarray(a["x"].transpose(0, 2, 1)).reshape(NB, KC, P, T),
        "x_rows": np.ascontiguousarray(a["x"].reshape(NB, TT, P, HID).transpose(0, 2, 1, 3)),
        "ctx_rows": np.ascontiguousarray(a["ctx_1024"].reshape(NB, TT, P, HID).transpose(0, 2, 1, 3)),
        "w_attn": np.ascontiguousarray(np.concatenate(
            [a["L0_attn_Wqkv"], a["L0_attn_Wgate"], a["L0_attn_Wout"]]).reshape(5, HID, KC, P).transpose(3, 2, 0, 1)),
        "w_ffn": np.ascontiguousarray(np.concatenate(
            [a["L0_ffn_w_up"].reshape(MT, P, HID), a["L0_ffn_w_gate"].reshape(MT, P, HID),
             a["L0_ffn_w_down"].reshape(KC, P, 3, HID).transpose(2, 0, 1, 3).reshape(MT, P, HID)])
            .reshape(NWG, WG, P, HID).transpose(0, 2, 1, 3)),
        "b_gate": np.ascontiguousarray(a["L0_attn_bgate"].reshape(KC, P, 1)),
        "decay": np.ascontiguousarray(np.repeat(a["L0_attn_decay_param"], HID // NH).reshape(KC, P, 1)),
    }
    nc = bacc.Bacc("TRN2", target_bir_lowering=False, num_devices=1)
    args = [nc.dram_tensor(f"in_{k}", v.shape, mybir.dt.from_np(v.dtype), kind="ExternalInput").ap()
            for k, v in arrays.items()]
    out = nc.dram_tensor("out_rows", (NB, P, TT, HID), F32, kind="ExternalOutput").ap()
    decoder(nc, *args, out)
    r = run_bass_kernel_spmd(nc, [{f"in_{k}": v for k, v in arrays.items()}], core_ids=[0])
    rows = r.results[0]["out_rows"]
    return np.ascontiguousarray(rows.transpose(0, 2, 1, 3)).reshape(NB, T, HID)
```

```python
import math

import numpy as np
import concourse.bass as bass
from concourse import mybir
from contextlib import ExitStack

F32 = mybir.dt.float32
F32R = mybir.dt.float32r
I16 = mybir.dt.int16
U16 = mybir.dt.uint16
ALU = mybir.AluOpType
ACT = mybir.ActivationFunctionType
AX = mybir.AxisListType

P = 128
NB, T, HID = 16, 512, 512
NH = 16
INNER = 1536
KC = HID // P
TT = T // P
MT = INNER // P
QB = 32
NQB = T // QB
WG = 4
NWG = 3 * MT // WG
XDECAY = 0.9
LN_EPS = 1e-5
QMAX16 = 32767.0
QMAX4 = 7.0
TINY = 1e-12
MAGIC = 1.5 * 2.0 ** 23
SIG_STEP = 2.0 ** -16
SIG_MAGIC = MAGIC * SIG_STEP


def low16(ap, dt):
    if len(ap.shape) == 2:
        return ap.bitcast(dt).rearrange("p (n h) -> p n h", h=2)[:, :, 0]
    return ap.bitcast(dt).rearrange("p a (n h) -> p a n h", h=2)[:, :, :, 0]


def wait(eng, sem, value):
    if isinstance(value, int) and value <= 0:
        return
    eng.wait_ge(sem, value)


def row_moments(dve, stats, msum, mdiff, m2, ve, parts_ready, square_ready, ve_ready, s):
    dve.tensor_tensor(msum, stats[:, :, 1], stats[:, :, 4], ALU.add).then_inc(parts_ready, 1)
    dve.tensor_tensor(mdiff, stats[:, :, 1], stats[:, :, 4], ALU.subtract).then_inc(parts_ready, 1)
    dve.scalar_tensor_tensor(m2, stats[:, :, 2], HID * LN_EPS, stats[:, :, 5], ALU.add, ALU.add).then_inc(parts_ready, 1)
    dve.wait_ge(parts_ready, 3 * s)
    dve.scalar_tensor_tensor(mdiff, mdiff, 0.25, mdiff, ALU.mult, ALU.mult).then_inc(square_ready, 1)
    dve.wait_ge(square_ready, s)
    dve.scalar_tensor_tensor(ve, m2, 1.0 / HID, mdiff, ALU.mult, ALU.add).then_inc(ve_ready, 1)


def phase_semaphore(nc, used, name):
    handle = nc.alloc_semaphore(name)
    used.append(handle)
    return handle


def prepare_weights(nc, w_attn, w_ffn, w_ffn_t, wah, wal):
    NA = 5
    AR = 3
    with ExitStack() as ctx:
        used = []
        ctx.callback(lambda: (nc.clear_and_free_semaphores(used), nc.all_engine_barrier()))

        def sb(name, shape, dt=F32):
            return ctx.enter_context(nc.sbuf_tensor(name, shape, dt))

        def sem(name):
            return phase_semaphore(nc, used, name)

        stage = sb("wa_stage", [P, AR, KC, T])
        w_raw = sb("w_raw", [P, 2, WG, T])
        w_int = sb("w_int", [P, 2, WG, T])
        w_deq = sb("w_deq", [P, 2, WG, T])
        w_out = sb("w_out", [P, 2, WG, T])
        blk_max = sb("blk_max", [P, 2, WG * NQB])
        blk_scale = sb("blk_scale", [P, 2, WG * NQB])
        blk_inv = sb("blk_inv", [P, 2, WG * NQB])
        ident = sb("w_ident", [P, P])
        turned = [ctx.enter_context(nc.psum_tensor(f"w_turned{i}", [P, WG, T], F32)) for i in range(2)]
        wa_in = [sem(f"wa_in{i}") for i in range(AR)]
        raw_in = [sem(f"w_raw_in{i}") for i in range(2)]
        stored = [sem(f"w_stored{i}") for i in range(2)]
        ident_ready = sem("w_ident_ready")
        wah_ready, wal_ready = sem("wah_ready"), sem("wal_ready")
        max_ready, scale_ready, inv_ready = sem("max_ready"), sem("scale_ready"), sem("inv_ready")
        ratio_ready, int_ready = sem("ratio_ready"), sem("int_ready")
        deq_ready = sem("deq_ready")
        turned_ready, copied = sem("turned_ready"), sem("w_copied")

        def blocks(ap):
            return ap.rearrange("p m (b q) -> p (m b) q", q=QB)

        def per_block(ap):
            return ap.unsqueeze(2).to_broadcast([P, WG * NQB, QB])

        with nc.Block() as block:
            @block.sync
            def _(sp):
                def load_ffn(g, u):
                    sp.dma_start(w_raw[:, u], w_ffn[g]).then_inc(raw_in[u], 16)

                def load_attn(a):
                    if a >= AR:
                        sp.wait_ge(wal_ready, a - AR + 1)
                    sp.dma_start(stage[:, a % AR], w_attn[:, :, a]).then_inc(wa_in[a % AR], 16)

                def step(g, u):
                    sp.wait_ge(ratio_ready, g + 1)
                    load_ffn(g + 2, u)
                load_ffn(0, 0)
                load_attn(0)
                load_ffn(1, 1)
                load_attn(1)
                load_attn(2)
                step(0, 0)
                load_attn(3)
                with sp.Fori(0, NWG // 2 - 1) as i:
                    step(2 * i + 1, 1)
                    step(2 * i + 2, 0)
                load_attn(4)
                sp.wait_ge(stored[0], 16 * ((NWG + 1) // 2))
                sp.wait_ge(stored[1], 16 * (NWG // 2))

            @block.gpsimd
            def _(pool):
                pool.memset(ident[:], 0.0).then_inc(ident_ready, 1)
                pool.wait_ge(ident_ready, 1)
                pool.affine_select(out=ident[:], in_=ident[:], compare_op=ALU.not_equal, fill=1.0,
                                   base=0, pattern=[[-1, P]], channel_multiplier=1).then_inc(ident_ready, 1)

                def ratio(g, u):
                    pool.wait_ge(inv_ready, g + 1)
                    wait(pool, deq_ready, g - 1)
                    pool.tensor_tensor(blocks(w_int[:, u]), blocks(w_raw[:, u]), per_block(blk_inv[:, u]),
                                       ALU.mult).then_inc(ratio_ready, 1)
                ratio(0, 0)
                ratio(1, 1)
                ratio(2, 0)
                with pool.Fori(1, NWG // 2) as i:
                    ratio(2 * i + 1, 1)
                    ratio(2 * i + 2, 0)

            @block.vector
            def _(dve):
                def attn_low(a):
                    dve.wait_ge(wah_ready, a + 1)
                    dve.tensor_tensor(wal[:, :, a], stage[:, a % AR], wah[:, :, a].bitcast(F32),
                                      ALU.subtract).then_inc(wal_ready, 1)

                def scales(g, u, k):
                    dve.wait_ge(raw_in[u], 16 * (k + 1))
                    wait(dve, ratio_ready, g - 1)
                    wait(dve, deq_ready, g - 1)
                    dve.tensor_reduce(blk_max[:, u], blocks(w_raw[:, u]), AX.X,
                                      ALU.max, apply_absolute_value=True).then_inc(max_ready, 1)
                    dve.wait_ge(max_ready, g + 1)
                    dve.tensor_scalar(blk_scale[:, u], blk_max[:, u], 1.0 / QMAX4, TINY,
                                      ALU.mult, ALU.max).then_inc(scale_ready, 1)
                    dve.wait_ge(scale_ready, g + 1)
                    dve.reciprocal(blk_inv[:, u], blk_scale[:, u]).then_inc(inv_ready, 1)

                def quantize(g, u):
                    dve.wait_ge(ratio_ready, g + 1)
                    dve.tensor_scalar(w_int[:, u], w_int[:, u], MAGIC, -MAGIC, ALU.add, ALU.add).then_inc(int_ready, 1)
                    dve.wait_ge(int_ready, g + 1)
                    wait(dve, turned_ready, g - 1)
                    dve.tensor_tensor(blocks(w_deq[:, u]), blocks(w_int[:, u]), per_block(blk_scale[:, u]),
                                      ALU.mult).then_inc(deq_ready, 1)

                scales(0, 0, 0)
                attn_low(0)
                scales(1, 1, 0)
                quantize(0, 0)
                attn_low(1)
                scales(2, 0, 1)
                quantize(1, 1)
                with dve.Fori(1, NWG // 2) as i:
                    scales(2 * i + 1, 1, i)
                    quantize(2 * i, 0)
                    scales(2 * i + 2, 0, i + 1)
                    quantize(2 * i + 1, 1)
                quantize(NWG - 1, 0)
                attn_low(2)
                for a in range(AR, NA):
                    attn_low(a)

            @block.tensor
            def _(pe):
                pe.wait_ge(ident_ready, 2)

                def turn(g, u):
                    pe.wait_ge(deq_ready, g + 1)
                    wait(pe, copied, g - 1)
                    for m in range(WG):
                        for k in range(KC):
                            mm = pe.transpose(turned[u][:, m, k * P:(k + 1) * P], w_deq[:, u, m, k * P:(k + 1) * P], ident[:])
                    mm.then_inc(turned_ready, 1)
                turn(0, 0)
                turn(1, 1)
                turn(2, 0)
                with pe.Fori(1, NWG // 2) as i:
                    turn(2 * i + 1, 1)
                    turn(2 * i + 2, 0)

            @block.scalar
            def _(act):
                def attn_high(a):
                    act.wait_ge(wa_in[a % AR], 16 * (a // AR + 1))
                    act.activation(wah[:, :, a], stage[:, a % AR], ACT.Copy).then_inc(wah_ready, 1)

                def store(g, u, k):
                    act.wait_ge(turned_ready, g + 1)
                    wait(act, stored[u], 16 * k)
                    act.activation(w_out[:, u], turned[u][:], ACT.Copy).then_inc(copied, 1)
                    act.wait_ge(copied, g + 1)
                    act.dma_start(w_ffn_t[g], w_out[:, u]).then_inc(stored[u], 16)
                for a in range(AR):
                    attn_high(a)
                store(0, 0, 0)
                store(1, 1, 0)
                attn_high(3)
                store(2, 0, 1)
                with act.Fori(1, NWG // 2) as i:
                    store(2 * i + 1, 1, i)
                    store(2 * i + 2, 0, i + 1)
                attn_high(4)


def attention_phase(nc, xT, x, ctx_in, b_gate, decay_in, wah, wal, x2_dram, amax_x2):
    with ExitStack() as ctx:
        used = []
        ctx.callback(lambda: (nc.clear_and_free_semaphores(used), nc.all_engine_barrier()))

        def sb(name, shape, dt=F32):
            return ctx.enter_context(nc.sbuf_tensor(name, shape, dt))

        def sem(name):
            return phase_semaphore(nc, used, name)

        xt_raw = sb("xt_raw", [P, 2, T])
        xh = sb("xh", [P, KC, T], F32R)
        xl = sb("xl", [P, KC, T], F32R)
        xrow = sb("xrow", [P, TT, HID])
        csq = sb("csq", [P, TT, HID])
        csq_h = sb("csq_h", [P, TT, HID], F32R)
        csq_l = sb("csq_l", [P, TT, HID], F32R)
        phi = sb("phi", [P, 2, 2, T])
        v_sb = sb("v_sb", [P, 2, KC, T])
        att = sb("att", [P, KC, T])
        ah = sb("ah", [P, KC, T], F32R)
        al = sb("al", [P, KC, T], F32R)
        kv = sb("kv", [P, 2, T])
        qks = sb("qks", [P, KC, T])
        den_rec = sb("den_rec", [P, TT, NH])
        rec_halves = sb("rec_halves", [P, TT, 2 * NH], F32R)
        rec_turned = sb("rec_turned", [2 * NH, T], F32R)
        head_bc = sb("head_bc", [2 * NH, KC, P], F32R)
        stripf = kv[:, 0]
        bc_high = qks[0:2 * NH, 0].rearrange("p (c m) -> p c m", m=P)
        bc_low = qks[0:2 * NH, 1].rearrange("p (c m) -> p c m", m=P)
        strip_h = sb("strip_h", [P, T], F32R)
        strip_l = sb("strip_l", [P, T], F32R)
        head_sum = sb("head_sum", [P, KC, NH])
        ident = sb("ident", [P, P])
        ident_r = sb("ident_r", [P, P], F32R)
        c09 = sb("c09", [P, 1])
        decay = sb("decay", [P, KC])
        half_bg = sb("half_bg", [P, KC])
        dtmp = sb("dtmp", [P, KC])
        dtmp2 = sb("dtmp2", [P, KC])
        mhalf = sb("mhalf", [P, TT])
        stats = [sb(f"stats{n}", [P, TT, 6]) for n in range(2)]
        msum = [sb(f"msum{n}", [P, TT]) for n in range(2)]
        mdiff = [sb(f"mdiff{n}", [P, TT]) for n in range(2)]
        msq = [sb(f"msq{n}", [P, TT]) for n in range(2)]
        var_eps = [sb(f"var_eps{n}", [P, TT]) for n in range(2)]
        rstd = [sb(f"rstd{n}", [P, TT]) for n in range(2)]
        nmr = [sb(f"nmr{n}", [P, TT]) for n in range(2)]
        amax_step = sb("amax_step", [P, 1])

        qk_ps = [ctx.enter_context(nc.psum_tensor(f"qk_ps{i}", [P, 2, T], F32)) for i in range(2)]
        v_ps = [ctx.enter_context(nc.psum_tensor(f"v_ps{i}", [P, T], F32)) for i in range(2)]
        mix_ps = [ctx.enter_context(nc.psum_tensor(f"mix_ps{i}", [P, T], F32)) for i in range(2)]
        den_bank = qk_ps[0][:, 0, 0:TT * NH].rearrange("p (j h) -> p j h", h=NH)
        turn_bank = qk_ps[0][0:2 * NH, 1]
        scan_banks = [mix_ps[0][:], mix_ps[1][:], qk_ps[1][:, 0], qk_ps[1][:, 1]]
        bc_banks = [qk_ps[1][:, 0], qk_ps[1][:, 1], v_ps[1][:], v_ps[0][:]]

        xt_in = [sem(f"xt_in{i}") for i in range(2)]
        xrow_in, ctx_landed, x2_stored, small_in = sem("xrow_in"), sem("ctx_landed"), sem("x2_stored"), sem("small_in")
        xh_ready, xl_ready = sem("xh_ready"), sem("xl_ready")
        qk_ready, v_ready = sem("qk_ready"), sem("v_ready")
        neg_ready, e_ready, v_copied = sem("neg_ready"), sem("e_ready"), sem("v_copied")
        phi_ready, kv_ready, ks_scanned, kv_scanned = sem("phi_ready"), sem("kv_ready"), sem("ks_scanned"), sem("kv_scanned")
        qks_ready, qkv_ready = sem("qks_ready"), sem("qkv_ready")
        den_ready, den_clipped, rec_ready, bc_ready, o_ready = (
            sem("den_ready"), sem("den_clipped"), sem("rec_ready"), sem("bc_ready"), sem("o_ready"))
        rech_ready, recl_ready, halves_turned, rec_turned_ready = (
            sem("rech_ready"), sem("recl_ready"), sem("rec_halves_turned"), sem("rec_turned_ready"))
        oh_ready, ol_ready, diff_ready = sem("oh_ready"), sem("ol_ready"), sem("diff_ready")
        gate_ready, tanh_ready, gated, mixed = sem("gate_ready"), sem("tanh_ready"), sem("gated"), sem("mixed")
        mh_ready, ml_ready, proj_ready = sem("mh_ready"), sem("ml_ready"), sem("proj_ready")
        y_ready = [sem("y1_ready"), sem("y2_ready")]
        stats_ready = [sem("stats1_ready"), sem("stats2_ready")]
        moments_ready = [sem("moments1_ready"), sem("moments2_ready")]
        square_ready = [sem("square1_ready"), sem("square2_ready")]
        ve_ready = [sem("ve1_ready"), sem("ve2_ready")]
        rstd_ready = [sem("rstd1_ready"), sem("rstd2_ready")]
        nmr_ready = [sem("nmr1_ready"), sem("nmr2_ready")]
        norm_ready = [sem("norm1_ready"), sem("norm2_ready")]
        sq_ready, sqh_ready, sql_ready, scan_ready = sem("sq_ready"), sem("sqh_ready"), sem("sql_ready"), sem("scan_ready")
        amax_step_ready, amax_taken = sem("amax_step_ready"), sem("amax_taken")
        const_pool, const_dve, const_act = sem("const_pool"), sem("const_dve"), sem("const_act")
        NPOOL = 16

        with nc.Block() as block:
            @block.sync
            def _(sp):
                def load_xt(b, k):
                    wait(sp, xl_ready, 4 * b + k - 1)
                    sp.dma_start(xt_raw[:, k % 2], xT[b, k]).then_inc(xt_in[k % 2], 16)

                def step(s, front, back, nxt):
                    if nxt:
                        for k in range(KC):
                            load_xt(s + 1, k)
                    if front:
                        wait(sp, sql_ready, s)
                        sp.dma_start(csq[:], ctx_in[s]).then_inc(ctx_landed, 16)
                    if back:
                        sp.wait_ge(norm_ready[1], TT * s)
                        sp.dma_start(x2_dram[s - 1], xrow[:]).then_inc(x2_stored, 16)
                    if front:
                        if back:
                            sp.wait_ge(x2_stored, 16 * s)
                            sp.wait_ge(amax_step_ready, s)
                        sp.dma_start(xrow[:], x[s]).then_inc(xrow_in, 16)

                for k in range(KC):
                    load_xt(0, k)
                    if k == 1:
                        sp.dma_start(half_bg[:], b_gate).then_inc(small_in, 16)
                        sp.dma_start(dtmp[:], decay_in).then_inc(small_in, 16)
                step(0, True, False, True)
                with sp.Fori(0, (NB - 2) // 2) as i:
                    for u in range(2):
                        step(2 * i + 1 + u, True, True, True)
                step(NB - 1, True, True, False)
                step(NB, False, True, False)
                sp.wait_ge(x2_stored, 16 * NB)

            @block.gpsimd
            def _(pool):
                pool.memset(head_sum[:], 1.0).then_inc(const_pool, 1)
                pool.memset(ident[:], 0.0).then_inc(const_pool, 1)
                pool.memset(stripf, 0.0).then_inc(const_pool, 1)
                pool.memset(mhalf[:], -0.5).then_inc(const_pool, 1)
                pool.memset(c09[:], XDECAY).then_inc(const_pool, 1)
                pool.memset(amax_x2[:], 0.0).then_inc(const_pool, 1)
                pool.memset(bc_high, 1.0).then_inc(const_pool, 1)
                pool.memset(bc_low, 1.0).then_inc(const_pool, 1)
                D = HID // NH
                pool.wait_ge(const_pool, 8)
                pool.affine_select(out=head_sum[:], in_=head_sum[:], compare_op=ALU.is_ge, fill=0.0,
                                   base=0, pattern=[[P, KC], [-D, NH]], channel_multiplier=1).then_inc(const_pool, 1)
                pool.affine_select(out=ident[:], in_=ident[:], compare_op=ALU.not_equal, fill=1.0,
                                   base=0, pattern=[[-1, P]], channel_multiplier=1).then_inc(const_pool, 1)
                pool.affine_select(out=stripf, in_=stripf, compare_op=ALU.not_equal, fill=1.0,
                                   base=0, pattern=[[-1, T]], channel_multiplier=1).then_inc(const_pool, 1)
                for rows, base in ((bc_high, 0), (bc_low, NH * D)):
                    pool.affine_select(out=rows, in_=rows, compare_op=ALU.is_ge, fill=0.0,
                                       base=base, pattern=[[P, KC], [1, P]], channel_multiplier=-D).then_inc(const_pool, 1)
                pool.wait_ge(const_pool, 13)
                for rows, base in ((bc_high, 0), (bc_low, NH * D)):
                    pool.affine_select(out=rows, in_=rows, compare_op=ALU.is_ge, fill=0.0,
                                       base=D - 1 - base, pattern=[[-P, KC], [-1, P]], channel_multiplier=D).then_inc(const_pool, 1)
                pool.affine_select(out=head_sum[:], in_=head_sum[:], compare_op=ALU.is_ge, fill=0.0,
                                   base=D - 1, pattern=[[-P, KC], [D, NH]], channel_multiplier=-1).then_inc(const_pool, 1)

                def root(n, s):
                    pool.wait_ge(ve_ready[n], s)
                    pool.tensor_tensor(rstd[n][:], var_eps[n][:], mhalf[:], ALU.pow).then_inc(rstd_ready[n], 1)

                def step(s, front, back):
                    if back:
                        pool.wait_ge(ctx_landed, 16 * s)
                        pool.tensor_tensor(csq[:], csq[:], csq[:], ALU.mult).then_inc(sq_ready, 1)
                        pool.wait_ge(sqh_ready, s)
                        pool.tensor_tensor(csq_l[:], csq[:], csq_h[:].bitcast(F32), ALU.subtract).then_inc(sql_ready, 1)
                        root(0, s)
                        root(1, s)

                with pool.Fori(0, (NB - 2) // 2) as i:
                    for u in range(2):
                        step(2 * i + 1 + u, True, True)
                step(NB - 1, True, True)
                step(NB, False, True)

            @block.scalar
            def _(act):
                act.wait_ge(small_in, 32)
                act.activation(dtmp2[:], dtmp[:], ACT.Tanh, scale=0.5).then_inc(const_act, 1)
                act.wait_ge(const_dve, 1)

                def split_x(b, tiles=range(KC)):
                    if 0 in tiles:
                        wait(act, v_ready, KC * b)
                    for k in tiles:
                        act.wait_ge(xt_in[k % 2], 16 * (2 * b + k // 2 + 1))
                        act.activation(xh[:, k], xt_raw[:, k % 2], ACT.Copy).then_inc(xh_ready, 1)

                def front_tile(b, c, par):
                    n = KC * b + c
                    act.wait_ge(qk_ready, n + 1)
                    wait(act, qkv_ready, n - 1)
                    act.activation(phi[:, c % 2], qk_ps[c % 2][:], ACT.Relu, scale=-1.0).then_inc(neg_ready, 1)
                    act.wait_ge(neg_ready, n + 1)
                    act.activation(phi[:, c % 2], phi[:, c % 2], ACT.Exp, scale=-1.0).then_inc(e_ready, 1)
                    act.wait_ge(v_ready, n + 1)
                    act.activation(v_sb[:, par, c], v_ps[c % 2][:], ACT.Copy).then_inc(v_copied, 1)

                def normalise(n, s):
                    act.wait_ge(nmr_ready[n], s)
                    for j in range(TT):
                        act.activation(xrow[:, j], xrow[:, j], ACT.Identity, scale=rstd[n][:, j:j + 1],
                                       bias=nmr[n][:, j:j + 1]).then_inc(norm_ready[n], 1)

                def step(s, par, front, back, nxt, due=True):
                    if front:
                        front_tile(s, 0, par)
                    if back:
                        for m in range(KC):
                            act.wait_ge(gate_ready, KC * (s - 1) + m + 1)
                            bank = mix_ps[(m + 1) % 2]
                            act.activation(bank[:], bank[:], ACT.Tanh, scale=0.5,
                                           bias=half_bg[:, m:m + 1]).then_inc(tanh_ready, 1)
                            if m == 0 and due:
                                normalise(1, s - 1)
                        for m in range(KC):
                            act.wait_ge(mixed, KC * (s - 1) + m + 1)
                            act.activation(ah[:, m], att[:, m], ACT.Copy).then_inc(mh_ready, 1)
                    if front:
                        front_tile(s, 1, par)
                    if back:
                        act.wait_ge(sq_ready, s)
                        wait(act, scan_ready, TT * (s - 1) if not isinstance(s, int) or s > 1 else 0)
                        act.activation(csq_h[:], csq[:], ACT.Copy).then_inc(sqh_ready, 1)
                    if front:
                        front_tile(s, 2, par)
                        front_tile(s, 3, par)
                    if nxt:
                        split_x(s + 1, (0, 1))
                    if front:
                        act.wait_ge(halves_turned, s + 1)
                        act.activation(rec_turned[:], turn_bank, ACT.Copy).then_inc(rec_turned_ready, 1)
                    if nxt:
                        split_x(s + 1, (2, 3))
                    if back:
                        normalise(0, s)
                    if front:
                        for c in range(KC):
                            act.wait_ge(o_ready, KC * s + c + 1)
                            act.activation(ah[:, c], att[:, c], ACT.Copy).then_inc(oh_ready, 1)

                split_x(0)
                step(0, 0, True, False, True, due=False)
                step(1, 1, True, True, True, due=False)
                step(2, 0, True, True, True)
                with act.Fori(1, (NB - 2) // 2) as i:
                    for u in range(2):
                        step(2 * i + 1 + u, (1 + u) % 2, True, True, True)
                step(NB - 1, 1, True, True, False)
                step(NB, 0, False, True, False)
                normalise(1, NB)

            @block.vector
            def _(dve):
                dve.wait_ge(small_in, 32)
                dve.tensor_scalar(half_bg[:], half_bg[:], 0.5, None, ALU.mult).then_inc(const_dve, 1)
                dve.wait_ge(const_act, 1)
                dve.tensor_scalar(decay[:], dtmp2[:], 0.5, 0.5, ALU.mult, ALU.add).then_inc(const_dve, 1)
                dve.wait_ge(const_dve, 2)
                dve.tensor_scalar(decay[:], decay[:], 1e-8, None, ALU.max).then_inc(const_dve, 1)
                dve.wait_ge(const_pool, NPOOL)
                dve.tensor_tensor_scan(stripf, c09[:, 0:1].to_broadcast([P, T]), stripf, 0.0,
                                       ALU.mult, ALU.add).then_inc(const_dve, 1)
                dve.wait_ge(const_dve, 4)
                dve.tensor_copy(strip_h[:], stripf).then_inc(const_dve, 1)
                dve.tensor_copy(ident_r[:], ident[:]).then_inc(const_dve, 1)
                dve.tensor_tensor(head_bc[:], bc_high, bc_low, ALU.add).then_inc(const_dve, 1)
                dve.wait_ge(const_dve, 7)
                dve.tensor_tensor(strip_l[:], stripf, strip_h[:].bitcast(F32), ALU.subtract).then_inc(const_dve, 1)

                def split_x(b, tiles=range(KC)):
                    for k in tiles:
                        dve.wait_ge(xh_ready, KC * b + k + 1)
                        dve.tensor_tensor(xl[:, k], xt_raw[:, k % 2], xh[:, k].bitcast(F32),
                                          ALU.subtract).then_inc(xl_ready, 1)

                def front_scans(b, c, par, between=None):
                    n = KC * b + c
                    sl = c % 2
                    dve.wait_ge(e_ready, n + 1)
                    dve.scalar_tensor_tensor(phi[:, sl], qk_ps[sl][:], 0.0, phi[:, sl], ALU.max, ALU.add).then_inc(phi_ready, 1)
                    dve.wait_ge(phi_ready, n + 1)
                    wait(dve, den_ready, b)
                    dve.tensor_tensor_scan(qks[:, c], decay[:, c:c + 1].to_broadcast([P, T]), phi[:, sl, 1], 0.0,
                                           ALU.mult, ALU.add).then_inc(ks_scanned, 1)
                    if between:
                        between()
                    dve.wait_ge(v_copied, n + 1)
                    dve.tensor_tensor(kv[:, sl], phi[:, sl, 1], v_sb[:, par, c], ALU.mult).then_inc(kv_ready, 1)
                    dve.wait_ge(ks_scanned, n + 1)
                    dve.tensor_tensor(qks[:, c], phi[:, sl, 0], qks[:, c], ALU.mult).then_inc(qks_ready, 1)
                    dve.wait_ge(kv_ready, n + 1)
                    dve.tensor_tensor_scan(kv[:, sl], decay[:, c:c + 1].to_broadcast([P, T]), kv[:, sl], 0.0,
                                           ALU.mult, ALU.add).then_inc(kv_scanned, 1)

                def front_product(b, c):
                    dve.wait_ge(kv_scanned, KC * b + c + 1)
                    dve.tensor_tensor(att[:, c], phi[:, c % 2, 0], kv[:, c % 2], ALU.mult).then_inc(qkv_ready, 1)

                def norm_scalars(n, s):
                    dve.wait_ge(stats_ready[n], TT * s)
                    row_moments(dve, stats[n], msum[n][:], mdiff[n][:], msq[n][:], var_eps[n][:],
                                moments_ready[n], square_ready[n], ve_ready[n], s)

                def norm_bias(n, s):
                    dve.wait_ge(rstd_ready[n], s)
                    dve.scalar_tensor_tensor(nmr[n][:], msum[n][:], -0.5, rstd[n][:],
                                             ALU.mult, ALU.mult).then_inc(nmr_ready[n], 1)

                def second_residual(s, tiles):
                    for j in tiles:
                        n = TT * (s - 1) + j + 1
                        dve.wait_ge(norm_ready[0], n)
                        dve.wait_ge(scan_ready, n)
                        dve.scalar_tensor_tensor(xrow[:, j], scan_banks[j], 1.0, xrow[:, j],
                                                 ALU.add, ALU.mult).then_inc(y_ready[1], 1)
                        dve.wait_ge(y_ready[1], n)
                        dve.bn_stats(stats[1][:, j], xrow[:, j]).then_inc(stats_ready[1], 1)

                def quotient(b, tiles):
                    for c in tiles:
                        n = KC * b + c + 1
                        dve.wait_ge(bc_ready, n)
                        dve.wait_ge(qkv_ready, n)
                        dve.tensor_tensor(att[:, c], att[:, c], bc_banks[c], ALU.mult).then_inc(o_ready, 1)

                def reciprocals(b):
                    dve.wait_ge(den_ready, b + 1)
                    dve.tensor_scalar(den_rec[:], den_bank, 1e-6, None, ALU.max).then_inc(den_clipped, 1)
                    dve.wait_ge(den_clipped, b + 1)
                    dve.reciprocal(den_rec[:], den_rec[:]).then_inc(rec_ready, 1)
                    dve.wait_ge(rec_ready, b + 1)
                    dve.tensor_copy(rec_halves[:, :, 0:NH], den_rec[:]).then_inc(rech_ready, 1)
                    dve.wait_ge(rech_ready, b + 1)
                    dve.tensor_tensor(rec_halves[:, :, NH:], den_rec[:], rec_halves[:, :, 0:NH].bitcast(F32),
                                      ALU.subtract).then_inc(recl_ready, 1)

                def split_quotient(b, par, tiles):
                    for c in tiles:
                        n = KC * b + c + 1
                        dve.wait_ge(oh_ready, n)
                        dve.tensor_tensor(al[:, c], att[:, c], ah[:, c].bitcast(F32), ALU.subtract).then_inc(ol_ready, 1)
                    for c in tiles:
                        n = KC * b + c + 1
                        dve.wait_ge(ol_ready, n)
                        dve.tensor_tensor(att[:, c], att[:, c], v_sb[:, par, c], ALU.subtract).then_inc(diff_ready, 1)

                def scale_difference(s, m):
                    n = KC * (s - 1) + m + 1
                    dve.wait_ge(tanh_ready, n)
                    dve.wait_ge(diff_ready, n)
                    dve.scalar_tensor_tensor(att[:, m], mix_ps[(m + 1) % 2][:], 1.0, att[:, m],
                                             ALU.add, ALU.mult).then_inc(gated, 1)

                def add_v(s, m, par):
                    dve.wait_ge(gated, KC * (s - 1) + m + 1)
                    dve.scalar_tensor_tensor(att[:, m], att[:, m], 0.5, v_sb[:, 1 - par, m],
                                             ALU.mult, ALU.add).then_inc(mixed, 1)

                def largest(s):
                    dve.wait_ge(norm_ready[1], TT * s)
                    dve.tensor_reduce(amax_step[:], xrow[:].rearrange("p j c -> p (j c)"), AX.X, ALU.max,
                                      apply_absolute_value=True).then_inc(amax_step_ready, 1)
                    dve.wait_ge(amax_step_ready, s)
                    dve.tensor_tensor(amax_x2[:], amax_x2[:], amax_step[:], ALU.max).then_inc(amax_taken, 1)
                    dve.wait_ge(amax_taken, s)

                def step(s, par, front, back, nxt, due=True):
                    def gate_first():
                        if due:
                            norm_bias(1, s - 1)
                        scale_difference(s, 0)
                    if front and back:
                        front_scans(s, 0, par, gate_first)
                    elif front:
                        front_scans(s, 0, par)
                    else:
                        gate_first()
                    if back:
                        add_v(s, 0, par)
                        for m in range(1, KC):
                            scale_difference(s, m)
                            add_v(s, m, par)
                        for m in range(KC):
                            dve.wait_ge(mh_ready, KC * (s - 1) + m + 1)
                            dve.tensor_tensor(al[:, m], att[:, m], ah[:, m].bitcast(F32), ALU.subtract).then_inc(ml_ready, 1)
                        dve.wait_ge(ml_ready, KC * s)
                        if due:
                            largest(s - 1)
                    if front:
                        front_product(s, 0)
                        for c in range(1, KC):
                            front_scans(s, c, par)
                            front_product(s, c)
                    if back:
                        dve.wait_ge(xrow_in, 16 * s)
                        for j in range(TT):
                            n = TT * (s - 1) + j + 1
                            dve.wait_ge(proj_ready, n)
                            dve.tensor_tensor(xrow[:, j], mix_ps[(j + 1) % 2][:], xrow[:, j], ALU.add).then_inc(y_ready[0], 1)
                            if j == 1 and front:
                                reciprocals(s)
                            dve.wait_ge(y_ready[0], n)
                            dve.bn_stats(stats[0][:, j], xrow[:, j]).then_inc(stats_ready[0], 1)
                            if j == 1 and nxt:
                                split_x(s + 1, (0, 1))
                        norm_scalars(0, s)
                    else:
                        split_x(s + 1, (0, 1))
                        reciprocals(s)
                    if front:
                        quotient(s, (0, 1))
                    if back:
                        norm_bias(0, s)
                    if front:
                        quotient(s, (2, 3))
                    if back:
                        second_residual(s, (0,))
                    if nxt:
                        split_x(s + 1, (2, 3))
                    if back:
                        second_residual(s, (1,))
                    if front:
                        split_quotient(s, par, (0, 1))
                    if back:
                        second_residual(s, (2,))
                    if front:
                        split_quotient(s, par, (2, 3))
                    if back:
                        second_residual(s, (3,))
                        norm_scalars(1, s)
                split_x(0)
                step(0, 0, True, False, True)
                step(1, 1, True, True, True, due=False)
                with dve.Fori(1, (NB - 2) // 2) as i:
                    for u in range(2):
                        step(2 * i + u, u, True, True, True)
                step(NB - 2, 0, True, True, True)
                step(NB - 1, 1, True, True, False)
                step(NB, 0, False, True, False)
                norm_bias(1, NB)
                largest(NB)

            @block.tensor
            def _(pe):
                pe.wait_ge(const_pool, NPOOL)
                pe.wait_ge(const_dve, 8)

                def product(out, stat, mov, between=None):
                    n = len(stat)
                    for k in range(n):
                        (sh, sl_), (mh, ml) = stat[k], mov[k]
                        pe.matmul(out, sh, mh, start=(k == 0), stop=False)
                        pe.matmul(out, sh, ml, start=False, stop=False)
                        if between:
                            between(k)
                        mm = pe.matmul(out, sl_, mh, start=False, stop=(k == n - 1))
                    return mm

                def w_tile(g, m):
                    cols = slice(m * P, (m + 1) * P)
                    return [(wah[:, k, g, cols], wal[:, k, g, cols]) for k in range(KC)]

                x_halves = [(xh[:, k], xl[:, k]) for k in range(KC)]
                a_halves = [(ah[:, k], al[:, k]) for k in range(KC)]

                def qkv(b, c):
                    n = KC * b + c
                    if c == 0:
                        pe.wait_ge(xl_ready, KC * (b + 1))
                    wait(pe, phi_ready, n - 1)
                    product(qk_ps[c % 2][:, 0], w_tile(0, c), x_halves)
                    product(qk_ps[c % 2][:, 1], w_tile(1, c), x_halves).then_inc(qk_ready, 1)
                    wait(pe, v_copied, n - 1)
                    if c == 0:
                        wait(pe, o_ready, KC * b)
                    product(v_ps[c % 2][:], w_tile(2, c), x_halves).then_inc(v_ready, 1)

                def gate(s):
                    pe.wait_ge(ol_ready, KC * s)
                    for m in range(KC):
                        if m >= 2:
                            pe.wait_ge(gated, KC * (s - 1) + m - 1)
                        product(mix_ps[(m + 1) % 2][:], w_tile(3, m), a_halves).then_inc(gate_ready, 1)

                def project(s, tiles, between=None):
                    if 0 in tiles:
                        pe.wait_ge(ml_ready, KC * s)
                    for j in tiles:
                        if j < 2:
                            pe.wait_ge(gated, KC * (s - 1) + j + 3)
                        else:
                            pe.wait_ge(y_ready[0], TT * (s - 1) + j - 1)
                        stat = [(ah[:, k, j * P:(j + 1) * P], al[:, k, j * P:(j + 1) * P]) for k in range(KC)]
                        mov = [(wah[:, k, 4], wal[:, k, 4]) for k in range(KC)]
                        product(mix_ps[(j + 1) % 2][:], stat, mov, between).then_inc(proj_ready, 1)

                def denominators(s, j):
                    if j == 0:
                        pe.wait_ge(qks_ready, KC * (s + 1))
                    for c in range(KC):
                        mm = pe.matmul(den_bank[:, j], qks[:, c, j * P:(j + 1) * P], head_sum[:, c],
                                       start=(c == 0), stop=(c == KC - 1))
                    if j == TT - 1:
                        mm.then_inc(den_ready, 1)

                def turn_reciprocals(s):
                    pe.wait_ge(recl_ready, s + 1)
                    for j in range(TT):
                        mm = pe.matmul(turn_bank[:, j * P:(j + 1) * P], rec_halves[:, j], ident_r[:], start=True, stop=True)
                    mm.then_inc(halves_turned, 1)

                def broadcast(s):
                    pe.wait_ge(rec_turned_ready, s + 1)
                    pe.wait_ge(v_copied, KC * (s + 1))
                    for c in range(KC):
                        pe.matmul(bc_banks[c], head_bc[:, c], rec_turned[:], start=True, stop=True).then_inc(bc_ready, 1)

                def context_scan(s, front):
                    pe.wait_ge(sql_ready, s)
                    for j in range(TT):
                        if j < 2:
                            pe.wait_ge(y_ready[0], TT * s - j)
                        elif front:
                            pe.wait_ge(o_ready, KC * s + j - 1)
                        stat = [(strip_h[:, (j - i) * P:(j - i + 1) * P], strip_l[:, (j - i) * P:(j - i + 1) * P])
                                for i in range(j + 1)]
                        mov = [(csq_h[:, i], csq_l[:, i]) for i in range(j + 1)]
                        product(scan_banks[j], stat, mov).then_inc(scan_ready, 1)

                def step(s, front, back):
                    if front:
                        qkv(s, 0)
                    if back:
                        gate(s)
                    if front:
                        for c in range(1, KC):
                            qkv(s, c)
                    if back:
                        project(s, (0,))
                    if front and back:
                        project(s, (1,), lambda j: denominators(s, j))
                    elif back:
                        project(s, (1,))
                    else:
                        for j in range(TT):
                            denominators(s, j)
                    if back:
                        project(s, (2,))
                    if front:
                        turn_reciprocals(s)
                    if back:
                        project(s, (3,))
                    if front:
                        broadcast(s)
                    if back:
                        context_scan(s, front)

                step(0, True, False)
                with pe.Fori(0, (NB - 2) // 2) as i:
                    for u in range(2):
                        step(2 * i + 1 + u, True, True)
                step(NB - 1, True, True)
                step(NB, False, True)


NCH = NB * 3
CH = 4 * T
QUICK = 2


def up_gate_phase(nc, x2_dram, w_ffn_t, up_dram, gate_dram, amax_x2, acc, rmax, scales):
    NM = 2 * MT
    GM = 4
    NG = NM // GM
    with ExitStack() as ctx:
        used = []
        ctx.callback(lambda: (nc.clear_and_free_semaphores(used), nc.all_engine_barrier()))

        def sb(name, shape, dt=F32):
            return ctx.enter_context(nc.sbuf_tensor(name, shape, dt))

        def sem(name):
            return phase_semaphore(nc, used, name)

        wh = sb("ug_wh", [P, NM, KC, P], F32R)
        wl = sb("ug_wl", [P, NM, KC, P], F32R)
        w_stage = sb("ug_w_stage", [P, 2, GM, KC * P])
        x2 = sb("ug_x2", [P, TT, HID])
        qh = sb("ug_qh", [P, 2, KC, T], F32R)
        ql = sb("ug_ql", [P, 2, KC, T], F32R)
        group = sb("ug_group", [P, 4, CH])
        silu = sb("ug_silu", [P, 2, CH])
        ident = sb("ug_ident", [P, P])
        step_max = sb("ug_step_max", [P, 3, 3])
        turn_ps = [ctx.enter_context(nc.psum_tensor(f"ug_turn{i}", [P, T], F32)) for i in range(2)]
        out_ps = [ctx.enter_context(nc.psum_tensor(f"ug_out{i}", [P, T], F32)) for i in range(6)]

        w_in = [sem(f"ug_w_in{i}") for i in range(2)]
        wh_ready, wl_ready = sem("ug_wh_ready"), sem("ug_wl_ready")
        x2_in = sem("ug_x2_in")
        stored = [sem(f"ug_stored{i}") for i in range(4)]
        consts, amax_all, scale_ready, inv_ready = sem("ug_consts"), sem("ug_amax_all"), sem("ug_scale_ready"), sem("ug_inv_ready")
        tq_ready, turned, qh_ready, ql_ready = sem("ug_tq_ready"), sem("ug_turned"), sem("ug_qh_ready"), sem("ug_ql_ready")
        out_ready, evacuated, silu_ready, prod_ready, rmax_ready = (
            sem("ug_out_ready"), sem("ug_evacuated"), sem("ug_silu_ready"), sem("ug_prod_ready"), sem("ug_rmax_ready"))
        step_max_ready, acc_ready = sem("ug_step_max_ready"), sem("ug_acc_ready")
        s_x, inv_x = scales[:, 0:1], scales[:, 1:2]

        def group_of(w, g):
            return w[:, g * GM:(g + 1) * GM].rearrange("p m k n -> p m (k n)")

        def slot(par, g):
            return (NG * par + g) % 4

        with nc.Block() as block:
            @block.sync
            def _(sp):
                sp.dma_start(x2[:], x2_dram[0]).then_inc(x2_in, 16)

                def load_weights(g):
                    if g < NG:
                        group_at = NWG // 3 * (g % 2) + g // 2
                        wait(sp, wl_ready, g - 1)
                        sp.dma_start(w_stage[:, g % 2], w_ffn_t[group_at]).then_inc(w_in[g % 2], 16)
                load_weights(0)
                load_weights(1)

                def step(b, par, nxt, first=False):
                    if nxt:
                        sp.wait_ge(turned, KC * (b + 1))
                        sp.dma_start(x2[:], x2_dram[b + 1]).then_inc(x2_in, 16)
                    for g in range(NG):
                        if first:
                            load_weights(g + 2)
                        sp.wait_ge(evacuated, GM * (NG * b + g + 1))
                        dst = (gate_dram if g % 2 else up_dram)[3 * b + g // 2]
                        sp.dma_start(dst, group[:, slot(par, g)]).then_inc(stored[slot(par, g)], 16)
                step(0, 0, True, True)
                step(1, 1, True)
                with sp.Fori(1, NB // 2 - 1) as i:
                    for u in range(2):
                        step(2 * i + u, u, True)
                step(NB - 2, 0, True)
                step(NB - 1, 1, False)
                for sl in range(4):
                    sp.wait_ge(stored[sl], 16 * NB * NG // 4)

            @block.gpsimd
            def _(pool):
                pool.memset(ident[:], 0.0).then_inc(consts, 1)
                pool.memset(acc[:], -3e38).then_inc(consts, 1)
                pool.partition_all_reduce(amax_x2[:], amax_x2[:], P, bass.bass_isa.ReduceOp.max).then_inc(amax_all, 1)
                pool.wait_ge(consts, 2)
                pool.affine_select(out=ident[:], in_=ident[:], compare_op=ALU.not_equal, fill=1.0,
                                   base=0, pattern=[[-1, P]], channel_multiplier=1).then_inc(consts, 1)

            @block.scalar
            def _(act):
                def weights_high(g):
                    if g < NG:
                        act.wait_ge(w_in[g % 2], 16 * (g // 2 + 1))
                        act.activation(group_of(wh, g), w_stage[:, g % 2], ACT.Copy).then_inc(wh_ready, 1)
                weights_high(0)
                act.wait_ge(inv_ready, 1)

                def high(b, par):
                    for c in range(KC):
                        act.wait_ge(turned, KC * b + c + 1)
                        act.activation(qh[:, par, c], low16(turn_ps[c % 2][:], I16), ACT.Copy).then_inc(qh_ready, 1)

                def outputs(b, par, k, g, first):
                    n = NG * par + g
                    wait(act, stored[n % 4], 16 * (3 * k + n // 4))
                    if not (first and n < 4):
                        act.wait_ge(prod_ready, 3 * b + g // 2 - 1)
                    for m in range(GM):
                        act.wait_ge(out_ready, NM * b + g * GM + m + 1)
                        act.activation(group[:, n % 4, m * T:(m + 1) * T], out_ps[(g * GM + m) % 6][:], ACT.Copy,
                                       scale=s_x).then_inc(evacuated, 1)
                    if g % 2:
                        p = 3 * par + g // 2
                        act.wait_ge(evacuated, GM * (NG * b + g + 1))
                        if not (first and p < 2):
                            act.wait_ge(rmax_ready, 3 * b + g // 2 - 1)
                        act.activation(silu[:, p % 2], group[:, n % 4], ACT.Silu).then_inc(silu_ready, 1)

                def step(b, par, k, nxt, first=False):
                    for g in range(NG):
                        outputs(b, par, k, g, first)
                        if first:
                            weights_high(g + 2)
                        if g == 2 and nxt:
                            high(b + 1, 1 - par)
                high(0, 0)
                weights_high(1)
                step(0, 0, 0, True, True)
                step(1, 1, 0, True)
                with act.Fori(1, NB // 2 - 1) as i:
                    for u in range(2):
                        step(2 * i + u, u, i, True)
                step(NB - 2, 0, NB // 2 - 1, True)
                step(NB - 1, 1, NB // 2 - 1, False)

            @block.vector
            def _(dve):
                dve.wait_ge(amax_all, 1)
                dve.tensor_scalar(s_x, amax_x2[:], 1.0 / QMAX16, TINY, ALU.mult, ALU.max).then_inc(scale_ready, 1)
                dve.wait_ge(scale_ready, 1)
                dve.reciprocal(inv_x, s_x).then_inc(inv_ready, 1)
                dve.wait_ge(inv_ready, 1)

                def quantize(b):
                    dve.wait_ge(x2_in, 16 * (b + 1))
                    dve.tensor_scalar(x2[:], x2[:], inv_x, MAGIC, ALU.mult, ALU.add).then_inc(tq_ready, 1)

                def low(b, par):
                    for c in range(KC):
                        dve.wait_ge(qh_ready, KC * b + c + 1)
                        dve.tensor_tensor(ql[:, par, c], low16(turn_ps[c % 2][:], I16), qh[:, par, c].bitcast(F32),
                                          ALU.subtract).then_inc(ql_ready, 1)

                def largest(b, par, g):
                    q = g // 2
                    part = group[:, slot(par, g)]
                    dve.wait_ge(evacuated, GM * (NG * b + g + 1))
                    if g % 2 == 0:
                        dve.tensor_reduce(step_max[:, 0, q:q + 1], part, AX.X, ALU.max,
                                          apply_absolute_value=True).then_inc(step_max_ready, 1)
                        return
                    dve.tensor_reduce(step_max[:, 1, q:q + 1], part, AX.X, ALU.max).then_inc(step_max_ready, 1)
                    dve.tensor_reduce(step_max[:, 2, q:q + 1], part, AX.X, ALU.min, negate=True).then_inc(step_max_ready, 1)
                    sil = silu[:, (3 * par + q) % 2]
                    dve.wait_ge(silu_ready, 3 * b + q + 1)
                    dve.tensor_tensor(sil, sil, group[:, slot(par, g - 1)], ALU.mult).then_inc(prod_ready, 1)
                    dve.wait_ge(prod_ready, 3 * b + q + 1)
                    t = 3 * b + q
                    dve.tensor_reduce(rmax[:, bass.ds(t, 1)], sil, AX.X, ALU.max, apply_absolute_value=True).then_inc(rmax_ready, 1)

                def weights_low(g):
                    if g < NG:
                        dve.wait_ge(wh_ready, g + 1)
                        dve.tensor_tensor(group_of(wl, g), w_stage[:, g % 2], group_of(wh, g).bitcast(F32),
                                          ALU.subtract).then_inc(wl_ready, 1)

                def step(b, par, nxt, first=False):
                    for g in range(NG):
                        if g == 1 and nxt:
                            quantize(b + 1)
                        if g == 3 and nxt:
                            low(b + 1, 1 - par)
                        largest(b, par, g)
                        if first:
                            weights_low(g + 2)
                    dve.wait_ge(step_max_ready, 9 * (b + 1))
                    dve.tensor_tensor(acc[:], acc[:], step_max[:], ALU.max).then_inc(acc_ready, 1)
                    dve.wait_ge(acc_ready, b + 1)

                dve.wait_ge(consts, 3)
                quantize(0)
                weights_low(0)
                low(0, 0)
                weights_low(1)
                step(0, 0, True, True)
                step(1, 1, True)
                with dve.Fori(1, NB // 2 - 1) as i:
                    for u in range(2):
                        step(2 * i + u, u, True)
                step(NB - 2, 0, True)
                step(NB - 1, 1, False)

            @block.tensor
            def _(pe):
                pe.wait_ge(consts, 3)

                def turn(b, tiles):
                    pe.wait_ge(tq_ready, b + 1)
                    for c in tiles:
                        wait(pe, ql_ready, KC * b + c - 1)
                        for j in range(TT):
                            mm = pe.transpose(turn_ps[c % 2][:, j * P:(j + 1) * P], x2[:, j, c * P:(c + 1) * P], ident[:])
                        mm.then_inc(turned, 1)

                def tile(b, par, m, first):
                    if not (first and m < 6):
                        pe.wait_ge(evacuated, NM * b + m - 5)
                    for k in range(KC):
                        o = out_ps[m % 6][:]
                        pe.matmul(o, wh[:, m, k], qh[:, par, k], start=(k == 0), stop=False)
                        pe.matmul(o, wh[:, m, k], ql[:, par, k], start=False, stop=False)
                        mm = pe.matmul(o, wl[:, m, k], qh[:, par, k], start=False, stop=(k == KC - 1))
                    mm.then_inc(out_ready, 1)

                def step(b, par, nxt, first=False):
                    pe.wait_ge(ql_ready, KC * (b + 1))
                    for m in range(NM):
                        if first and m % GM == 0:
                            pe.wait_ge(wl_ready, m // GM + 1)
                        tile(b, par, m, first)
                        if m == 11 and nxt:
                            turn(b + 1, (0, 1))
                        if m == 13 and nxt:
                            turn(b + 1, (2, 3))
                turn(0, range(KC))
                step(0, 0, True, True)
                step(1, 1, True)
                with pe.Fori(1, NB // 2 - 1) as i:
                    for u in range(2):
                        step(2 * i + u, u, True)
                step(NB - 2, 0, True)
                step(NB - 1, 1, False)


def quantizer(dve, scale, inv, amax, sem, count):
    dve.tensor_scalar(scale, amax, 1.0 / QMAX16, TINY, ALU.mult, ALU.max).then_inc(sem, 1)
    dve.wait_ge(sem, count + 1)
    dve.reciprocal(inv, scale).then_inc(sem, 1)
    dve.wait_ge(sem, count + 2)
    return count + 2


def scales_phase(nc, up_dram, gate_dram, w_ffn_t, acc, rmax, scales, wh, wl):
    MARGIN = 1e-3 * QMAX16 * QMAX16
    SILU_SURE = 0.28
    with ExitStack() as ctx:
        used = []
        ctx.callback(lambda: (nc.clear_and_free_semaphores(used), nc.all_engine_barrier()))

        def sb(name, shape, dt=F32):
            return ctx.enter_context(nc.sbuf_tensor(name, shape, dt))

        def sem(name):
            return phase_semaphore(nc, used, name)

        R = 3
        gate = sb("sc_gate", [P, R, CH])
        up = sb("sc_up", [P, R, CH])
        gs = sb("sc_gs", [P, R, CH])
        w_stage = sb("sc_w_stage", [P, NWG // 3, KC, KC * P])
        packed = sb("sc_packed", [P, 3 + NCH])
        packed_all = sb("sc_packed_all", [P, 3 + NCH])
        gmag = sb("sc_gmag", [P, 1])
        top = sb("sc_top", [P, 4])
        amax_gs = sb("sc_amax_gs", [P, 1])
        amax_o = sb("sc_amax_o", [P, 1])
        part_max = sb("sc_part_max", [P, 1])
        tmp = sb("sc_tmp", [P, 8])
        magic = sb("sc_magic", [P, 1])
        best = sb("sc_best", [P, 8])
        best_at = sb("sc_best_at", [P, 8], mybir.dt.uint32)
        go_through = sb("sc_go_through", [P, 1], mybir.dt.int32)
        s_u, inv_u, s_g, inv_g, s_gs, inv_gs, gs_factor, s_o, inv_o, o_factor = (scales[:, i:i + 1] for i in range(2, 12))

        consts, packed_ready, all_ready, sc, top_ready, top_sig = (
            sem("sc_consts"), sem("sc_packed_ready"), sem("sc_all_ready"), sem("sc_scalars"), sem("sc_top_ready"), sem("sc_top_sig"))
        decided, gs_known, gs_reduced, gs_max_part, o_max_part, o_reduced = (
            sem("sc_decided"), sem("sc_gs_known"), sem("sc_gs_reduced"), sem("sc_gs_max_part"), sem("sc_o_max_part"), sem("sc_o_reduced"))
        a_in = [sem(f"sc_a_in{i}") for i in range(R)]
        a_round, a_sig, a_sig_round, a_gs, a_max, a_taken = (
            sem("sc_a_round"), sem("sc_a_sig"), sem("sc_a_sig_round"), sem("sc_a_gs"), sem("sc_a_max"), sem("sc_a_taken"))
        g_in = [sem(f"sc_g_in{i}") for i in range(R)]
        up_in = [sem(f"sc_up_in{i}") for i in range(R)]
        p_round, p_sig, p_up, p_sig_round, p_gs, p_gs_round, p_prod, p_max, p_taken = (
            sem("sc_p_round"), sem("sc_p_sig"), sem("sc_p_up"), sem("sc_p_sig_round"), sem("sc_p_gs"), sem("sc_p_gs_round"),
            sem("sc_p_prod"), sem("sc_p_max"), sem("sc_p_taken"))

        w_in = [sem(f"sc_w_in{n}") for n in range(NWG // 3)]
        wh_ready, wl_ready = sem("sc_wh_ready"), sem("sc_wl_ready")

        def group_of(w, n):
            return w[:, n * KC:(n + 1) * KC].rearrange("p m k n -> p m (k n)")

        def all_needed(eng):
            eng.wait_ge(decided, 1)
            return eng.value_load(go_through[0:1, 0:1], min_val=0, max_val=1)

        with nc.Block() as block:
            @block.sync
            def _(sp):
                for n in range(NWG // 3):
                    sp.dma_start(w_stage[:, n], w_ffn_t[NWG // 3 * 2 + n]).then_inc(w_in[n], 16)
                every = all_needed(sp)

                def load_pair(slot, t):
                    sp.dma_start(gate[:, slot], gate_dram[t]).then_inc(g_in[slot], 16)
                    sp.dma_start(up[:, slot], up_dram[t]).then_inc(up_in[slot], 16)
                with sp.If(every > 0):
                    for u in range(R):
                        sp.dma_start(gate[:, u], gate_dram[u]).then_inc(a_in[u], 16)
                    with sp.Fori(0, NCH // R - 1) as i:
                        for u in range(R):
                            sp.wait_ge(a_gs, R * i + u + 1)
                            sp.dma_start(gate[:, u], gate_dram[R * i + u + R]).then_inc(a_in[u], 16)
                    sp.wait_ge(a_gs, NCH)
                    for u in range(R):
                        load_pair(u, u)
                    with sp.Fori(0, NCH // R - 1) as i:
                        for u in range(R):
                            sp.wait_ge(p_prod, R * i + u + 1)
                            load_pair(u, R * i + u + R)
                with sp.Else():
                    at = [sp.value_load(best_at[0:1, n:n + 1], min_val=0, max_val=NCH - 1) for n in range(QUICK)]
                    for n in range(QUICK):
                        load_pair(n, at[n])

            @block.gpsimd
            def _(pool):
                pool.memset(magic[:], MAGIC).then_inc(consts, 1)
                pool.memset(amax_o[:], 0.0).then_inc(consts, 1)
                pool.wait_ge(packed_ready, 2)
                pool.partition_all_reduce(packed_all[:], packed[:], P, bass.bass_isa.ReduceOp.max).then_inc(all_ready, 1)
                every = all_needed(pool)
                with pool.If(every > 0):
                    pool.wait_ge(gs_max_part, 1)
                    pool.partition_all_reduce(amax_gs[:], amax_gs[:], P, bass.bass_isa.ReduceOp.max).then_inc(gs_reduced, 1)
                with pool.Else():
                    pool.memset(part_max[:], 0.0).then_inc(gs_reduced, 1)
                pool.wait_ge(o_max_part, 1)
                pool.partition_all_reduce(amax_o[:], amax_o[:], P, bass.bass_isa.ReduceOp.max).then_inc(o_reduced, 1)

            @block.scalar
            def _(act):
                act.wait_ge(top_ready, 1)
                act.activation(top[:, 1:2], low16(top[:, 0:1], I16), ACT.Sigmoid, scale=s_g).then_inc(top_sig, 1)
                for n in range(NWG // 3):
                    act.wait_ge(w_in[n], 16)
                    act.activation(group_of(wh, n), w_stage[:, n], ACT.Copy).then_inc(wh_ready, 1)
                act.wait_ge(consts, 2)
                every = all_needed(act)

                def head(t, u, k):
                    act.wait_ge(g_in[u], 16 * k + 16)
                    act.activation(gate[:, u], gate[:, u], ACT.Identity, scale=inv_g, bias=magic[:]).then_inc(p_round, 1)
                    act.wait_ge(p_round, t + 1)
                    wait(act, p_max, t + 1 - R)
                    act.activation(gs[:, u], low16(gate[:, u], I16), ACT.Sigmoid, scale=s_g).then_inc(p_sig, 1)
                    act.wait_ge(up_in[u], 16 * k + 16)
                    act.activation(up[:, u], up[:, u], ACT.Identity, scale=inv_u, bias=magic[:]).then_inc(p_up, 1)

                def tail(t, u):
                    act.wait_ge(p_gs, t + 1)
                    act.activation(gs[:, u], gs[:, u], ACT.Identity, scale=gs_factor, bias=magic[:]).then_inc(p_gs_round, 1)
                with act.If(every > 0):
                    for u in range(R):
                        act.wait_ge(a_in[u], 16)
                        act.activation(gate[:, u], gate[:, u], ACT.Identity, scale=inv_g, bias=magic[:]).then_inc(a_round, 1)
                        act.wait_ge(a_round, u + 1)
                        act.activation(gs[:, u], low16(gate[:, u], I16), ACT.Sigmoid, scale=s_g).then_inc(a_sig, 1)
                    with act.Fori(1, NCH // R) as i:
                        for u in range(R):
                            t = R * i + u
                            act.wait_ge(a_in[u], 16 * i + 16)
                            act.activation(gate[:, u], gate[:, u], ACT.Identity, scale=inv_g, bias=magic[:]).then_inc(a_round, 1)
                            act.wait_ge(a_round, t + 1)
                            act.wait_ge(a_max, t + 1 - R)
                            act.activation(gs[:, u], low16(gate[:, u], I16), ACT.Sigmoid, scale=s_g).then_inc(a_sig, 1)
                    act.wait_ge(gs_known, 1)
                    head(0, 0, 0)
                    for t in range(1, R):
                        head(t, t, 0)
                        tail(t - 1, t - 1)
                    with act.Fori(1, NCH // R) as i:
                        for u in range(R):
                            head(R * i + u, u, i)
                            tail(R * i + u - 1, (u - 1) % R)
                    tail(NCH - 1, R - 1)
                with act.Else():
                    for n in range(QUICK):
                        head(n, n, 0)
                    act.wait_ge(gs_known, 1)
                    for n in range(QUICK):
                        tail(n, n)

            @block.vector
            def _(dve):
                for n in range(3):
                    dve.tensor_reduce(packed[:, n:n + 1], acc[:, n], AX.X, ALU.max).then_inc(sc, 1)
                dve.tensor_copy(packed[:, 3:], rmax[:]).then_inc(packed_ready, 1)
                dve.wait_ge(sc, 3)
                dve.memset(part_max[:], 0.0).then_inc(packed_ready, 1)
                dve.wait_ge(all_ready, 1)
                dve.tensor_tensor(gmag[:], packed_all[:, 1:2], packed_all[:, 2:3], ALU.max).then_inc(sc, 1)
                dve.wait_ge(sc, 4)
                n = quantizer(dve, s_u, inv_u, packed_all[:, 0:1], sc, 4)
                n = quantizer(dve, s_g, inv_g, gmag[:], sc, n)
                dve.tensor_scalar(top[:, 0:1], packed_all[:, 1:2], inv_g, MAGIC, ALU.mult, ALU.add).then_inc(top_ready, 1)
                dve.max(best[:], packed_all[:, 3:]).then_inc(sc, 1)
                dve.tensor_tensor(tmp[:, 0:1], s_u, s_g, ALU.mult).then_inc(sc, 1)
                dve.wait_ge(sc, 10)
                dve.max_index(best_at[:], best[:], packed_all[:, 3:]).then_inc(sc, 1)
                dve.scalar_tensor_tensor(tmp[:, 1:2], tmp[:, 0:1], MARGIN, best[:, QUICK:QUICK + 1],
                                         ALU.mult, ALU.add).then_inc(sc, 1)
                dve.wait_ge(sc, 12)
                dve.tensor_tensor(tmp[:, 2:3], tmp[:, 1:2], best[:, 0:1], ALU.is_ge).then_inc(sc, 1)
                dve.wait_ge(top_sig, 1)
                dve.tensor_scalar(top[:, 2:3], top[:, 1:2], 65535.0 * SIG_STEP, SIG_MAGIC, ALU.min, ALU.add).then_inc(top_ready, 1)
                dve.wait_ge(top_ready, 2)
                dve.tensor_tensor(top[:, 3:4], low16(top[:, 0:1], I16), low16(top[:, 2:3], U16), ALU.mult).then_inc(top_ready, 1)
                dve.tensor_scalar(tmp[:, 3:4], s_g, SIG_STEP, None, ALU.mult).then_inc(sc, 1)
                dve.wait_ge(top_ready, 3)
                dve.wait_ge(sc, 14)
                dve.tensor_tensor(tmp[:, 4:5], top[:, 3:4], tmp[:, 3:4], ALU.mult).then_inc(sc, 1)
                dve.tensor_copy(amax_gs[:], top[:, 3:4]).then_inc(sc, 1)
                dve.wait_ge(sc, 16)
                dve.scalar_tensor_tensor(tmp[:, 5:6], tmp[:, 4:5], SILU_SURE, tmp[:, 2:3], ALU.is_lt, ALU.max).then_inc(sc, 1)
                dve.wait_ge(sc, 17)
                dve.tensor_copy(go_through[:], tmp[:, 5:6]).then_inc(decided, 1)
                dve.wait_ge(consts, 2)
                every = all_needed(dve)

                def round_sigmoid(buf, done):
                    dve.tensor_scalar(buf, buf, 65535.0 * SIG_STEP, SIG_MAGIC, ALU.min, ALU.add).then_inc(done, 1)

                with dve.If(every > 0):
                    dve.memset(amax_gs[:], 0.0).then_inc(a_taken, 1)
                    with dve.Fori(0, NCH // R) as i:
                        for u in range(R):
                            t = R * i + u
                            dve.wait_ge(a_sig, t + 1)
                            round_sigmoid(gs[:, u], a_sig_round)
                            dve.wait_ge(a_sig_round, t + 1)
                            dve.tensor_tensor(gs[:, u], low16(gate[:, u], I16), low16(gs[:, u], U16), ALU.mult).then_inc(a_gs, 1)
                            dve.wait_ge(a_gs, t + 1)
                            dve.wait_ge(a_taken, t + 1)
                            dve.tensor_reduce(part_max[:], gs[:, u], AX.X, ALU.max, apply_absolute_value=True).then_inc(a_max, 1)
                            dve.wait_ge(a_max, t + 1)
                            dve.tensor_tensor(amax_gs[:], amax_gs[:], part_max[:], ALU.max).then_inc(a_taken, 1)
                    dve.wait_ge(a_taken, NCH + 1)
                    dve.tensor_copy(tmp[:, 6:7], amax_gs[:]).then_inc(gs_max_part, 1)
                with dve.Else():
                    dve.tensor_copy(tmp[:, 6:7], amax_gs[:]).then_inc(gs_max_part, 1)
                dve.wait_ge(gs_reduced, 1)
                dve.tensor_tensor(tmp[:, 4:5], tmp[:, 3:4], amax_gs[:], ALU.mult).then_inc(sc, 1)
                dve.wait_ge(sc, 18)
                n = quantizer(dve, s_gs, inv_gs, tmp[:, 4:5], sc, 18)
                dve.tensor_tensor(gs_factor, tmp[:, 3:4], inv_gs, ALU.mult).then_inc(gs_known, 1)
                for n in range(NWG // 3):
                    dve.wait_ge(wh_ready, n + 1)
                    dve.tensor_tensor(group_of(wl, n), w_stage[:, n], group_of(wh, n).bitcast(F32),
                                      ALU.subtract).then_inc(wl_ready, 1)

                def head(t, u):
                    dve.wait_ge(p_sig, t + 1)
                    round_sigmoid(gs[:, u], p_sig_round)
                    dve.wait_ge(p_sig_round, t + 1)
                    dve.tensor_tensor(gs[:, u], low16(gate[:, u], I16), low16(gs[:, u], U16), ALU.mult).then_inc(p_gs, 1)

                def tail(t, u):
                    dve.wait_ge(p_gs_round, t + 1)
                    dve.wait_ge(p_up, t + 1)
                    dve.tensor_tensor(gs[:, u], low16(gs[:, u], I16), low16(up[:, u], I16), ALU.mult).then_inc(p_prod, 1)
                    dve.wait_ge(p_prod, t + 1)
                    wait(dve, p_taken, t)
                    dve.tensor_reduce(part_max[:], gs[:, u], AX.X, ALU.max, apply_absolute_value=True).then_inc(p_max, 1)
                    dve.wait_ge(p_max, t + 1)
                    dve.tensor_tensor(amax_o[:], amax_o[:], part_max[:], ALU.max).then_inc(p_taken, 1)
                with dve.If(every > 0):
                    for t in range(R):
                        head(t, t)
                        tail(t, t)
                    with dve.Fori(1, NCH // R) as i:
                        for u in range(R):
                            head(R * i + u, u)
                            tail(R * i + u, u)
                    dve.wait_ge(p_taken, NCH)
                    dve.memset(part_max[:], 0.0).then_inc(o_max_part, 1)
                with dve.Else():
                    for n in range(QUICK):
                        head(n, n)
                    for n in range(QUICK):
                        tail(n, n)
                    dve.wait_ge(p_taken, QUICK)
                    dve.memset(part_max[:], 0.0).then_inc(o_max_part, 1)
                dve.wait_ge(o_reduced, 1)
                dve.tensor_tensor(tmp[:, 0:1], s_gs, s_u, ALU.mult).then_inc(sc, 1)
                dve.wait_ge(sc, 21)
                dve.tensor_tensor(tmp[:, 1:2], tmp[:, 0:1], amax_o[:], ALU.mult).then_inc(sc, 1)
                dve.wait_ge(sc, 22)
                quantizer(dve, s_o, inv_o, tmp[:, 1:2], sc, 22)
                dve.tensor_tensor(o_factor, tmp[:, 0:1], inv_o, ALU.mult).then_inc(sc, 1)
                dve.wait_ge(sc, 25)
                dve.wait_ge(wl_ready, NWG // 3)


def down_phase(nc, up_dram, gate_dram, x2_dram, out, scales, wh, wl):
    with ExitStack() as ctx:
        used = []
        ctx.callback(lambda: (nc.clear_and_free_semaphores(used), nc.all_engine_barrier()))

        def sb(name, shape, dt=F32):
            return ctx.enter_context(nc.sbuf_tensor(name, shape, dt))

        def sem(name):
            return phase_semaphore(nc, used, name)

        NC3 = 3
        gate = sb("dn_gate", [P, NC3, CH])
        up = sb("dn_up", [P, NC3, CH])
        gs = sb("dn_gs", [P, NC3, CH])
        oh = sb("dn_oh", [P, NC3, KC, T], F32R)
        ol = sb("dn_ol", [P, NC3, KC, T], F32R)
        x2 = sb("dn_x2", [P, 2, TT, HID])
        magic = sb("dn_magic", [P, 1])
        mhalf = sb("dn_mhalf", [P, TT])
        tick = sb("dn_tick", [P, 1])
        stats = sb("dn_stats", [P, TT, 6])
        msum, mdiff, msq = (sb(f"dn_{n}", [P, TT]) for n in ("msum", "mdiff", "msq"))
        var_eps = sb("dn_var_eps", [P, TT])
        rstd = sb("dn_rstd", [P, TT])
        nmr = sb("dn_nmr", [P, TT])
        out_ps = [ctx.enter_context(nc.psum_tensor(f"dn_ps{i}", [P, HID], F32)) for i in range(8)]
        g_in = [sem(f"dn_g_in{i}") for i in range(NC3)]
        up_in = [sem(f"dn_up_in{i}") for i in range(NC3)]
        x2_in = [sem(f"dn_x2_in{i}") for i in range(2)]
        stored = [sem(f"dn_stored{i}") for i in range(2)]
        consts, tick_done = sem("dn_consts"), sem("dn_tick_done")
        g_round, sig_ready, sig_round, gs_ready, gs_round, up_round, prod_ready, prod_round, oh_ready, ol_ready = (
            sem("dn_g_round"), sem("dn_sig_ready"), sem("dn_sig_round"), sem("dn_gs_ready"), sem("dn_gs_round"),
            sem("dn_up_round"), sem("dn_prod_ready"), sem("dn_prod_round"), sem("dn_oh_ready"), sem("dn_ol_ready"))
        part_used, y_ready, sum_ready, stats_ready, moments_ready, square_ready, ve_ready, rstd_ready, nmr_ready, norm_ready = (
            sem("dn_part_used"), sem("dn_y_ready"), sem("dn_sum_ready"), sem("dn_stats_ready"), sem("dn_moments_ready"),
            sem("dn_square_ready"), sem("dn_ve_ready"), sem("dn_rstd_ready"), sem("dn_nmr_ready"), sem("dn_norm_ready"))
        s_u, inv_u, s_g, inv_g, s_gs, inv_gs, gs_factor, s_o, inv_o, o_factor = (scales[:, i:i + 1] for i in range(2, 12))

        def earlier(b, n, back):
            return (b, n - back) if n >= back else (b - 1, n - back + NC3)

        def chunk_steps(b, n, begin, carry_on, finish, last):
            if b < NB if isinstance(b, int) else True:
                begin(b, n)
            for back, f in ((1, carry_on), (2, finish)):
                bb, nn = earlier(b, n, back)
                if not isinstance(bb, int) or 0 <= bb < NB:
                    f(bb, nn)
            if n in last and (not isinstance(b, int) or b >= 2):
                last[n](b - 2)

        with nc.Block() as block:
            @block.sync
            def _(sp):
                def load_gate(b, n):
                    sp.dma_start(gate[:, n], gate_dram[NC3 * b + n]).then_inc(g_in[n], 16)

                def load_up(b, n):
                    sp.dma_start(up[:, n], up_dram[NC3 * b + n]).then_inc(up_in[n], 16)
                for n in range(NC3):
                    load_gate(0, n)
                    load_up(0, n)

                def step(b, u, k, nxt):
                    for n in range(NC3):
                        if nxt:
                            sp.wait_ge(gs_ready, NC3 * b + n + 1)
                            load_gate(b + 1, n)
                        bb, nn = earlier(b, n, 2)
                        if not isinstance(bb, int) or 0 <= bb < NB - 1:
                            sp.wait_ge(ol_ready, NC3 * bb + nn + 1)
                            load_up(bb + 1, nn)
                    if k is not None:
                        sp.wait_ge(stored[u], 16 * k)
                    sp.dma_start(x2[:, u], x2_dram[b]).then_inc(x2_in[u], 16)
                step(0, 0, None, True)
                step(1, 1, None, True)
                with sp.Fori(1, NB // 2 - 1) as i:
                    for u in range(2):
                        step(2 * i + u, u, i, True)
                step(NB - 2, 0, NB // 2 - 1, True)
                step(NB - 1, 1, NB // 2 - 1, False)
                for u in range(2):
                    sp.wait_ge(stored[u], 16 * (NB // 2))

            @block.gpsimd
            def _(pool):
                pool.memset(magic[:], MAGIC).then_inc(consts, 1)
                pool.memset(mhalf[:], -0.5).then_inc(consts, 1)
                pool.wait_ge(consts, 2)

                def round_gate(b, n, with_up):
                    wait(pool, tick_done, NC3 * b + n)
                    pool.wait_ge(g_in[n], 16 * (b + 1))
                    if with_up:
                        bb, nn = earlier(b, n, 1)
                        pool.wait_ge(up_in[nn], 16 * (bb + 1))
                    pool.tensor_tensor(tick[:], mhalf[:, 0:1], mhalf[:, 0:1], ALU.mult).then_inc(tick_done, 1)
                    pool.tensor_scalar(gate[:, n], gate[:, n], inv_g, MAGIC, ALU.mult, ALU.add).then_inc(g_round, 1)
                    if with_up:
                        round_up(nn)

                def round_up(n):
                    pool.tensor_scalar(up[:, n], up[:, n], inv_u, MAGIC, ALU.mult, ALU.add).then_inc(up_round, 1)

                def root(b):
                    pool.wait_ge(ve_ready, b + 1)
                    pool.tensor_tensor(rstd[:], var_eps[:], mhalf[:], ALU.pow).then_inc(rstd_ready, 1)
                for b in range(2):
                    for n in range(NC3):
                        round_gate(b, n, b + n > 0)
                with pool.Fori(2, NB) as b:
                    for n in range(NC3):
                        round_gate(b, n, True)
                    root(b - 2)
                pool.wait_ge(up_in[NC3 - 1], 16 * NB)
                round_up(NC3 - 1)
                root(NB - 2)
                root(NB - 1)

            @block.scalar
            def _(act):
                act.wait_ge(consts, 2)

                def begin(b, n):
                    t = NC3 * b + n
                    act.wait_ge(g_round, t + 1)
                    wait(act, prod_ready, t - NC3 + 1)
                    act.activation(gs[:, n], low16(gate[:, n], I16), ACT.Sigmoid, scale=s_g).then_inc(sig_ready, 1)

                def carry_on(b, n):
                    act.wait_ge(gs_ready, NC3 * b + n + 1)
                    act.activation(gs[:, n], gs[:, n], ACT.Identity, scale=gs_factor, bias=magic[:]).then_inc(gs_round, 1)

                def finish(b, n):
                    t = NC3 * b + n
                    act.wait_ge(prod_ready, t + 1)
                    act.activation(up[:, n], up[:, n], ACT.Identity, scale=o_factor, bias=magic[:]).then_inc(prod_round, 1)
                    act.wait_ge(prod_round, t + 1)
                    if not isinstance(b, int) or b > 0:
                        if n < 2:
                            act.wait_ge(part_used, 2 * (b - 1) + n + 1)
                        else:
                            act.wait_ge(y_ready, TT * b)
                    act.activation(oh[:, n].rearrange("p m t -> p (m t)"), low16(up[:, n], I16), ACT.Copy).then_inc(oh_ready, 1)

                def normalise(b, par):
                    act.wait_ge(nmr_ready, b + 1)
                    for j in range(TT):
                        act.activation(x2[:, par, j], x2[:, par, j], ACT.Identity, scale=rstd[:, j:j + 1],
                                       bias=nmr[:, j:j + 1]).then_inc(norm_ready, 1)
                    act.wait_ge(norm_ready, TT * (b + 1))
                    act.dma_start(out[b], x2[:, par]).then_inc(stored[par], 16)

                def step(b, par):
                    for n in range(NC3):
                        chunk_steps(b, n, begin, carry_on, finish, {2: lambda bb: normalise(bb, par)})
                step(0, 0)
                step(1, 1)
                with act.Fori(1, NB // 2) as i:
                    for u in range(2):
                        step(2 * i + u, u)
                step(NB, 0)
                normalise(NB - 1, 1)

            @block.vector
            def _(dve):
                def begin(b, n):
                    t = NC3 * b + n
                    dve.wait_ge(sig_ready, t + 1)
                    dve.tensor_scalar(gs[:, n], gs[:, n], 65535.0 * SIG_STEP, SIG_MAGIC, ALU.min, ALU.add).then_inc(sig_round, 1)
                    dve.wait_ge(sig_round, t + 1)
                    dve.tensor_tensor(gs[:, n], low16(gate[:, n], I16), low16(gs[:, n], U16), ALU.mult).then_inc(gs_ready, 1)

                def carry_on(b, n):
                    t = NC3 * b + n
                    dve.wait_ge(gs_round, t + 1)
                    dve.wait_ge(up_round, t + 1)
                    dve.tensor_tensor(up[:, n], low16(gs[:, n], I16), low16(up[:, n], I16), ALU.mult).then_inc(prod_ready, 1)

                def finish(b, n):
                    dve.wait_ge(oh_ready, NC3 * b + n + 1)
                    dve.tensor_tensor(ol[:, n].rearrange("p m t -> p (m t)"), low16(up[:, n], I16),
                                      oh[:, n].rearrange("p m t -> p (m t)").bitcast(F32), ALU.subtract).then_inc(ol_ready, 1)

                def sums(b, par, k):
                    dve.wait_ge(x2_in[par], 16 * (k + 1))
                    for j in range(TT):
                        n = TT * b + j + 1
                        dve.wait_ge(y_ready, n)
                        dve.scalar_tensor_tensor(x2[:, par, j], out_ps[TT * par + j][:], s_o, x2[:, par, j],
                                                 ALU.mult, ALU.add).then_inc(sum_ready, 1)
                        dve.wait_ge(sum_ready, n)
                        dve.bn_stats(stats[:, j], x2[:, par, j]).then_inc(stats_ready, 1)
                    wait(dve, norm_ready, TT * b)
                    dve.wait_ge(stats_ready, TT * (b + 1))
                    row_moments(dve, stats, msum[:], mdiff[:], msq[:], var_eps[:], moments_ready, square_ready, ve_ready, b + 1)

                def norm_bias(b):
                    dve.wait_ge(rstd_ready, b + 1)
                    dve.scalar_tensor_tensor(nmr[:], msum[:], -0.5, rstd[:], ALU.mult, ALU.mult).then_inc(nmr_ready, 1)

                def step(b, par, k):
                    for n in range(NC3):
                        chunk_steps(b, n, begin, carry_on, finish, {0: lambda bb: sums(bb, par, k), 1: norm_bias})
                step(0, 0, 0)
                step(1, 1, 0)
                step(2, 0, 0)
                step(3, 1, 0)
                with dve.Fori(2, NB // 2) as i:
                    for u in range(2):
                        step(2 * i + u, u, i - 1)
                step(NB, 0, NB // 2 - 1)
                sums(NB - 1, 1, NB // 2 - 1)
                norm_bias(NB - 1)

            @block.tensor
            def _(pe):
                def step(b, u):
                    for n in range(NC3):
                        pe.wait_ge(ol_ready, NC3 * b + n + 1)
                        if n == 0 and (not isinstance(b, int) or b > 1):
                            pe.wait_ge(sum_ready, TT * (b - 1))
                        for j in range(TT):
                            rows = slice(j * P, (j + 1) * P)
                            o = out_ps[TT * u + j][:].rearrange("p (m n) -> p m n", n=P)
                            for k in range(KC):
                                mh, ml = (w[:, n * KC:(n + 1) * KC, k] for w in (wh, wl))
                                pe.matmul(o, oh[:, n, k, rows], mh, start=(n == 0 and k == 0), stop=False)
                                pe.matmul(o, oh[:, n, k, rows], ml, start=False, stop=False)
                                mm = pe.matmul(o, ol[:, n, k, rows], mh, start=False, stop=(n == NC3 - 1 and k == KC - 1))
                            if n == NC3 - 1:
                                mm.then_inc(y_ready, 1)
                        if n < NC3 - 1:
                            mm.then_inc(part_used, 1)
                step(0, 0)
                step(1, 1)
                with pe.Fori(1, NB // 2) as i:
                    for u in range(2):
                        step(2 * i + u, u)


def decoder(nc, xT, x, ctx_in, w_attn, w_ffn, b_gate, decay, out):
    def scratch(name, shape):
        return nc.dram_tensor(name, shape, F32, kind="Internal").ap()

    w_ffn_t = scratch("w_ffn_t", (NWG, P, WG, T))
    x2_dram = scratch("x2_rows", (NB, P, TT, HID))
    up_dram = scratch("up_products", (NCH, P, CH))
    gate_dram = scratch("gate_products", (NCH, P, CH))
    with ExitStack() as ctx:
        def sb(name, shape, dt=F32):
            return ctx.enter_context(nc.sbuf_tensor(name, shape, dt))
        amax_x2 = sb("amax_x2", [P, 1])
        acc = sb("acc", [P, 3, 3])
        rmax = sb("rmax", [P, NCH])
        scales = sb("scales", [P, 12])
        with ExitStack() as attn:
            wah = attn.enter_context(nc.sbuf_tensor("wah", [P, KC, 5, T], F32R))
            wal = attn.enter_context(nc.sbuf_tensor("wal", [P, KC, 5, T], F32R))
            prepare_weights(nc, w_attn, w_ffn, w_ffn_t, wah, wal)
            attention_phase(nc, xT, x, ctx_in, b_gate, decay, wah, wal, x2_dram, amax_x2)
        up_gate_phase(nc, x2_dram, w_ffn_t, up_dram, gate_dram, amax_x2, acc, rmax, scales)
        wh = sb("down_wh", [P, MT, KC, P], F32R)
        wl = sb("down_wl", [P, MT, KC, P], F32R)
        scales_phase(nc, up_dram, gate_dram, w_ffn_t, acc, rmax, scales, wh, wl)
        down_phase(nc, up_dram, gate_dram, x2_dram, out, scales, wh, wl)


def kernel(**inputs):
    import concourse.bacc as bacc
    from concourse.bass_utils import run_bass_kernel_spmd

    a = {k: np.asarray(v) for k, v in inputs.items()}
    arrays = {
        "xT": np.ascontiguousarray(a["x"].transpose(0, 2, 1)).reshape(NB, KC, P, T),
        "x_rows": np.ascontiguousarray(a["x"].reshape(NB, TT, P, HID).transpose(0, 2, 1, 3)),
        "ctx_rows": np.ascontiguousarray(a["ctx_1024"].reshape(NB, TT, P, HID).transpose(0, 2, 1, 3)),
        "w_attn": np.ascontiguousarray(np.concatenate(
            [a["L0_attn_Wqkv"], a["L0_attn_Wgate"], a["L0_attn_Wout"]]).reshape(5, HID, KC, P).transpose(3, 2, 0, 1)),
        "w_ffn": np.ascontiguousarray(np.concatenate(
            [a["L0_ffn_w_up"].reshape(MT, P, HID), a["L0_ffn_w_gate"].reshape(MT, P, HID),
             a["L0_ffn_w_down"].reshape(KC, P, 3, HID).transpose(2, 0, 1, 3).reshape(MT, P, HID)])
            .reshape(NWG, WG, P, HID).transpose(0, 2, 1, 3)),
        "b_gate": np.ascontiguousarray(a["L0_attn_bgate"].reshape(KC, P).T),
        "decay": np.ascontiguousarray(np.repeat(a["L0_attn_decay_param"], HID // NH).reshape(KC, P).T),
    }
    nc = bacc.Bacc("TRN2", target_bir_lowering=False, num_devices=1)
    args = [nc.dram_tensor(f"in_{k}", v.shape, mybir.dt.from_np(v.dtype), kind="ExternalInput").ap()
            for k, v in arrays.items()]
    out = nc.dram_tensor("out_rows", (NB, P, TT, HID), F32, kind="ExternalOutput").ap()
    decoder(nc, *args, out)
    r = run_bass_kernel_spmd(nc, [{f"in_{k}": v for k, v in arrays.items()}], core_ids=[0])
    rows = r.results[0]["out_rows"]
    return np.ascontiguousarray(rows.transpose(0, 2, 1, 3)).reshape(NB, T, HID)
```
